# Optimizing a Trainium2 kernel written in Bass

```python
import numpy as np
import jax
import jax.numpy as jnp

def _softmax(x, axis=-1):
    return jax.nn.softmax(x, axis=axis)

def _gelu(x):
    return jax.nn.gelu(x, approximate=True)

def _silu(x):
    return jax.nn.silu(x)

def _sigmoid(x):
    return jax.nn.sigmoid(x)

def _layernorm(x, axis=-1, eps=1e-05):
    m = jnp.mean(x, axis=axis, keepdims=True)
    v = jnp.var(x, axis=axis, keepdims=True)
    return (x - m) / jnp.sqrt(v + eps)

def _scatter_add(tgt, idx, src, axis=0):
    return tgt.at[idx].add(src)

def _segment_sum(src, seg, n):
    return jax.ops.segment_sum(src, seg, n)
kernel_name = 'mk_gnn_preln_d2_gnn_r16_b16f2f'

def setup_inputs(seed: int=0):
    np.random.seed(seed)
    _w = jnp.asarray

    def _rec_inputs():
        import jax
        import jax.numpy as jnp
        _gk = jax.random.key(seed)
        x = -0.0003713 + 1 * jax.random.normal(jax.random.fold_in(_gk, 1), (6250, 256), jnp.float32)
        src = jax.random.randint(jax.random.fold_in(_gk, 2), (100000,), 0, 6250, jnp.int32)
        dst = jax.random.randint(jax.random.fold_in(_gk, 3), (100000,), 0, 6250, jnp.int32)
        _o = jnp.argsort(dst, stable=True)
        src = src[_o]
        dst = dst[_o]
        return (x, src, dst)
    x, src, dst = _rec_inputs()

    def _L0_gnn_setup():
        import jax, jax.numpy as jnp
        import numpy as np
        N_NODES = 3125
        N_EDGES = 50000
        HIDDEN = 256
        K_HOP = 3
        key = jax.random.key(seed)
        k1, k2, k3, k4 = jax.random.split(key, 4)
        x = jax.random.normal(k1, (N_NODES, HIDDEN), dtype=jnp.float32)
        W = jax.random.normal(k2, (K_HOP, HIDDEN, HIDDEN), dtype=jnp.float32) / jnp.sqrt(HIDDEN).astype(jnp.float32)
        b = jnp.zeros((K_HOP, HIDDEN), dtype=jnp.float32)
        src = jax.random.randint(k3, (N_EDGES,), 0, N_NODES, dtype=jnp.int32)
        dst = jax.random.randint(k4, (N_EDGES,), 0, N_NODES, dtype=jnp.int32)
        return {'x': x, 'W': W, 'b': b, 'src': src, 'dst': dst}
    _L0_gnn_all = _L0_gnn_setup()
    _L0_gnn_in = {k: v for k, v in _L0_gnn_all.items() if k in ('W', 'b')}
    del _L0_gnn_all

    def _L1_gnn_setup():
        import jax, jax.numpy as jnp
        import numpy as np
        N, E = (3125, 50000)
        H, C_IN, C_HID, C_OUT = (4, 256, 64, 64)
        NEG_SLOPE = 0.2

        def leaky_relu(x, s=NEG_SLOPE):
            return jnp.where(x >= 0, x, s * x)

        def gat_conv(x, src, dst, W, att_src, att_dst, bias, n_nodes):
            Hh, Cc = (att_src.shape[1], att_src.shape[2])
            h = (x @ W).reshape(n_nodes, Hh, Cc)
            a_src = (h * att_src).sum(-1)
            a_dst = (h * att_dst).sum(-1)
            alpha = leaky_relu(a_src[src] + a_dst[dst])
            m = jax.ops.segment_max(alpha, dst, num_segments=n_nodes)
            e = jnp.exp(alpha - m[dst])
            denom = jax.ops.segment_sum(e, dst, num_segments=n_nodes)
            w = e / jnp.clip(denom, 1e-16)[dst]
            out = jax.ops.segment_sum(w[:, :, None] * h[src], dst, num_segments=n_nodes)
            return out.reshape(n_nodes, Hh * Cc) + bias
        key = jax.random.key(seed)
        ks = jax.random.split(key, 10)
        glorot = lambda k, shp: jax.random.normal(k, shp, jnp.float32) * np.sqrt(2.0 / (shp[0] + shp[-1]))
        return {'x': jax.random.normal(ks[0], (N, C_IN), jnp.float32), 'edge_index': jax.random.randint(ks[1], (2, E), 0, N, jnp.int32), 'W1': glorot(ks[2], (C_IN, H * C_HID)), 'att_src1': glorot(ks[3], (1, H, C_HID)), 'att_dst1': glorot(ks[4], (1, H, C_HID)), 'b1': jnp.zeros((H * C_HID,), jnp.float32), 'W2': glorot(ks[5], (H * C_HID, H * C_OUT)), 'att_src2': glorot(ks[6], (1, H, C_OUT)), 'att_dst2': glorot(ks[7], (1, H, C_OUT)), 'b2': jnp.zeros((H * C_OUT,), jnp.float32)}
    _L1_gnn_all = _L1_gnn_setup()
    _L1_gnn_in = {k: v for k, v in _L1_gnn_all.items() if k in ('W1', 'att_src1', 'att_dst1', 'b1', 'W2', 'att_src2', 'att_dst2', 'b2')}
    del _L1_gnn_all
    return {'x': x, 'src': src, 'dst': dst, 'L0_gnn_W': _L0_gnn_in['W'], 'L0_gnn_b': _L0_gnn_in['b'], 'L1_gnn_W1': _L1_gnn_in['W1'], 'L1_gnn_att_src1': _L1_gnn_in['att_src1'], 'L1_gnn_att_dst1': _L1_gnn_in['att_dst1'], 'L1_gnn_b1': _L1_gnn_in['b1'], 'L1_gnn_W2': _L1_gnn_in['W2'], 'L1_gnn_att_src2': _L1_gnn_in['att_src2'], 'L1_gnn_att_dst2': _L1_gnn_in['att_dst2'], 'L1_gnn_b2': _L1_gnn_in['b2']}

def reference(x, src, dst, L0_gnn_W, L0_gnn_b, L1_gnn_W1, L1_gnn_att_src1, L1_gnn_att_dst1, L1_gnn_b1, L1_gnn_W2, L1_gnn_att_src2, L1_gnn_att_dst2, L1_gnn_b2):
    import jax
    import jax.numpy as jnp

    def _L0_gnn_ref(x, W, b, src, dst):
        import jax, jax.numpy as jnp
        import numpy as np
        N_NODES = 3125
        N_EDGES = 50000
        HIDDEN = 256
        K_HOP = 3
        N = x.shape[0]
        ones = jnp.ones(src.shape[0], dtype=x.dtype)
        out_deg = jax.ops.segment_sum(ones, src, num_segments=N)
        in_deg = jax.ops.segment_sum(ones, dst, num_segments=N)
        out_norm = jnp.clip(out_deg, 1.0, None) ** (-0.5)
        in_norm = jnp.clip(in_deg, 1.0, None) ** (-0.5)
        k_hop = W.shape[0]
        h = x
        for i in range(k_hop):
            h = h * out_norm[:, None]
            h = jax.ops.segment_sum(h[src], dst, num_segments=N)
            h = h * in_norm[:, None]
            h = h @ W[i] + b[i]
            if i < k_hop - 1:
                h = jax.nn.relu(h)
        return h

    def _L1_gnn_ref(x, edge_index, W1, att_src1, att_dst1, b1, W2, att_src2, att_dst2, b2):
        import jax, jax.numpy as jnp
        import numpy as np
        N, E = (3125, 50000)
        H, C_IN, C_HID, C_OUT = (4, 256, 64, 64)
        NEG_SLOPE = 0.2

        def leaky_relu(x, s=NEG_SLOPE):
            return jnp.where(x >= 0, x, s * x)

        def gat_conv(x, src, dst, W, att_src, att_dst, bias, n_nodes):
            Hh, Cc = (att_src.shape[1], att_src.shape[2])
            h = (x @ W).reshape(n_nodes, Hh, Cc)
            a_src = (h * att_src).sum(-1)
            a_dst = (h * att_dst).sum(-1)
            alpha = leaky_relu(a_src[src] + a_dst[dst])
            m = jax.ops.segment_max(alpha, dst, num_segments=n_nodes)
            e = jnp.exp(alpha - m[dst])
            denom = jax.ops.segment_sum(e, dst, num_segments=n_nodes)
            w = e / jnp.clip(denom, 1e-16)[dst]
            out = jax.ops.segment_sum(w[:, :, None] * h[src], dst, num_segments=n_nodes)
            return out.reshape(n_nodes, Hh * Cc) + bias
        n = x.shape[0]
        loops = jnp.arange(n, dtype=edge_index.dtype)
        src = jnp.concatenate([edge_index[0], loops])
        dst = jnp.concatenate([edge_index[1], loops])
        h1 = gat_conv(x, src, dst, W1, att_src1, att_dst1, b1, n)
        h1 = jax.nn.relu(h1)
        out = gat_conv(h1, src, dst, W2, att_src2, att_dst2, b2, n)
        return out
    edge_index = jnp.stack([src, dst])
    h = jnp.maximum(_layernorm(x, axis=-1), 0.0)
    x = x + _L0_gnn_ref(h, L0_gnn_W, L0_gnn_b, src, dst)
    h = jnp.maximum(_layernorm(x, axis=-1), 0.0)
    x = x + _L1_gnn_ref(h, edge_index, L1_gnn_W1, L1_gnn_att_src1, L1_gnn_att_dst1, L1_gnn_b1, L1_gnn_W2, L1_gnn_att_src2, L1_gnn_att_dst2, L1_gnn_b2)
    return x

_drawn_inputs = setup_inputs


def setup_inputs(seed=0):
    import zlib

    import numpy as np

    out = dict(_drawn_inputs(seed))
    spreads = {'L0_gnn_b': (0.0, 0.1), 'L1_gnn_b1': (0.0, 0.1), 'L1_gnn_b2': (0.0, 0.1)}
    factors = {'L1_gnn_att_dst1': 165.991, 'L1_gnn_att_src2': 22.502, 'L1_gnn_att_dst2': 110.337}
    for name, (base, spread) in spreads.items():
        noise = np.random.default_rng([zlib.crc32(name.encode()), seed]).standard_normal(out[name].shape)
        drawn = base * np.exp(spread * noise) if base else spread * noise
        out[name] = jnp.asarray(drawn.astype(out[name].dtype))
    for name, factor in factors.items():
        out[name] = (out[name] * factor).astype(out[name].dtype)
    return out
```

```python
import concourse.bass as bass
from concourse import mybir
from contextlib import ExitStack

F32 = mybir.dt.float32
BF16 = mybir.dt.bfloat16
I32 = mybir.dt.int32
ALU = mybir.AluOpType
ACT = mybir.ActivationFunctionType
AX = mybir.AxisListType

P = 128
N = 6250
E = 100000
C = 256
H = 4
CH = C // H
HOPS = 3
LAYERS = 2
NT = -(-N // P)
NFULL = N // P
NREST = N - NFULL * P
EC = -(-E // P)
EPAD = EC * P - E
G = 32
NG = -(-(EC + NT - 1) // G)
S = NG * G
SB = -(-(S + G) // P)
SX = SB * P
OUTSIDE = 50 * P
BIG = 1e30
EPS = 1e-5
SLOPE = 0.2
AW = C + 2 * H
TW = C + H
PW = C + 2 * H
RING = 2 * G
U = 32
UH = U // 2
AHEAD = 3
OHR = 4
TB = 7
NI = NT // TB
HB = 17
NH = EC // (2 * HB)
DVEC = 3 * CH
CR = U
assert EC % (2 * HB) == 0 and NT % TB == 0 and S % U == 0 and NG % 2 == 0 and S >= EC + NT - 1


def gnn(nc, x, src, dst, gw, gb, w1, as1, ad1, b1, w2, as2, ad2, b2, out):
    ctx = ExitStack()
    with ctx:
        def sb(name, shape, dt=F32):
            return ctx.enter_context(nc.sbuf_tensor(name, shape, dt))

        def sem(name):
            return ctx.enter_context(nc.semaphore(name))

        def dram(name, shape, dt=F32):
            return nc.dram_tensor(name, shape, dt, kind="Internal").ap()

        src_pad = dram("src_pad", (EC, P), I32)
        dst_pad = dram("dst_pad", (EC, P), I32)
        keys = dram("keys", (1, SX * P + 2))
        start_rows = dram("start_rows", (SX, P))
        end_rows = dram("end_rows", (SX, P))
        start_any = dram("start_any", (1, SX))
        end_any = dram("end_any", (1, SX))
        tile_of = dram("tile_of", (1, SX))
        conv_tab = [dram(f"conv_tab{k}", (NT * P, C)) for k in range(HOPS)]
        attn_tab = [dram(f"attn_tab{k}", (NT * P, TW)) for k in range(LAYERS)]
        x1_tab = dram("x1_tab", (NT * P, C))

        ring = sb("ring", [P, RING * AW])
        acc = sb("acc", [P, NT * AW])
        oh = sb("oh", [P, RING * P])
        dloc = sb("dloc", [P, SX])
        sidx = sb("sidx", [P, SX], I32)
        endt = sb("endt", [P, SX])
        tpk = sb("tpk", [1, SX // 4], I32)
        iota = sb("iota", [P, P])
        ident = sb("ident", [P, P])
        ones = sb("ones", [P, P])
        zrow = sb("zrow", [P, AW])
        onorm = sb("onorm", [P, NT])
        inorm = sb("inorm", [P, NT])
        indeg0 = sb("indeg0", [P, NT])
        stat = sb("stat", [P, NT * 2])
        bnst = sb("bnst", [P, 2 * 6])
        rstd = sb("rstd", [P, NT])
        nbias = sb("nbias", [P, NT])
        wc = sb("wc", [P, 2 * C])
        wcat = sb("wcat", [P, 2 * PW])
        bias = sb("bias", [P, C])
        att = sb("att", [P, 2 * C])
        nb = sb("nb", [P, 2 * C])
        aT = sb("aT", [P, 2 * C])
        tmp = sb("tmp", [P, 2 * C])
        tv = sb("tv", [P, NT * 2 * H])
        ohT = sb("ohT", [P, 2 * 4 * P])
        idx = sb("idx", [P, 2 * G], I32)
        ad = sb("ad", [P, G * 2 * H])
        sfl = sb("sfl", [P, 2 * P])
        efl = sb("efl", [P, 2 * P])
        rsf = sb("rsf", [1, 2 * H * G])
        ref = sb("ref", [1, 2 * H * G])
        v = sb("v", [P, P])
        f1 = sb("f1", [P, P])
        r1 = sb("r1", [P, P])
        f2 = sb("f2", [P, P])
        r2 = sb("r2", [P, P])
        mrow = sb("mrow", [P, P])
        alpha = sb("alpha", [P, P])
        mx = sb("mx", [P, P])
        t1 = sb("t1", [P, P])
        t2 = sb("t2", [P, P])
        dd = sb("dd", [P, 2 * P])
        eself = sb("eself", [P, P])
        cin = sb("cin", [P, 2])
        cw = sb("cw", [1, H * G])
        dw = sb("dw", [1, H * G])
        co = sb("co", [1, H * G])
        do = sb("do", [1, H * G])
        rlast = sb("rlast", [1, 2])
        nxt = sb("nxt", [1, H])
        sm4 = sb("sm4", [1, 4 * H + 1])
        lf = sb("lf", [1, H])
        resc = sb("resc", [P, H])
        es = sb("es", [P, NT * H])
        rs = sb("rs", [P, NT * H])

        main = [ctx.enter_context(nc.psum_tensor(f"main{i}", [P, 512], F32)) for i in range(4)]
        pso = [ctx.enter_context(nc.psum_tensor(f"pso{i}", [P, 512], F32)) for i in range(2)]
        psad = ctx.enter_context(nc.psum_tensor("psad", [P, 512], F32))
        psb = ctx.enter_context(nc.psum_tensor("psb", [P, 512], F32))

        ring3 = ring[:, :].rearrange("p (s w) -> p s w", w=AW)
        acc3 = acc[:, :].rearrange("p (t w) -> p t w", w=AW)
        xr = ring[:, 0:NT * C].rearrange("p (t c) -> p t c", c=C)
        xa = acc[:, 0:NT * C].rearrange("p (t c) -> p t c", c=C)
        stage = oh[:, 0:2 * TB * AW].rearrange("p (b t w) -> p b t w", b=2, w=AW)
        stat3 = stat[:, :].rearrange("p (t k) -> p t k", k=2)
        tv3 = tv[:, :].rearrange("p (t k) -> p t k", k=2 * H)
        es3 = es[:, :].rearrange("p (t h) -> p t h", h=H)
        rs3 = rs[:, :].rearrange("p (t h) -> p t h", h=H)
        ad3 = ad[:, :].rearrange("p (g k) -> p g k", k=2 * H)

        def hg(ap):
            return ap.rearrange("p (h g) -> p h g", h=H)

        asrc_dst = ad3[:, :, 0:H].rearrange("p g h -> p h g")
        adst_dst = ad3[:, :, H:2 * H].rearrange("p g h -> p h g")

        def slot(b):
            return ring3[:, b * G:(b + 1) * G, :]

        lin = ring[:, 0:EC].bitcast(I32)
        lo_i = ring[:, EC:2 * EC].bitcast(I32)
        hi_i = ring[:, 2 * EC:3 * EC].bitcast(I32)
        lo_b = ring[:, 3 * EC:3 * EC + EC // 2].bitcast(BF16)
        hi_b = ring[:, 3 * EC + EC // 2:4 * EC].bitcast(BF16)
        dlin = ring[:, 4 * EC:5 * EC].bitcast(I32)
        dlin_f = ring[:, 5 * EC:6 * EC]
        sgn = ring[:, 6 * EC:7 * EC]
        o_lo, o_hi = 7 * EC, 7 * EC + HB * P
        oh_lo = ring[:, o_lo:o_hi].bitcast(BF16).rearrange("p (b k n) -> p b k n", b=2, n=P)
        oh_hi = ring[:, o_hi:o_hi + HB * NT].bitcast(BF16).rearrange("p (b k n) -> p b k n", b=2, n=NT)
        o_c = o_hi + HB * NT
        iota_b = ring[:, o_c:o_c + P // 2].bitcast(BF16)
        zero_b = ring[:, o_c + P // 2:o_c + P].bitcast(BF16)
        o_c += P
        thr = ring[:, o_c:o_c + NT]
        cnt = ring[:, o_c + NT:o_c + 2 * NT]
        bf = ring[:, o_c + 2 * NT:o_c + 3 * NT]
        bi = ring[:, o_c + 3 * NT:o_c + 4 * NT].bitcast(I32)
        fl = ring[:, o_c + 4 * NT:o_c + 5 * NT].bitcast(I32)
        ce = ring[:, o_c + 5 * NT:o_c + 6 * NT].bitcast(I32)
        ov = ring[:, o_c + 6 * NT:o_c + 7 * NT]
        pre = ring[:, o_c + 7 * NT:o_c + 8 * NT]
        cum = ring[:, o_c + 8 * NT:o_c + 9 * NT]
        zt = ring[:, o_c + 9 * NT:o_c + 10 * NT]
        o_c += 10 * NT
        sid = ring[:, o_c:o_c + SB]
        ts = ring[:, o_c + SB:o_c + 2 * SB]
        cs = ring[:, o_c + 2 * SB:o_c + 3 * SB]
        ci = ring[:, o_c + 3 * SB:o_c + 4 * SB].bitcast(I32)
        tsc = ring[:, o_c + 4 * SB:o_c + 5 * SB]
        t128 = ring[:, o_c + 5 * SB:o_c + 6 * SB]
        sany = ring[:, o_c + 6 * SB:o_c + 7 * SB]
        eany = ring[:, o_c + 7 * SB:o_c + 8 * SB]
        padi = ring[0:1, o_c + 8 * SB:o_c + 8 * SB + P].bitcast(I32)
        strayf = ring[0:1, o_c + 8 * SB + P:o_c + 8 * SB + P + 2]
        o_c += 8 * SB + P + 2
        assert o_c <= RING * AW
        srow = oh[:, 0:SX].bitcast(I32)
        drow = oh[:, SX:2 * SX].bitcast(I32)
        key = oh[:, 2 * SX:2 * SX + SB * (P + 2)].rearrange("p (b e) -> p b e", e=P + 2)
        o_k = 2 * SX + SB * (P + 2)
        srowf = oh[:, o_k:o_k + SX]
        dl = oh[:, o_k + SX:o_k + 2 * SX]
        sfr = oh[:, o_k + 2 * SX:o_k + 3 * SX]
        assert o_k + 3 * SX <= RING * P
        efr = ohT[:, 0:SX]
        cmpt = dloc[:, 0:SB * NT].rearrange("p (b t) -> p b t", t=NT)
        cmpo = endt[:, 0:SB * NT].rearrange("p (b t) -> p b t", t=NT)
        trow = sb("trow", [1, SX])
        tsum = sb("tsum", [1, SX // 4])

        def b3(ap):
            return ap.rearrange("p (b e) -> p b e", e=P)

        def bc(ap, shape):
            return ap.to_broadcast(shape)

        edges_in = sem("edges_in")
        pads_set = sem("pads_set")
        pads_out = sem("pads_out")
        lin_in = sem("lin_in")
        x_in = sem("x_in")
        consts = sem("consts")
        pool_chain = sem("pool_chain")
        dve_chain = sem("dve_chain")
        act_chain = sem("act_chain")
        hist_onehots = sem("hist_onehots")
        hist_done = sem("hist_done")
        dlin_ready = sem("dlin_ready")
        counts_ready = sem("counts_ready")
        counts_sum = sem("counts_sum")
        chunks_ready = sem("chunks_ready")
        rows_in = sem("rows_in")
        rowsf_ready = sem("rowsf_ready")
        rowsT_done = sem("rowsT_done")
        rowsT_read = sem("rowsT_read")
        key_out = sem("key_out")
        key_edge = sem("key_edge")
        flags_ready = sem("flags_ready")
        flags_out = sem("flags_out")
        tiles_out = sem("tiles_out")
        tiles_in = sem("tiles_in")
        steps_ready = sem("steps_ready")
        norm_in = sem("norm_in")
        norm_sq = sem("norm_sq")
        norm_ready = sem("norm_ready")
        ln_rows = sem("ln_rows")
        acc_clear = sem("acc_clear")
        table_stored = sem("table_stored")
        gathered = [sem(f"gathered{j}") for j in range(U)]
        idx_in = [sem(f"idx_in{j}") for j in range(2)]
        group_in = [sem(f"group_in{j}") for j in range(2)]
        onehots = sem("onehots")
        products_done = sem("products_done")
        added = sem("added")
        w_in = sem("w_in")
        wcat_ready = sem("wcat_ready")
        nb_ready = sem("nb_ready")
        rows_T = sem("rows_T")
        rows_T_copied = sem("rows_T_copied")
        projected = sem("projected")
        proj_read = sem("proj_read")
        staged = sem("staged")
        mid_ready = sem("mid_ready")
        back_in = sem("back_in")
        rest_in = sem("rest_in")
        stored = sem("stored")
        ohT_done = sem("ohT_done")
        ohT_copied = sem("ohT_copied")
        logits_done = sem("logits_done")
        ad_ready = sem("ad_ready")
        flags_in = [sem(f"flags_in{j}") for j in range(2)]
        v_ready = sem("v_ready")
        vT_done = sem("vT_done")
        scan_ready = sem("scan_ready")
        ends_done = sem("ends_done")
        carry_ready = sem("carry_ready")
        carry_done = sem("carry_done")
        max_ready = sem("max_ready")
        maxT_done = sem("maxT_done")
        expo_ready = sem("expo_ready")
        lf_done = sem("lf_done")
        e_ready = sem("e_ready")
        factor_ready = sem("factor_ready")
        weighted_v = sem("weighted_v")
        weighted_a = sem("weighted_a")
        self_ready = sem("self_ready")
        nself = sem("nself")

        def tile_number(value):
            return nc.s_assert_within(value, 0, NT - 1, skip_runtime_bounds_check_because="clamped on the chip before it is packed")

        ONES_COL = C
        FLAG_INCS = 16 * (4 * H + 1)

        def oh_base(k):
            return min(k, HOPS) * (S + AHEAD) + max(k - HOPS, 0) * (S + G)

        def rows_of(tab, i, width):
            return tab.rearrange("(t p) c -> p t c", p=P)[:, bass.ds(i * TB, TB), 0:width]

        block = ctx.enter_context(nc.Block())

        @block.sync
        def _(sp):
            sp.dma_start(src_pad.rearrange("a b -> (a b)")[0:E].rearrange("(k f) -> k f", k=16),
                         src.rearrange("(k f) -> k f", k=16)).then_inc(edges_in, 16)
            sp.dma_start(dst_pad.rearrange("a b -> (a b)")[0:E].rearrange("(k f) -> k f", k=16),
                         dst.rearrange("(k f) -> k f", k=16)).then_inc(edges_in, 16)
            for q in range(7):
                sp.dma_start(xa[:, q * TB:min((q + 1) * TB, NFULL), :],
                             x[q * TB * P:min((q + 1) * TB, NFULL) * P, :].rearrange("(t p) c -> p t c", p=P)
                             ).then_inc(x_in, 16)
            sp.wait_ge(pads_set, 2)
            sp.dma_start(xa[0:NREST, NFULL, :], x[NFULL * P:N, :]).then_inc(x_in, 16)
            sp.dma_start(src_pad[EC - 1:EC, P - EPAD:P], padi[0:1, 0:EPAD]).then_inc(pads_out, 16)
            sp.dma_start(dst_pad[EC - 1:EC, P - EPAD:P], padi[0:1, 0:EPAD]).then_inc(pads_out, 16)
            sp.dma_start(keys[0:1, 0:1], strayf[0:1, 0:1]).then_inc(pads_out, 16)
            sp.dma_start(keys[0:1, SX * P + 1:SX * P + 2], strayf[0:1, 1:2]).then_inc(pads_out, 16)
            sp.wait_ge(edges_in, 32)
            sp.wait_ge(pads_out, 64)
            sp.dma_start(lin, src_pad.rearrange("a b -> (a b)").rearrange("(p f) -> p f", p=P)).then_inc(lin_in, 16)
            sp.wait_ge(lin_in, 16)
            sp.dma_start(dlin, dst_pad.rearrange("a b -> (a b)").rearrange("(p f) -> p f", p=P)).then_inc(lin_in, 16)

            sp.wait_ge(chunks_ready, 2)
            sp.dma_start(keys[0:1, 1:1 + SX * P].rearrange("o (b p e) -> (o p) b e", p=P, e=P),
                         key[:, :, 1:P + 1]).then_inc(key_out, 16)
            with nc.allow_non_contiguous_dma(reason="one element of each step"):
                sp.dma_start(tile_of.rearrange("o (b p) -> (o p) b", p=P), tsc).then_inc(tiles_out, 16)
                sp.wait_ge(key_out, 16)
                kv = keys[0:1, 0:SX * P].rearrange("o (b p e) -> (o p) b e", p=P, e=P)
                sp.dma_start(key[:, :, 0:1], kv[:, :, 0:1]).then_inc(key_edge, 16)
                kn = keys[0:1, 2:SX * P + 2].rearrange("o (b p e) -> (o p) b e", p=P, e=P)
                sp.dma_start(key[:, :, P + 1:P + 2], kn[:, :, P - 1:P]).then_inc(key_edge, 16)
                sp.wait_ge(tiles_out, 16)
                sp.dma_start(trow[0:1, :], tile_of).then_inc(tiles_in, 16)
                sp.wait_ge(flags_ready, 1)
                sp.dma_start(start_rows.rearrange("(b p) e -> p b e", p=P), b3(sfr)).then_inc(flags_out, 16)
                sp.dma_start(end_rows.rearrange("(b p) e -> p b e", p=P), b3(efr)).then_inc(flags_out, 16)
                sp.dma_start(start_any.rearrange("o (b p) -> (o p) b", p=P), sany).then_inc(flags_out, 16)
                sp.dma_start(end_any.rearrange("o (b p) -> (o p) b", p=P), eany).then_inc(flags_out, 16)

            for q in range(NI):
                sp.wait_ge(ln_rows, TB * (q + 1))
                sp.dma_start(conv_tab[0].rearrange("(t p) c -> p t c", p=P)[:, q * TB:(q + 1) * TB, :],
                             xa[:, q * TB:(q + 1) * TB, :]).then_inc(table_stored, 16)

            def store_stage(table, width, m):
                with nc.sync.Fori(0, NI) as i:
                    sp.wait_ge(staged, 2 + m * NT + i * TB + TB)
                    sp.dma_start(rows_of(table, i, width), stage[:, 0, :, 0:width]).then_inc(table_stored, 16)

            def fetch_idx(b, col, width):
                sp.dma_start(idx[:, b * G:b * G + width], sidx[:, bass.ds(col, width)]).then_inc(idx_in[b], 16)

            for k in range(HOPS):
                if k:
                    sp.wait_ge(staged, 2 + k * NT)
                sp.dma_start(wc[:, :].rearrange("p (b n) -> p b n", b=2),
                             gw[k].rearrange("(b p) n -> p b n", p=P)).then_inc(w_in, 16)
                sp.dma_start(bias[:, :], gb[k:k + 1, :].to_broadcast([P, C])).then_inc(w_in, 16)
                if k == 0:
                    sp.wait_ge(steps_ready, 1)
                with nc.sync.Fori(0, S // U) as i:
                    for b in range(2):
                        sp.wait_ge(products_done, k * S + i * U + (b + 1) * UH)
                        fetch_idx(b, i * U + b * UH, UH)
                if k < HOPS - 1:
                    store_stage(conv_tab[k + 1], C, k)
                else:
                    sp.wait_ge(added, 4 + HOPS * S)
                    for q in range(NI):
                        a, b = q * TB, min((q + 1) * TB, NFULL)
                        sp.dma_start(xr[:, a:b, :], x[a * P:b * P, :].rearrange("(t p) c -> p t c", p=P)
                                     ).then_inc(back_in, 16)
                        if q == 0:
                            sp.dma_start(xr[0:NREST, NFULL, :], x[NFULL * P:N, :]).then_inc(rest_in, 16)
                        sp.wait_ge(back_in, 16 * (q + 1))
                    with nc.sync.Fori(0, NI) as i:
                        sp.wait_ge(mid_ready, i * TB + TB)
                        sp.dma_start(rows_of(x1_tab, i, C), acc3[:, bass.ds(i * TB, TB), 0:C]).then_inc(stored, 16)

            for l in range(LAYERS):
                w, s_, d_ = ((w1, as1, ad1), (w2, as2, ad2))[l]
                if l:
                    sp.wait_ge(projected, 2 + (HOPS + l) * NT)
                sp.dma_start(wcat[:, :].rearrange("p (b n) -> p b n", b=2)[:, :, 0:C],
                             w.rearrange("(b p) n -> p b n", p=P)).then_inc(w_in, 16)
                sp.dma_start(att[:, 0:C], s_.rearrange("o h c -> o (h c)").to_broadcast([P, C])).then_inc(w_in, 16)
                sp.dma_start(att[:, C:2 * C], d_.rearrange("o h c -> o (h c)").to_broadcast([P, C])).then_inc(w_in, 16)
                store_stage(attn_tab[l], TW, HOPS - 1 + l)
                sp.wait_ge(mid_ready, (l + 1) * NT)
                sp.dma_start(bias[:, :], (b1, b2)[l].rearrange("(o c) -> o c", o=1).to_broadcast([P, C])).then_inc(w_in, 16)
                if l == 0:
                    sp.wait_ge(flags_out, 64)
                with nc.sync.Fori(0, NG // 2) as it:
                    for b in range(2):
                        sp.wait_ge(max_ready, l * NG + it * 2 + b + 1)
                        g0 = it * 2 * G + b * G
                        sp.wait_ge(v_ready, l * NG + it * 2 + b + 1)
                        fetch_idx(b, g0, G)
                        for h in range(H):
                            sp.dma_start(sfl[h * G:(h + 1) * G, b * P:(b + 1) * P],
                                         start_rows[bass.ds(g0, G), :]).then_inc(flags_in[b], 16)
                            sp.dma_start(efl[h * G:(h + 1) * G, b * P:(b + 1) * P],
                                         end_rows[bass.ds(g0, G), :]).then_inc(flags_in[b], 16)
                            o = (b * H + h) * G
                            sp.dma_start(rsf[0:1, o + 1:o + G], start_any[0:1, bass.ds(g0, G - 1)]).then_inc(flags_in[b], 16)
                            sp.dma_start(ref[0:1, o:o + G - 1], end_any[0:1, bass.ds(g0 + 1, G - 1)]).then_inc(flags_in[b], 16)
                        sp.dma_start(rlast[0:1, b:b + 1], start_any[0:1, bass.ds(g0 + G - 1, 1)]).then_inc(flags_in[b], 16)
                sp.wait_ge(added, 4 + (HOPS + l + 1) * S)
                for q in range(NI):
                    sp.dma_start(xr[:, q * TB:(q + 1) * TB, :],
                                 attn_tab[l].rearrange("(t p) c -> p t c", p=P)[:, q * TB:(q + 1) * TB, 0:C]
                                 ).then_inc(back_in, 16)
                    sp.wait_ge(back_in, 16 * (NI + l * NI + q + 1))
            for q in range(NI):
                sp.wait_ge(mid_ready, 2 * NT + TB * (q + 1))
                sp.dma_start(xr[:, q * TB:(q + 1) * TB, :],
                             x1_tab.rearrange("(t p) c -> p t c", p=P)[:, q * TB:(q + 1) * TB, :]
                             ).then_inc(back_in, 16)
                sp.wait_ge(back_in, 16 * (3 * NI + q + 1))
            for q in range(NI):
                a, b = q * TB, min((q + 1) * TB, NFULL)
                sp.wait_ge(mid_ready, 3 * NT + TB * (q + 1))
                sp.dma_start(out[a * P:b * P, :].rearrange("(t p) c -> p t c", p=P), acc3[:, a:b, 0:C]
                             ).then_inc(stored, 16)
            sp.dma_start(out[NFULL * P:N, :], acc3[0:NREST, NFULL, 0:C]).then_inc(stored, 16)
            sp.wait_ge(stored, 16 * (2 * NI + 1))
            sp.wait_ge(table_stored, 16 * NI * (HOPS + LAYERS))

        @block.gpsimd
        def _(pool):
            chain = [0]

            def link(ins):
                chain[0] += 1
                ins.then_inc(pool_chain, 1)
                pool.wait_ge(pool_chain, chain[0])

            nc.gpsimd.memset(padi, OUTSIDE).then_inc(pads_set, 1)
            link(nc.gpsimd.memset(strayf, -5.0))
            nc.gpsimd.memset(xa[:, NFULL, :], 0.0).then_inc(pads_set, 1)
            link(nc.gpsimd.memset(ident[:, :], 0.0))
            link(nc.gpsimd.affine_select(out=ident[:, :], in_=ident[:, :], compare_op=ALU.not_equal, fill=1.0,
                                         base=0, pattern=[[-1, P]], channel_multiplier=1))
            link(nc.gpsimd.memset(ones[:, :], 1.0))
            link(nc.gpsimd.memset(zt, 0.0))
            link(nc.gpsimd.memset(zrow[:, :], 0.0))
            link(nc.gpsimd.iota(iota[:, :], pattern=[[1, P]], base=0, channel_multiplier=0,
                                allow_small_or_imprecise_dtypes=True))
            link(nc.gpsimd.iota(iota_b, pattern=[[1, P]], base=0, channel_multiplier=0,
                                allow_small_or_imprecise_dtypes=True))
            link(nc.gpsimd.iota(thr, pattern=[[P, NT]], base=P, channel_multiplier=0,
                                allow_small_or_imprecise_dtypes=True))
            link(nc.gpsimd.iota(sid, pattern=[[P, SB]], base=0, channel_multiplier=1,
                                allow_small_or_imprecise_dtypes=True))
            nc.gpsimd.memset(zero_b, 0.0).then_inc(consts, 1)

            pool.wait_ge(chunks_ready, 1)
            pool.wait_ge(lin_in, 32)
            for b in range(SB):
                for row, tab in ((srow, src_pad), (drow, dst_pad)):
                    pool.indirect_dma_start(b3(row)[:, b, :], None, tab,
                                            bass.IndirectOffsetOnAxis(ap=ci[:, b:b + 1], axis=0)
                                            ).then_inc(rows_in, 16)

            def clear_first():
                pool.wait_ge(table_stored, 16 * NI)
                with nc.gpsimd.Fori(0, NT) as i:
                    pool.nop(nofuse=True)
                    nc.gpsimd.tensor_copy(acc[:, bass.ds(i * AW, AW)], zrow[:, :]).then_inc(acc_clear, 1)

            def feed(k):
                pool.wait_ge(added, 4 + (k + 1) * S)
                if k == 0:
                    pool.wait_ge(norm_in, 3)
                with nc.gpsimd.Fori(0, NI) as i:
                    for j in range(TB):
                        t = i * TB + j
                        pool.wait_ge(rows_T, CR + k * NT + t + (0 if j == 0 else -1))
                        pool.nop(nofuse=True)
                        nc.gpsimd.tensor_copy(nb[:, (j % 2) * C:(j % 2 + 1) * C], acc[:, bass.ds(t * AW, C)]
                                              ).then_inc(nb_ready, 1)
                        if k < HOPS - 1:
                            pool.wait_ge(nb_ready, k * NT + t + 1)
                            pool.nop(nofuse=True)
                            nc.gpsimd.tensor_copy(acc[:, bass.ds(t * AW, AW)], zrow[:, :]).then_inc(acc_clear, 1)

            def clear(m):
                with nc.gpsimd.Fori(0, NT) as i:
                    pool.wait_ge(nb_ready, m * NT + i + 1)
                    pool.nop(nofuse=True)
                    nc.gpsimd.tensor_copy(acc[:, bass.ds(i * AW, AW)], zrow[:, :]).then_inc(acc_clear, 1)

            def gather_conv(k):
                pool.wait_ge(table_stored, 16 * NI * (k + 1))
                with nc.gpsimd.Fori(0, S // U) as i:
                    for j in range(U):
                        if j % UH == 0:
                            pool.wait_ge(idx_in[j // UH], 16 * k * (S // U) + i * 16 + 16)
                        pool.wait_ge(products_done, k * S + i * U + j + 1)
                        pool.nop(nofuse=True)
                        pool.indirect_dma_start(ring3[:, j, 0:C], None, conv_tab[k],
                                                bass.IndirectOffsetOnAxis(ap=idx[:, (j // UH) * G + j % UH:(j // UH) * G + j % UH + 1], axis=0)
                                                ).then_inc(gathered[j], 16)

            def gather_attn(l):
                pool.wait_ge(table_stored, 16 * NI * (HOPS + l + 1))
                with nc.gpsimd.Fori(0, NG // 2) as i:
                    for j in range(2 * G):
                        if j % G == 0:
                            pool.wait_ge(idx_in[j // G], 16 * (HOPS * (S // U) + l * (NG // 2)) + i * 16 + 16)
                        pool.wait_ge(products_done, CR + (HOPS + l) * S + i * 2 * G + j + 1 - 2 * G)
                        pool.nop(nofuse=True)
                        pool.indirect_dma_start(ring3[:, j, 0:TW], None, attn_tab[l],
                                                bass.IndirectOffsetOnAxis(ap=idx[:, j:j + 1], axis=0)
                                                ).then_inc(group_in[j // G], 16)

            clear_first()
            pool.wait_ge(steps_ready, 1)
            link(nc.gpsimd.memset(xr[:, NFULL, :], 0.0))
            nc.gpsimd.memset(ring3[:, 0:U, ONES_COL:ONES_COL + 1], 1.0).then_inc(steps_ready, 1)
            for k in range(HOPS):
                gather_conv(k)
                feed(k)
            pool.wait_ge(stored, 16 * NI)
            clear(HOPS)
            for l in range(LAYERS):
                gather_attn(l)
                pool.wait_ge(nself, l + 1)
                with nc.gpsimd.Fori(0, NI) as i:
                    pool.wait_ge(back_in, 16 * (NI + l * NI) + i * 16 + 16)
                    for j in range(TB):
                        r4 = ring[:, bass.ds((i * TB + j) * C, C)].rearrange("p (h c) -> p h c", h=H)
                        e4 = es[:, bass.ds((i * TB + j) * H, H)].rearrange("p (h o) -> p h o", o=1).to_broadcast([P, H, CH])
                        nc.gpsimd.tensor_tensor(r4, r4, e4, ALU.mult).then_inc(self_ready, 1)
                if l < LAYERS - 1:
                    clear(HOPS + 1)

        @block.scalar
        def _(act):
            chain = [0]

            def link(ins):
                chain[0] += 1
                ins.then_inc(act_chain, 1)
                act.wait_ge(act_chain, chain[0])

            act.wait_ge(consts, 1)
            nc.scalar.copy(t1[:, 1:2], ones[:, 0:1]).then_inc(staged, 2)
            act.wait_ge(dlin_ready, 1)
            for t in range(NT):
                link(nc.scalar.activation(sgn, dlin_f, ACT.Sign, scale=-1.0, bias=thr[:, t:t + 1],
                                          accum_out=cnt[:, t:t + 1]))
            nc.scalar.copy(t1[:, 0:1], cnt[:, 0:1]).then_inc(counts_ready, 1)

            def root(dst_, n):
                act.wait_ge(norm_in, n)
                nc.scalar.activation(dst_, dst_, ACT.Sqrt).then_inc(norm_sq, 1)

            root(rstd[:, :], 1)
            root(onorm[:, :], 2)
            act.wait_ge(norm_ready, 1)
            for t in range(NT):
                nc.scalar.activation(xa[:, t, :], xa[:, t, :], ACT.Relu, scale=rstd[:, t:t + 1],
                                     bias=nbias[:, t:t + 1]).then_inc(ln_rows, 1)

            for k in range(HOPS - 1):
                if k == 0:
                    root(inorm[:, :], 3)
                with nc.scalar.Fori(0, NI) as i:
                    act.wait_ge(table_stored, 16 * (NI * (k + 1)) + i * 16)
                    for j in range(TB):
                        act.wait_ge(proj_read, 2 + k * NT + i * TB + j + 1)
                        nc.scalar.activation(stage[:, 0, j, 0:C], tmp[:, (j % 2) * C:(j % 2 + 1) * C], ACT.Relu,
                                             scale=onorm[:, bass.ds(i * TB + j, 1)]).then_inc(staged, 1)
            root(rstd[:, :], 4)
            act.wait_ge(norm_ready, 2)
            def feed(m, ready, scaled):
                with nc.scalar.Fori(0, NI) as i:
                    for j in range(TB):
                        t = i * TB + j
                        act.wait_ge(ready[0], ready[1] + t + 1)
                        act.wait_ge(rows_T, CR + m * NT + t + (0 if j == 0 else -1))
                        to, a = nb[:, (j % 2) * C:(j % 2 + 1) * C], acc[:, bass.ds(t * AW, C)]
                        if scaled:
                            nc.scalar.activation(to, a, ACT.Relu, scale=rstd[:, bass.ds(t, 1)],
                                                 bias=nbias[:, bass.ds(t, 1)]).then_inc(nb_ready, 1)
                        else:
                            nc.scalar.activation(to, a, ACT.Relu).then_inc(nb_ready, 1)

            feed(HOPS, (mid_ready, 0), True)

            for l in range(LAYERS):
                def copy_quad(q, qq):
                    act.wait_ge(ohT_done, q + 1)
                    act.wait_ge(logits_done, q + 1)
                    nc.scalar.copy(ohT[:, (qq % 2) * 4 * P:(qq % 2 + 1) * 4 * P], pso[qq % 2][:, :]
                                   ).then_inc(ohT_copied, 1)

                qb = l * (NG + 1) * (G // 4)
                for q in range(G // 4):
                    copy_quad(qb + q, q)
                with nc.scalar.Fori(0, NG // 2) as it:
                    for b in range(2):
                        gg = l * NG + it * 2 + b
                        act.wait_ge(logits_done, it * 2 * (G // 4) + (2 + qb + (b + 1) * (G // 4)))
                        nc.scalar.copy(ad[:, :], psad[:, 0:G * 2 * H]).then_inc(ad_ready, 1)
                        act.wait_ge(expo_ready, gg + 1)
                        nc.scalar.activation(slot(b)[:, :, C:C + H].rearrange("p g h -> p h g"),
                                             hg(dd[:, 0:P]), ACT.Exp).then_inc(e_ready, 1)
                        nc.scalar.activation(eself[:, :], dd[:, P:2 * P], ACT.Exp).then_inc(e_ready, 1)
                        act.wait_ge(lf_done, gg + 1)
                        nc.scalar.activation(resc[:, :], psb[:, 260:260 + H], ACT.Exp).then_inc(factor_ready, 1)
                        act.wait_ge(e_ready, l * NG * 2 + it * 4 + (b + 1) * 2)
                        for q in range(G // 4):
                            copy_quad(it * 2 * (G // 4) + (qb + (b + 1) * (G // 4) + q), q)
                            for k in range(4 * q, 4 * q + 4):
                                for h in range(DVEC // CH, H):
                                    r = ring3[:, b * G + k, h * CH:(h + 1) * CH]
                                    nc.scalar.activation(r, r, ACT.Copy, scale=ring3[:, b * G + k, C + h:C + h + 1]
                                                         ).then_inc(weighted_a, 1)
                if l < LAYERS - 1:
                    feed(HOPS + 1, (mid_ready, NT), False)

        @block.tensor
        def _(pe):
            pe.wait_ge(consts, 1)
            nc.tensor.matmul(psad[:, 0:NT], zero_b, zero_b[:, 0:NT], start=True, stop=False,
                             skip_group_check=True).then_inc(products_done, CR)
            nc.tensor.matmul(psb[:, 0:2], ident[:, :], ident[:, 0:2], start=True, stop=True).then_inc(hist_done, 2)
            nc.tensor.matmul(psb[:, 0:2], ident[:, :], ident[:, 0:2], start=True, stop=True).then_inc(rows_T, CR)
            nc.tensor.matmul(psb[:, 0:2], ident[:, :], ident[:, 0:2], start=True, stop=True).then_inc(logits_done, 2)
            nc.tensor.matmul(psb[:, 0:2], ident[:, :], ident[:, 0:2], start=True, stop=True).then_inc(projected, 2)
            def hist(first, end):
                with nc.tensor.Fori(first, end) as i:
                    for b in range(2):
                        pe.wait_ge(hist_onehots, 2 * i + b + 1)
                        for j in range(HB):
                            mm = nc.tensor.matmul(psad[:, 0:NT], oh_lo[:, b, j, :], oh_hi[:, b, j, :], start=False,
                                                  stop=False, skip_group_check=True)
                        mm.then_inc(hist_done, 1)

            hist(0, NH // 2)
            pe.wait_ge(counts_ready, 1)
            nc.tensor.matmul(main[0][:, 0:NT], ones[:, :], cnt, start=True, stop=True).then_inc(counts_sum, 1)
            hist(NH // 2, NH)
            nc.tensor.matmul(psad[:, 0:NT], zero_b, zero_b[:, 0:NT], start=False, stop=True,
                             skip_group_check=True).then_inc(hist_done, 1)
            n = 0
            for tabl, w in ((srowf, 1), (dl, 1), (efr, 2)):
                pe.wait_ge(rowsf_ready, w)
                for b in range(SB):
                    if n >= 4:
                        pe.wait_ge(rowsT_read, n - 3)
                    nc.tensor.transpose(main[n % 4][:, 0:P], b3(tabl)[:, b, :], ident[:, :]).then_inc(rowsT_done, 1)
                    n += 1

            def conv(k):
                with nc.tensor.Fori(0, S // U) as i:
                    for j in range(U):
                        pe.wait_ge(onehots, oh_base(k) + i * U + j + 1)
                        pe.wait_ge(added, k * S + i * U + j + 1)
                        pe.wait_ge(gathered[j], 16 * k * (S // U) + i * 16 + 16)
                        nc.tensor.matmul(main[j % 4][:, 0:C + 1], oh[:, (j % OHR) * P:(j % OHR + 1) * P],
                                         ring3[:, j, 0:C + 1], start=True, stop=True).then_inc(products_done, 1)

            def project(m, weights, width):
                def turn(i, j):
                    pe.wait_ge(nb_ready, m * NT + i * TB + j + 1)
                    pe.wait_ge(rows_T_copied, m * NT + i * TB + j + (2 if j == 0 else 1))
                    for b in range(2):
                        mm = nc.tensor.transpose(pso[j % 2][:, b * P:(b + 1) * P],
                                                 nb[:, (j % 2) * C + b * P:(j % 2) * C + (b + 1) * P], ident[:, :])
                    mm.then_inc(rows_T, 1)

                def multiply(i, j):
                    pe.wait_ge(rows_T_copied, m * NT + i * TB + j + 3)
                    pe.wait_ge(proj_read, m * NT + i * TB + j + (2 if j == 0 else 1))
                    for b in range(2):
                        mm = nc.tensor.matmul(main[j % 2][:, 0:width], aT[:, (j % 2) * C + b * P:(j % 2) * C + (b + 1) * P],
                                              weights[:, b * width:(b + 1) * width], start=b == 0, stop=b == 1)
                    mm.then_inc(projected, 1)

                with nc.tensor.Fori(0, NI) as i:
                    turn(i, 0)
                    for j in range(TB):
                        if j < TB - 1:
                            turn(i, j + 1)
                        multiply(i, j)

            for k in range(HOPS):
                conv(k)
                pe.wait_ge(added, 4 + (k + 1) * S)
                pe.wait_ge(w_in, 32 * (k + 1))
                project(k, wc, C)
            for l in range(LAYERS):
                pe.wait_ge(wcat_ready, l + 1)
                project(HOPS + l, wcat, PW)
                qb = l * (NG + 1) * (G // 4)

                def turn_quad(n, b, q):
                    pe.wait_ge(onehots, n * 4 + (oh_base(HOPS + l) - qb * 4 + 4 * q + 4))
                    pe.wait_ge(ohT_copied, n + q + 1)
                    for k in range(4 * q, 4 * q + 4):
                        mm = nc.tensor.transpose(pso[q % 2][:, (k % 4) * P:(k % 4 + 1) * P],
                                                 oh[:, (b * G + k) * P:(b * G + k + 1) * P], ident[:, :])
                    mm.then_inc(ohT_done, 1)

                def logit_quad(n, step0, q):
                    pk = pe.value_load(tpk[0:1, bass.ds(step0 + q, 1)], min_val=0, max_val=(1 << 24) - 1)
                    pe.wait_ge(ohT_copied, n + q + 3)
                    for k in range(4):
                        t = tile_number((pk >> (6 * k)) & 63)
                        mm = nc.tensor.matmul(psad[:, (4 * q + k) * 2 * H:(4 * q + k + 1) * 2 * H],
                                              ohT[:, ((q % 2) * 4 + k) * P:((q % 2) * 4 + k + 1) * P],
                                              tv[:, bass.ds(t * 2 * H, 2 * H)], start=True, stop=True)
                    mm.then_inc(logits_done, 1)

                for q in range(G // 4):
                    turn_quad(qb, 0, q)
                    logit_quad(qb, 0, q)
                with nc.tensor.Fori(0, NG // 2) as it:
                    for b in range(2):
                        gg = l * NG + it * 2 + b
                        pe.wait_ge(v_ready, 2 + gg + 1)
                        nc.tensor.transpose(psb[:, 0:P], v[:, :], ident[:, :]).then_inc(vT_done, 1)
                        pe.wait_ge(scan_ready, gg + 1)
                        nc.tensor.transpose(psb[0:1, 2 * P:3 * P], f1[:, P - 1:P], ident[:, :])
                        nc.tensor.transpose(psb[0:1, 3 * P:4 * P], r1[:, 0:1], ident[:, :]).then_inc(ends_done, 1)
                        pe.wait_ge(carry_ready, gg + 1)
                        nc.tensor.matmul(psb[:, 2 * P:2 * P + 1], co[0:1, :], ones[0:1, 0:1],
                                         start=True, stop=True)
                        nc.tensor.matmul(psb[:, 2 * P + 1:2 * P + 2], do[0:1, :], ones[0:1, 0:1],
                                         start=True, stop=True).then_inc(carry_done, 1)
                        pe.wait_ge(max_ready, 2 + gg + 1)
                        nc.tensor.transpose(psb[:, P:2 * P], mrow[:, :], ident[:, :]).then_inc(maxT_done, 1)
                        pe.wait_ge(expo_ready, gg + 1)
                        nc.tensor.matmul(psb[:, 260:260 + H], oh[0:1, b * G * P:b * G * P + P], lf[0:1, :],
                                         start=True, stop=True).then_inc(lf_done, 1)
                        pe.wait_ge(ad_ready, gg + 1)
                        n = it * 2 * (G // 4) + (qb + (b + 1) * (G // 4))
                        for q in range(G // 4):
                            turn_quad(n, 1 - b, q)
                            for k in range(4 * q, 4 * q + 4):
                                s = (HOPS + l) * S + it * 2 * G + b * G + k
                                pe.wait_ge(added, s + 1)
                                pe.wait_ge(weighted_v, s - HOPS * S + 1)
                                pe.wait_ge(weighted_a, (s - HOPS * S + 1) * (H - DVEC // CH))
                                nc.tensor.matmul(main[k % 4][:, 0:AW], oh[:, (b * G + k) * P:(b * G + k + 1) * P],
                                                 ring3[:, b * G + k, :], start=True, stop=True).then_inc(products_done, 1)
                            logit_quad(n, it * 2 * (G // 4) + (b + 1) * (G // 4), q)

        @block.vector
        def _(dve):
            chain = [0]

            def link(ins):
                chain[0] += 1
                ins.then_inc(dve_chain, 1)
                dve.wait_ge(dve_chain, chain[0])

            link(nc.vector.memset(sm4[:, :], 0.0))
            nc.vector.memset(t2[:, :], 0.0).then_inc(added, 4)
            nc.vector.memset(f1[:, :], 0.0).then_inc(rows_T_copied, 2)
            nc.vector.memset(r1[:, :], 0.0).then_inc(proj_read, 2)
            nc.vector.memset(v[:, :], 0.0).then_inc(ohT_copied, 2)
            nc.vector.memset(alpha[:, :], 0.0).then_inc(v_ready, 2)
            nc.vector.memset(mrow[:, :], 0.0).then_inc(max_ready, 2)

            dve.wait_ge(lin_in, 16)
            link(nc.vector.tensor_scalar(hi_i, lin, 7, None, ALU.arith_shift_right))
            link(nc.vector.tensor_scalar(lo_i, lin, P - 1, None, ALU.bitwise_and))
            link(nc.vector.tensor_copy(hi_b, hi_i))
            link(nc.vector.tensor_copy(lo_b, lo_i))
            dve.wait_ge(consts, 1)
            dve.wait_ge(lin_in, 32)
            link(nc.vector.tensor_scalar(thr, thr, -0.5, None, ALU.add))
            nc.vector.tensor_copy(dlin_f, dlin).then_inc(dlin_ready, 1)

            def hist(a, b):
                with nc.vector.Fori(a, b) as i:
                    for c in range(2):
                        dve.wait_ge(hist_done, 2 * i + c + 1)
                        for to, of, n in ((oh_lo, lo_b, P), (oh_hi, hi_b, NT)):
                            mm = nc.vector.tensor_tensor(
                                to[:, c, :, :],
                                of[:, bass.ds((2 * i + c) * HB, HB)].rearrange("p (k o) -> p k o", o=1)
                                .to_broadcast([P, HB, n]),
                                iota_b[:, 0:n].rearrange("p (o n) -> p o n", o=1).to_broadcast([P, HB, n]),
                                ALU.is_equal)
                        mm.then_inc(hist_onehots, 1)

            hist(0, NH // 2)

            dve.wait_ge(counts_sum, 1)
            link(nc.vector.tensor_scalar(bf, main[0][:, 0:NT], float(EC * P), 0.5, ALU.add, ALU.mult))
            link(nc.vector.tensor_scalar(bf, bf, float(E), None, ALU.min))
            link(nc.vector.tensor_copy(bi, bf))
            link(nc.vector.tensor_scalar(fl, bi, 7, None, ALU.arith_shift_right))
            link(nc.vector.tensor_scalar(bi, bi, float(P - 1), None, ALU.add))
            link(nc.vector.tensor_scalar(ce, bi, 7, None, ALU.arith_shift_right))
            link(nc.vector.tensor_tensor(ov, ce, fl, ALU.subtract))
            link(nc.vector.tensor_tensor_scan(out=pre, data0=zt, data1=ov, initial=0.0, op0=ALU.add, op1=ALU.add))
            link(nc.vector.tensor_tensor(pre, pre, ov, ALU.subtract))
            link(nc.vector.tensor_tensor(cum, pre, ce, ALU.add))
            link(nc.vector.tensor_tensor(cmpt, sid.rearrange("p (b o) -> p b o", o=1).to_broadcast([P, SB, NT]),
                                         cum.rearrange("p (o t) -> p o t", o=1).to_broadcast([P, SB, NT]), ALU.is_ge))
            link(nc.vector.tensor_reduce(ts, cmpt, AX.X, ALU.add))
            link(nc.vector.tensor_tensor(cmpo, cmpt, ov.rearrange("p (o t) -> p o t", o=1).to_broadcast([P, SB, NT]),
                                         ALU.mult))
            link(nc.vector.tensor_reduce(cs, cmpo, AX.X, ALU.add))
            link(nc.vector.tensor_tensor(cs, sid, cs, ALU.subtract))
            link(nc.vector.tensor_scalar(cs, cs, float(EC - 1), 0.0, ALU.min, ALU.max))
            link(nc.vector.tensor_scalar(tsc, ts, float(NT - 1), None, ALU.min))
            link(nc.vector.tensor_scalar(t128, ts, float(P), None, ALU.mult))
            nc.vector.tensor_copy(ci, cs).then_inc(chunks_ready, 1)

            hist(NH // 2, NH)

            dve.wait_ge(rows_in, 16 * 2 * SB)
            tb = t128.rearrange("p (b o) -> p b o", o=1).to_broadcast([P, SB, P])
            link(nc.vector.tensor_tensor(b3(dl), b3(drow), tb, ALU.subtract))
            link(nc.vector.tensor_scalar(dl, dl, -1.0, float(P), ALU.max, ALU.min))
            link(nc.vector.tensor_tensor(key[:, :, 1:P + 1], b3(dl), tb, ALU.add))
            nc.vector.tensor_tensor(key[:, :, 1:P + 1], key[:, :, 1:P + 1], tb, ALU.add).then_inc(chunks_ready, 1)
            nc.vector.tensor_scalar(srowf, srow, float(N - 1), None, ALU.min).then_inc(rowsf_ready, 1)

            dve.wait_ge(hist_done, 2 * NH + 3)
            link(nc.vector.tensor_scalar(onorm[:, :], psad[:, 0:NT], 1.0, None, ALU.max))
            dve.wait_ge(x_in, 16 * 8)
            for t in range(NT):
                link(nc.vector.bn_stats(bnst[:, 0:6], xa[:, t, :]))
                link(nc.vector.bn_aggr(stat3[:, t, :], bnst[:, 0:6]))

            def row_scales(n, m):
                nc.vector.tensor_scalar(rstd[:, :], stat3[:, :, 1], EPS, None, ALU.add).then_inc(norm_in, 1)
                dve.wait_ge(norm_sq, n)
                link(nc.vector.reciprocal(rstd[:, :], rstd[:, :]))
                link(nc.vector.tensor_tensor(nbias[:, :], stat3[:, :, 0], rstd[:, :], ALU.mult))
                return nc.vector.tensor_scalar(nbias[:, :], nbias[:, :], -1.0, None, ALU.mult)

            link(row_scales(1, 1))
            nc.vector.tensor_copy(onorm[:, :], onorm[:, :]).then_inc(norm_in, 1)
            dve.wait_ge(norm_sq, 2)
            link(nc.vector.reciprocal(onorm[:, :], onorm[:, :]))
            link(nc.vector.tensor_tensor(rstd[:, :], rstd[:, :], onorm[:, :], ALU.mult))
            nc.vector.tensor_tensor(nbias[:, :], nbias[:, :], onorm[:, :], ALU.mult).then_inc(norm_ready, 1)

            dve.wait_ge(key_edge, 32)
            link(nc.vector.tensor_tensor(b3(sfr), key[:, :, 1:P + 1], key[:, :, 0:P], ALU.not_equal))
            link(nc.vector.tensor_scalar(sfr, sfr, -BIG, None, ALU.mult))
            nc.vector.tensor_tensor(b3(efr), key[:, :, 1:P + 1], key[:, :, 2:P + 2], ALU.not_equal
                                    ).then_inc(rowsf_ready, 1)
            for n in range(2 * SB):
                dve.wait_ge(rowsT_done, n + 1)
                to = sidx if n < SB else dloc
                b = n % SB
                nc.vector.tensor_copy(to[:, b * P:(b + 1) * P], main[n % 4][:, 0:P]).then_inc(rowsT_read, 1)
            for n in range(2 * SB, 3 * SB):
                dve.wait_ge(rowsT_done, n + 1)
                b = n % SB
                nc.vector.tensor_copy(endt[:, b * P:(b + 1) * P], main[n % 4][:, 0:P]).then_inc(rowsT_read, 1)
            link(nc.vector.tensor_scalar(efr, efr, -BIG, None, ALU.mult))
            link(nc.vector.tensor_reduce(sany, b3(sfr), AX.X, ALU.min))
            nc.vector.tensor_reduce(eany, b3(efr), AX.X, ALU.min).then_inc(flags_ready, 1)
            dve.wait_ge(rowsT_read, 3 * SB)
            dve.wait_ge(tiles_in, 16)
            tq = trow[0:1, :].rearrange("p (q k) -> p q k", k=4)
            link(nc.vector.tensor_copy(tsum[0:1, :], tq[:, :, 3]))
            for k in (2, 1, 0):
                link(nc.vector.scalar_tensor_tensor(out=tsum[0:1, :], in0=tsum[0:1, :], scalar=64.0, in1=tq[:, :, k],
                                                    op0=ALU.mult, op1=ALU.add))
            link(nc.vector.tensor_copy(tpk[0:1, :], tsum[0:1, :]))
            dve.wait_ge(flags_out, 64)
            nc.vector.memset(sm4[:, :], 0.0).then_inc(steps_ready, 1)
            dve.wait_ge(steps_ready, 2)
            dve.wait_ge(acc_clear, NT)

            def onehot(col, at):
                return nc.vector.tensor_scalar(oh[:, at * P:(at + 1) * P], iota[:, :], dloc[:, col], None,
                                               ALU.is_equal).then_inc(onehots, 1)

            def accumulate(t, k, width, s):
                dve.wait_ge(products_done, CR + s + 1)
                dve.wait_ge(added, 4 + s)
                a = acc[:, bass.ds(t * AW, width)]
                nc.vector.tensor_tensor(a, a, main[k][:, 0:width], ALU.add).then_inc(added, 1)

            def conv(k):
                dve.wait_ge(table_stored, 16 * NI * (k + 1))
                if k:
                    dve.wait_ge(onehots, oh_base(k))
                    dve.wait_ge(acc_clear, NT * (k + 1))
                for s in range(AHEAD):
                    onehot(slice(s, s + 1), s)
                with nc.vector.Fori(0, S // U) as i:
                    for j in range(U):
                        if j % 4 == 0:
                            pk = dve.value_load(tpk[0:1, bass.ds(i * (U // 4) + j // 4, 1)], min_val=0,
                                                max_val=(1 << 24) - 1)
                        dve.wait_ge(products_done, CR + k * S + i * U + j)
                        onehot(bass.ds(i * U + j + AHEAD, 1), (j + AHEAD) % OHR)
                        t = tile_number((pk >> (6 * (j % 4))) & 63)
                        accumulate(t, j % 4, C + 1, k * S + i * U + j)

            def project(m, epilogue, prepare=None):
                def copy_out(i, j):
                    dve.wait_ge(rows_T, CR + m * NT + i * TB + j + 1)
                    dve.wait_ge(projected, m * NT + i * TB + j + (2 if j == 0 else 1))
                    nc.vector.tensor_copy(aT[:, (j % 2) * C:(j % 2 + 1) * C], pso[j % 2][:, 0:C]
                                          ).then_inc(rows_T_copied, 1)

                with nc.vector.Fori(0, NI) as i:
                    copy_out(i, 0)
                    for j in range(TB):
                        if j < TB - 1:
                            copy_out(i, j + 1)
                        dve.wait_ge(projected, 2 + m * NT + i * TB + j + 1)
                        epilogue(i, j)

            def with_norm_and_bias(to, i, j):
                return nc.vector.scalar_tensor_tensor(out=to, in0=main[j % 2][:, 0:C],
                                                      scalar=inorm[:, bass.ds(i * TB + j, 1)], in1=bias[:, :],
                                                      op0=ALU.mult, op1=ALU.add)

            for k in range(HOPS):
                conv(k)
                dve.wait_ge(added, 4 + (k + 1) * S)
                dve.wait_ge(w_in, 32 * (k + 1))
                if k == 0:
                    link(nc.vector.tensor_scalar(indeg0[:, :], acc3[:, :, ONES_COL], 0.0, None, ALU.is_equal))
                    nc.vector.tensor_scalar(inorm[:, :], acc3[:, :, ONES_COL], 1.0, None, ALU.max).then_inc(norm_in, 1)
                    dve.wait_ge(norm_sq, 3)
                    link(nc.vector.reciprocal(inorm[:, :], inorm[:, :]))
                if k < HOPS - 1:
                    def epilogue(i, j):
                        dve.wait_ge(staged, k * NT + i * TB + j + (2 if j == 0 else 1))
                        with_norm_and_bias(tmp[:, (j % 2) * C:(j % 2 + 1) * C], i, j).then_inc(proj_read, 1)
                    project(k, epilogue)
                else:
                    def epilogue(i, j):
                        if j == 0:
                            dve.wait_ge(rest_in, 16)
                            dve.wait_ge(back_in, i * 16 + 16)
                        t = i * TB + j
                        a = acc[:, bass.ds(t * AW, C)]
                        dve.wait_ge(proj_read, 2 + k * NT + t)
                        with_norm_and_bias(tmp[:, 0:C], i, j).then_inc(proj_read, 1)
                        dve.wait_ge(proj_read, 2 + k * NT + t + 1)
                        nc.vector.tensor_tensor(tmp[:, C:2 * C], tmp[:, 0:C], ring[:, bass.ds(t * C, C)], ALU.add
                                                ).then_inc(dve_chain, 1)
                        dve.wait_ge(dve_chain, chain[0] + 4 * t + 1)
                        dve.nop(nofuse=True)
                        nc.vector.bn_stats(bnst[:, 0:6], tmp[:, C:2 * C]).then_inc(dve_chain, 1)
                        nc.vector.tensor_copy(a, tmp[:, C:2 * C]).then_inc(mid_ready, 1)
                        dve.wait_ge(dve_chain, chain[0] + 4 * t + 2)
                        dve.nop(nofuse=True)
                        nc.vector.bn_aggr(bnst[:, 6:8], bnst[:, 0:6]).then_inc(dve_chain, 1)
                        dve.wait_ge(dve_chain, chain[0] + 4 * t + 3)
                        nc.vector.tensor_copy(stat[:, bass.ds(t * 2, 2)], bnst[:, 6:8]).then_inc(dve_chain, 1)
                        dve.wait_ge(dve_chain, chain[0] + 4 * t + 4)
                        dve.wait_ge(mid_ready, t + 1)
                    project(k, epilogue)
                    chain[0] += 4 * NT
                    row_scales(4, 2).then_inc(norm_ready, 1)

            def logit_columns(l):
                dve.wait_ge(w_in, 32 * HOPS + 64 * l + 48)
                for b in range(2):
                    for a in range(2):
                        link(nc.vector.tensor_tensor(tmp[:, 0:C], wcat[:, b * PW:b * PW + C], att[:, a * C:(a + 1) * C],
                                                     ALU.mult))
                        red = nc.vector.tensor_reduce(wcat[:, b * PW + C + a * H:b * PW + C + (a + 1) * H],
                                                      tmp[:, 0:C].rearrange("p (h c) -> p h c", h=H), AX.X, ALU.add)
                        if a + b < 2:
                            link(red)
                red.then_inc(wcat_ready, 1)
                dve.wait_ge(wcat_ready, l + 1)

            for l in range(LAYERS):
                logit_columns(l)

                def epilogue(i, j):
                    t = i * TB + j
                    if j == 0:
                        dve.wait_ge(table_stored, 16 * NI * (HOPS + l) + i * 16)
                    nc.vector.tensor_copy(stage[:, 0, j, 0:PW], main[j % 2][:, 0:PW]).then_inc(staged, 1)
                    dve.wait_ge(staged, 2 + (HOPS - 1 + l) * NT + t + 1)
                    nc.vector.tensor_copy(tv[:, bass.ds(t * 2 * H, 2 * H)], stage[:, 0, j, C:PW]
                                          ).then_inc(proj_read, 1)
                project(HOPS + l, epilogue)
                dve.wait_ge(proj_read, 2 + (HOPS + l + 1) * NT)
                dve.wait_ge(table_stored, 16 * NI * (HOPS + l + 1))
                dve.wait_ge(acc_clear, NT * (HOPS + l + 1))

                for b in range(2):
                    o = b * H * G
                    link(nc.vector.memset(hg(rsf[0:1, o:o + H * G])[:, :, 0:1], -BIG))
                    link(nc.vector.memset(hg(ref[0:1, o:o + H * G])[:, :, G - 1:G], -BIG))
                link(nc.vector.memset(hg(dw[0:1, :])[:, :, G - 1:G], -BIG))
                link(nc.vector.memset(hg(cw[0:1, :])[:, :, 0:1], 0.0))
                for g in range(G):
                    onehot(slice(g, g + 1), g)

                cb = chain[0]
                per = [0]

                with nc.vector.Fori(0, NG // 2) as it:
                    counts = [0]

                    def step(ins):
                        counts[0] += 1
                        ins.then_inc(dve_chain, 1)
                        dve.wait_ge(dve_chain, it * LINKS + (cb + counts[0]))

                    LINKS = 2 * 24
                    for b in range(2):
                        gg = l * NG + it * 2 + b
                        sl = slot(b)
                        asrc = sl[:, :, C:C + H].rearrange("p g h -> p h g")
                        sf = sfl[:, b * P:(b + 1) * P]
                        ef = efl[:, b * P:(b + 1) * P]
                        o = b * H * G
                        dve.wait_ge(group_in[b], 16 * G * (l * (NG // 2)) + it * 16 * G + 16 * G)
                        dve.wait_ge(ad_ready, gg + 1)
                        nc.vector.tensor_tensor(hg(v[:, :]), asrc, asrc_dst, ALU.max).then_inc(v_ready, 1)
                        step(nc.vector.tensor_tensor(hg(t1[:, :]), asrc, adst_dst, ALU.add))
                        step(nc.vector.scalar_tensor_tensor(out=alpha[:, :], in0=t1[:, :], scalar=SLOPE, in1=t1[:, :],
                                                            op0=ALU.mult, op1=ALU.max))
                        dve.wait_ge(flags_in[b], FLAG_INCS * l * (NG // 2) + it * FLAG_INCS + FLAG_INCS)
                        dve.wait_ge(vT_done, gg + 1)
                        step(nc.vector.tensor_tensor_scan(out=f1[:, :], data0=sf, data1=psb[:, 0:P], initial=-BIG,
                                                          op0=ALU.add, op1=ALU.max))
                        nc.vector.tensor_tensor_scan(out=r1[:, ::-1], data0=ef[:, ::-1], data1=psb[:, 0:P][:, ::-1],
                                                     initial=-BIG, op0=ALU.add, op1=ALU.max).then_inc(scan_ready, 1)
                        cf = sm4[0:1, 4 * H:4 * H + 1]
                        step(nc.vector.tensor_scalar(cf, sf[0:1, 0:1], 0.0, None, ALU.is_equal))
                        dve.wait_ge(ends_done, gg + 1)
                        step(nc.vector.tensor_copy(hg(cw[0:1, :])[:, :, 1:G],
                                                   hg(psb[0:1, 2 * P:3 * P])[:, :, 0:G - 1]))
                        step(nc.vector.tensor_copy(hg(dw[0:1, :])[:, :, 0:G - 1],
                                                   hg(psb[0:1, 3 * P:4 * P])[:, :, 1:G]))
                        step(nc.vector.tensor_tensor_scan(out=co[0:1, :], data0=rsf[0:1, o:o + H * G],
                                                          data1=cw[0:1, :], initial=-BIG, op0=ALU.add, op1=ALU.max))
                        step(nc.vector.scalar_tensor_tensor(
                            out=nxt[0:1, :].rearrange("p (h o) -> p h o", o=1), in0=hg(co[0:1, :])[:, :, G - 1:G],
                            scalar=rlast[0:1, b:b + 1], in1=hg(psb[0:1, 2 * P:3 * P])[:, :, G - 1:G],
                            op0=ALU.add, op1=ALU.max))
                        nc.vector.tensor_tensor_scan(out=do[0:1, ::-1], data0=ref[0:1, o:o + H * G][:, ::-1],
                                                     data1=dw[0:1, ::-1], initial=-BIG, op0=ALU.add,
                                                     op1=ALU.max).then_inc(carry_ready, 1)
                        dve.wait_ge(carry_done, gg + 1)
                        step(nc.vector.tensor_copy(cin[:, :], psb[:, 2 * P:2 * P + 2]))
                        step(nc.vector.tensor_tensor_scan(out=f2[:, :], data0=sf, data1=psb[:, 0:P],
                                                          initial=cin[:, 0:1], op0=ALU.add, op1=ALU.max))
                        step(nc.vector.tensor_tensor_scan(out=r2[:, ::-1], data0=ef[:, ::-1],
                                                          data1=psb[:, 0:P][:, ::-1], initial=cin[:, 1:2],
                                                          op0=ALU.add, op1=ALU.max))
                        nc.vector.tensor_tensor(mrow[:, :], f2[:, :], r2[:, :], ALU.max).then_inc(max_ready, 1)
                        dve.wait_ge(maxT_done, gg + 1)
                        step(nc.vector.tensor_tensor(hg(t1[:, :]), hg(psb[:, P:2 * P]), adst_dst, ALU.add))
                        step(nc.vector.scalar_tensor_tensor(out=mx[:, :], in0=t1[:, :], scalar=SLOPE, in1=t1[:, :],
                                                            op0=ALU.mult, op1=ALU.max))
                        step(nc.vector.tensor_tensor(dd[:, 0:P], alpha[:, :], mx[:, :], ALU.subtract))
                        step(nc.vector.tensor_tensor(hg(t2[:, :]), asrc_dst, adst_dst, ALU.add))
                        step(nc.vector.scalar_tensor_tensor(out=t1[:, :], in0=t2[:, :], scalar=SLOPE, in1=t2[:, :],
                                                            op0=ALU.mult, op1=ALU.max))
                        step(nc.vector.tensor_tensor(dd[:, P:2 * P], t1[:, :], mx[:, :], ALU.subtract))
                        old, new = sm4[0:1, 0:H], sm4[0:1, H:2 * H]
                        step(nc.vector.tensor_tensor(old.rearrange("p (h o) -> p h o", o=1), hg(cw[0:1, :])[:, :, 0:1],
                                                     adst_dst[0:1, :, 0:1], ALU.add))
                        step(nc.vector.scalar_tensor_tensor(out=new, in0=old, scalar=SLOPE, in1=old,
                                                            op0=ALU.mult, op1=ALU.max))
                        step(nc.vector.tensor_tensor(old.rearrange("p (h o) -> p h o", o=1),
                                                     new.rearrange("p (h o) -> p h o", o=1),
                                                     hg(mx[0:1, :])[:, :, 0:1], ALU.subtract))
                        nc.vector.tensor_scalar(lf[0:1, :], old, cf, None, ALU.mult).then_inc(expo_ready, 1)
                        dve.wait_ge(expo_ready, gg + 1)
                        step(nc.vector.tensor_copy(hg(cw[0:1, :])[:, :, 0:1],
                                                   nxt[0:1, :].rearrange("p (h o) -> p h o", o=1)))
                        dve.wait_ge(e_ready, l * NG * 2 + it * 4 + (b + 1) * 2)
                        step(nc.vector.tensor_tensor(
                            sl[:, :, C + H:C + 2 * H].rearrange("p g h -> p h g"), hg(eself[:, :]),
                            endt[:, bass.ds(it * 2 * G + b * G, G)].rearrange("p (o g) -> p o g", o=1)
                            .to_broadcast([P, H, G]), ALU.mult))
                        dve.wait_ge(factor_ready, gg + 1)
                        dve.wait_ge(added, 4 + (HOPS + l) * S + it * 2 * G + b * G)
                        pk = dve.value_load(tpk[0:1, bass.ds(it * 2 * (G // 4) + b * (G // 4), 1)], min_val=0,
                                            max_val=(1 << 24) - 1)
                        t = tile_number(pk & 63)
                        a4 = acc[:, bass.ds(t * AW, C)].rearrange("p (h c) -> p h c", h=H)
                        f4 = resc[:, :].rearrange("p (h o) -> p h o", o=1).to_broadcast([P, H, CH])
                        step(nc.vector.tensor_tensor(a4, a4, f4, ALU.mult))
                        aw = acc[:, bass.ds(t * AW + C, H)]
                        step(nc.vector.tensor_tensor(aw, aw, resc[:, :], ALU.mult))

                        def add(k, t):
                            accumulate(t, k % 4, AW, (HOPS + l) * S + it * 2 * G + b * G + k)

                        held = []
                        for q in range(G // 4):
                            for k in range(4 * q, 4 * q + 4):
                                onehot(bass.ds(it * 2 * G + (b + 1) * G + k, 1), (1 - b) * G + k)
                            pk = dve.value_load(tpk[0:1, bass.ds(it * 2 * (G // 4) + (b * (G // 4) + q), 1)], min_val=0,
                                                max_val=(1 << 24) - 1)
                            for k in range(4 * q, 4 * q + 4):
                                r = ring3[:, b * G + k, 0:DVEC].rearrange("p (h c) -> p h c", c=CH)
                                w = ring3[:, b * G + k, C:C + DVEC // CH].rearrange("p (h o) -> p h o", o=1)
                                nc.vector.tensor_tensor(r, r, w.to_broadcast([P, DVEC // CH, CH]), ALU.mult
                                                        ).then_inc(weighted_v, 1)
                                held.append((k, tile_number((pk >> (6 * (k % 4))) & 63)))
                                if len(held) > 2:
                                    add(*held.pop(0))
                        while held:
                            add(*held.pop(0))
                    per[0] = counts[0]
                assert per[0] == LINKS, per[0]
                chain[0] += LINKS * (NG // 2)

                dve.wait_ge(added, 4 + (HOPS + l + 1) * S)
                link(nc.vector.tensor_tensor(es3, acc3[:, :, C + H:AW],
                                             indeg0[:, :].rearrange("p (t o) -> p t o", o=1).to_broadcast([P, NT, H]),
                                             ALU.add))
                link(nc.vector.tensor_tensor(rs3, es3, acc3[:, :, C:C + H], ALU.add))
                link(nc.vector.tensor_scalar(rs[:, :], rs[:, :], 1e-16, None, ALU.max))
                nc.vector.reciprocal(rs[:, :], rs[:, :]).then_inc(nself, 1)
                dve.wait_ge(nself, l + 1)
                dve.wait_ge(w_in, 32 * HOPS + 64 * (l + 1))
                cb2 = chain[0]
                with nc.vector.Fori(0, NT) as i:
                    dve.wait_ge(self_ready, l * NT + i + 1)
                    a = acc[:, bass.ds(i * AW, C)]
                    a4 = a.rearrange("p (h c) -> p h c", h=H)
                    nc.vector.tensor_tensor(a, a, ring[:, bass.ds(i * C, C)], ALU.add).then_inc(dve_chain, 1)
                    dve.wait_ge(dve_chain, cb2 + 2 * i + 1)
                    nc.vector.tensor_tensor(a4, a4, rs[:, bass.ds(i * H, H)].rearrange("p (h o) -> p h o", o=1)
                                            .to_broadcast([P, H, CH]), ALU.mult).then_inc(dve_chain, 1)
                    dve.wait_ge(dve_chain, cb2 + 2 * i + 2)
                    nc.vector.tensor_tensor(a, a, bias[:, :], ALU.add).then_inc(mid_ready, 1)
                chain[0] += 2 * NT
            dve.wait_ge(mid_ready, 3 * NT)
            with nc.vector.Fori(0, NI) as i:
                dve.wait_ge(back_in, 16 * (3 * NI) + i * 16 + 16)
                for j in range(TB):
                    a = acc[:, bass.ds((i * TB + j) * AW, C)]
                    nc.vector.tensor_tensor(a, a, ring[:, bass.ds((i * TB + j) * C, C)], ALU.add).then_inc(mid_ready, 1)


_INS = ['x', 'src', 'dst', 'L0_gnn_W', 'L0_gnn_b', 'L1_gnn_W1', 'L1_gnn_att_src1', 'L1_gnn_att_dst1', 'L1_gnn_b1',
        'L1_gnn_W2', 'L1_gnn_att_src2', 'L1_gnn_att_dst2', 'L1_gnn_b2']


def kernel(**inputs):
    import numpy as _np
    import concourse.bacc as _bacc
    from concourse import mybir as _mybir
    from concourse.bass_utils import run_bass_kernel_spmd as _run

    nc = _bacc.Bacc("TRN2", target_bir_lowering=False, num_devices=1)
    arrays, args = {}, []
    for name in _INS:
        a = _np.ascontiguousarray(inputs[name])
        arrays[f"in_{name}_dram"] = a
        args.append(nc.dram_tensor(f"in_{name}_dram", a.shape, _mybir.dt.from_np(a.dtype), kind="ExternalInput").ap())
    args.append(nc.dram_tensor("out_0_dram", (N, C), _mybir.dt.float32, kind="ExternalOutput").ap())
    gnn(nc, *args)
    r = _run(nc, [arrays], core_ids=[0])
    return r.results[0]["out_0_dram"]
```

```python
import concourse.bass as bass
from concourse import mybir
from contextlib import ExitStack

F32 = mybir.dt.float32
BF16 = mybir.dt.bfloat16
I32 = mybir.dt.int32
ALU = mybir.AluOpType
ACT = mybir.ActivationFunctionType
AX = mybir.AxisListType

P = 128
N = 6250
E = 100000
C = 256
H = 4
CH = C // H
HOPS = 3
LAYERS = 2
NT = -(-N // P)
NFULL = N // P
NREST = N - NFULL * P
EC = -(-E // P)
EPAD = EC * P - E
G = 16
GB = 4
NG = -(-(EC + NT - 1) // G)
NG += -NG % GB
S = NG * G
Q = G // 4
SB = -(-(S + 2 * G + 4) // P)
SX = SB * P
OUTSIDE = 50 * P
BIG = 1e30
EPS = 1e-5
SLOPE = 0.2
AW = C + 2 * H
TW = C + H
PW = C + 2 * H
RING = GB * G
U = 32
UH = U // 2
AHEAD = 3
OHR = 4
TB = 7
NI = NT // TB
HB = 17
NH = EC // (2 * HB)
DVEC = 3 * CH
CR = U
assert EC % (2 * HB) == 0 and NT % TB == 0 and S % U == 0 and  S >= EC + NT - 1


def gnn(nc, x, src, dst, gw, gb, w1, as1, ad1, b1, w2, as2, ad2, b2, out):
    ctx = ExitStack()
    with ctx:
        def sb(name, shape, dt=F32):
            return ctx.enter_context(nc.sbuf_tensor(name, shape, dt))

        def sem(name):
            return ctx.enter_context(nc.semaphore(name))

        def dram(name, shape, dt=F32):
            return nc.dram_tensor(name, shape, dt, kind="Internal").ap()

        src_pad = dram("src_pad", (EC, P), I32)
        dst_pad = dram("dst_pad", (EC, P), I32)
        keys = dram("keys", (1, SX * P + 2))
        start_rows = dram("start_rows", (SX, P))
        end_rows = dram("end_rows", (SX, P))
        start_any = dram("start_any", (1, SX))
        end_any = dram("end_any", (1, SX))
        tile_of = dram("tile_of", (1, SX))
        conv_tab = [dram(f"conv_tab{k}", (NT * P, C)) for k in range(HOPS)]
        attn_tab = [dram(f"attn_tab{k}", (NT * P, TW)) for k in range(LAYERS)]
        x1_tab = dram("x1_tab", (NT * P, C))

        ring = sb("ring", [P, RING * AW])
        acc = sb("acc", [P, NT * AW])
        oh = sb("oh", [P, RING * P])
        dloc = sb("dloc", [P, SX])
        sidx = sb("sidx", [P, SX], I32)
        endt = sb("endt", [P, SX])
        tpk = sb("tpk", [1, SX // 4], I32)
        iota = sb("iota", [P, P])
        ident = sb("ident", [P, P])
        ones = sb("ones", [P, P])
        zrow = sb("zrow", [P, AW])
        onorm = sb("onorm", [P, NT])
        inorm = sb("inorm", [P, NT])
        indeg0 = sb("indeg0", [P, NT])
        stat = sb("stat", [P, NT * 2])
        bnst = sb("bnst", [P, 2 * 6])
        rstd = sb("rstd", [P, NT])
        nbias = sb("nbias", [P, NT])
        wc = sb("wc", [P, 2 * C])
        wcat = sb("wcat", [P, 2 * PW])
        bias = sb("bias", [P, C])
        att = sb("att", [P, 2 * C])
        nb = sb("nb", [P, 2 * C])
        aT = sb("aT", [P, 2 * C])
        tmp = sb("tmp", [P, 2 * C])
        tv = sb("tv", [P, NT * 2 * H])
        ohT = sb("ohT", [P, 2 * 4 * P])
        idx = sb("idx", [P, GB * G], I32)
        ad = sb("ad", [P, 2 * G * 2 * H])
        sfl = sb("sfl", [H * G, GB * P])
        efl = sb("efl", [H * G, GB * P])
        rsf = sb("rsf", [1, GB * H * G])
        ref = sb("ref", [1, GB * H * G])
        v = sb("v", [P, H * G])
        f1 = sb("f1", [H * G, P])
        r1 = sb("r1", [H * G, P])
        f2 = sb("f2", [H * G, P])
        r2 = sb("r2", [H * G, P])
        mrow = sb("mrow", [H * G, P])
        alpha = sb("alpha", [P, H * G])
        mx = sb("mx", [P, H * G])
        t1 = sb("t1", [P, H * G])
        t2 = sb("t2", [P, H * G])
        dd = sb("dd", [P, 2 * H * G])
        lself = sb("lself", [P, H * G])
        eself = sb("eself", [P, H * G])
        cin = sb("cin", [H * G, 2])
        cw = sb("cw", [1, H * G])
        dw = sb("dw", [1, H * G])
        co = sb("co", [1, H * G])
        do = sb("do", [1, H * G])
        rlast = sb("rlast", [1, GB])
        nxt = sb("nxt", [1, H])
        sm4 = sb("sm4", [1, 4 * H + 1])
        lf = sb("lf", [1, H])
        resc = sb("resc", [P, H])
        es = sb("es", [P, NT * H])
        rs = sb("rs", [P, NT * H])

        main = [ctx.enter_context(nc.psum_tensor(f"main{i}", [P, 512], F32)) for i in range(4)]
        pso = [ctx.enter_context(nc.psum_tensor(f"pso{i}", [P, 512], F32)) for i in range(2)]
        psad = ctx.enter_context(nc.psum_tensor("psad", [P, 512], F32))
        psb = ctx.enter_context(nc.psum_tensor("psb", [P, 512], F32))

        ring3 = ring[:, :].rearrange("p (s w) -> p s w", w=AW)
        acc3 = acc[:, :].rearrange("p (t w) -> p t w", w=AW)
        xr = ring[:, 0:NT * C].rearrange("p (t c) -> p t c", c=C)
        xa = acc[:, 0:NT * C].rearrange("p (t c) -> p t c", c=C)
        stage = oh[:, 0:2 * TB * AW].rearrange("p (b t w) -> p b t w", b=2, w=AW)
        stat3 = stat[:, :].rearrange("p (t k) -> p t k", k=2)
        tv3 = tv[:, :].rearrange("p (t k) -> p t k", k=2 * H)
        es3 = es[:, :].rearrange("p (t h) -> p t h", h=H)
        rs3 = rs[:, :].rearrange("p (t h) -> p t h", h=H)
        ad3 = ad[:, :].rearrange("p (b g k) -> p b g k", b=2, k=2 * H)

        def hg(ap):
            return ap.rearrange("p (h g) -> p h g", h=H)

        def logits_of(b):
            return (ad3[:, b % 2, :, 0:H].rearrange("p g h -> p h g"), ad3[:, b % 2, :, H:2 * H].rearrange("p g h -> p h g"))

        def slot(b):
            return ring3[:, b * G:(b + 1) * G, :]

        lin = ring[:, 0:EC].bitcast(I32)
        lo_i = ring[:, EC:2 * EC].bitcast(I32)
        hi_i = ring[:, 2 * EC:3 * EC].bitcast(I32)
        lo_b = ring[:, 3 * EC:3 * EC + EC // 2].bitcast(BF16)
        hi_b = ring[:, 3 * EC + EC // 2:4 * EC].bitcast(BF16)
        dlin = ring[:, 4 * EC:5 * EC].bitcast(I32)
        dlin_f = ring[:, 5 * EC:6 * EC]
        sgn = ring[:, 6 * EC:7 * EC]
        o_lo, o_hi = 7 * EC, 7 * EC + HB * P
        oh_lo = ring[:, o_lo:o_hi].bitcast(BF16).rearrange("p (b k n) -> p b k n", b=2, n=P)
        oh_hi = ring[:, o_hi:o_hi + HB * NT].bitcast(BF16).rearrange("p (b k n) -> p b k n", b=2, n=NT)
        o_c = o_hi + HB * NT
        iota_b = ring[:, o_c:o_c + P // 2].bitcast(BF16)
        zero_b = ring[:, o_c + P // 2:o_c + P].bitcast(BF16)
        o_c += P
        thr = ring[:, o_c:o_c + NT]
        cnt = ring[:, o_c + NT:o_c + 2 * NT]
        bf = ring[:, o_c + 2 * NT:o_c + 3 * NT]
        bi = ring[:, o_c + 3 * NT:o_c + 4 * NT].bitcast(I32)
        fl = ring[:, o_c + 4 * NT:o_c + 5 * NT].bitcast(I32)
        ce = ring[:, o_c + 5 * NT:o_c + 6 * NT].bitcast(I32)
        ov = ring[:, o_c + 6 * NT:o_c + 7 * NT]
        pre = ring[:, o_c + 7 * NT:o_c + 8 * NT]
        cum = ring[:, o_c + 8 * NT:o_c + 9 * NT]
        zt = ring[:, o_c + 9 * NT:o_c + 10 * NT]
        o_c += 10 * NT
        sid = ring[:, o_c:o_c + SB]
        ts = ring[:, o_c + SB:o_c + 2 * SB]
        cs = ring[:, o_c + 2 * SB:o_c + 3 * SB]
        ci = ring[:, o_c + 3 * SB:o_c + 4 * SB].bitcast(I32)
        tsc = ring[:, o_c + 4 * SB:o_c + 5 * SB]
        t128 = ring[:, o_c + 5 * SB:o_c + 6 * SB]
        sany = ring[:, o_c + 6 * SB:o_c + 7 * SB]
        eany = ring[:, o_c + 7 * SB:o_c + 8 * SB]
        padi = ring[0:1, o_c + 8 * SB:o_c + 8 * SB + P].bitcast(I32)
        strayf = ring[0:1, o_c + 8 * SB + P:o_c + 8 * SB + P + 2]
        o_c += 8 * SB + P + 2
        assert o_c <= RING * AW
        srow = oh[:, 0:SX].bitcast(I32)
        drow = oh[:, SX:2 * SX].bitcast(I32)
        key = oh[:, 2 * SX:2 * SX + SB * (P + 2)].rearrange("p (b e) -> p b e", e=P + 2)
        o_k = 2 * SX + SB * (P + 2)
        srowf = oh[:, o_k:o_k + SX]
        dl = oh[:, o_k + SX:o_k + 2 * SX]
        sfr = oh[:, o_k + 2 * SX:o_k + 3 * SX]
        assert o_k + 3 * SX <= RING * P
        efr = ohT[:, 0:SX]
        cmpt = dloc[:, 0:SB * NT].rearrange("p (b t) -> p b t", t=NT)
        cmpo = endt[:, 0:SB * NT].rearrange("p (b t) -> p b t", t=NT)
        trow = sb("trow", [1, SX])
        tsum = sb("tsum", [1, SX // 4])

        def b3(ap):
            return ap.rearrange("p (b e) -> p b e", e=P)

        def bc(ap, shape):
            return ap.to_broadcast(shape)

        edges_in = sem("edges_in")
        pads_set = sem("pads_set")
        pads_out = sem("pads_out")
        lin_in = sem("lin_in")
        x_in = sem("x_in")
        consts = sem("consts")
        pool_chain = sem("pool_chain")
        dve_chain = sem("dve_chain")
        act_chain = sem("act_chain")
        hist_onehots = sem("hist_onehots")
        hist_done = sem("hist_done")
        dlin_ready = sem("dlin_ready")
        counts_ready = sem("counts_ready")
        counts_sum = sem("counts_sum")
        chunks_ready = sem("chunks_ready")
        rows_in = sem("rows_in")
        rowsf_ready = sem("rowsf_ready")
        rowsT_done = sem("rowsT_done")
        rowsT_read = sem("rowsT_read")
        key_out = sem("key_out")
        key_edge = sem("key_edge")
        flags_ready = sem("flags_ready")
        flags_out = sem("flags_out")
        tiles_out = sem("tiles_out")
        tiles_in = sem("tiles_in")
        steps_ready = sem("steps_ready")
        norm_in = sem("norm_in")
        norm_sq = sem("norm_sq")
        norm_ready = sem("norm_ready")
        ln_rows = sem("ln_rows")
        acc_clear = sem("acc_clear")
        table_stored = sem("table_stored")
        gathered = [sem(f"gathered{j}") for j in range(U)]
        idx_in = [sem(f"idx_in{j}") for j in range(GB)]
        group_in = [sem(f"group_in{j}") for j in range(GB)]
        onehots = sem("onehots")
        quads_ready = sem("quads_ready")
        squares_ready = sem("squares_ready")
        products_done = sem("products_done")
        added = sem("added")
        w_in = sem("w_in")
        wcat_ready = sem("wcat_ready")
        nb_ready = sem("nb_ready")
        rows_T = sem("rows_T")
        rows_T_copied = sem("rows_T_copied")
        projected = sem("projected")
        proj_read = sem("proj_read")
        staged = sem("staged")
        mid_ready = sem("mid_ready")
        back_in = sem("back_in")
        rest_in = sem("rest_in")
        stored = sem("stored")
        ohT_done = sem("ohT_done")
        ohT_copied = sem("ohT_copied")
        logits_done = sem("logits_done")
        ad_ready = sem("ad_ready")
        flags_in = [sem(f"flags_in{j}") for j in range(GB)]
        v_ready = sem("v_ready")
        vT_done = sem("vT_done")
        scan_ready = sem("scan_ready")
        ends_done = sem("ends_done")
        carry_ready = sem("carry_ready")
        carry_done = sem("carry_done")
        max_ready = sem("max_ready")
        maxT_done = sem("maxT_done")
        expo_ready = sem("expo_ready")
        lf_done = sem("lf_done")
        e_ready = sem("e_ready")
        factor_ready = sem("factor_ready")
        weighted_v = sem("weighted_v")
        weighted_a = sem("weighted_a")
        self_ready = sem("self_ready")
        nself = sem("nself")

        def tile_number(value):
            return nc.s_assert_within(value, 0, NT - 1, skip_runtime_bounds_check_because="clamped on the chip before it is packed")

        ONES_COL = C
        FLAG_INCS = 16 * (2 * H + 3)
        LEAD = 3
        MARKS = GB * 24
        HALF = 2 * P

        def oh_base(k):
            return k * (S + AHEAD)

        QL = (NG + 2) * Q + 1

        def rows_of(tab, i, width):
            return tab.rearrange("(t p) c -> p t c", p=P)[:, bass.ds(i * TB, TB), 0:width]

        block = ctx.enter_context(nc.Block())

        @block.sync
        def _(sp):
            sp.dma_start(src_pad.rearrange("a b -> (a b)")[0:E].rearrange("(k f) -> k f", k=16),
                         src.rearrange("(k f) -> k f", k=16)).then_inc(edges_in, 16)
            sp.dma_start(dst_pad.rearrange("a b -> (a b)")[0:E].rearrange("(k f) -> k f", k=16),
                         dst.rearrange("(k f) -> k f", k=16)).then_inc(edges_in, 16)
            for q in range(7):
                sp.dma_start(xa[:, q * TB:min((q + 1) * TB, NFULL), :],
                             x[q * TB * P:min((q + 1) * TB, NFULL) * P, :].rearrange("(t p) c -> p t c", p=P)
                             ).then_inc(x_in, 16)
            sp.wait_ge(pads_set, 2)
            sp.dma_start(xa[0:NREST, NFULL, :], x[NFULL * P:N, :]).then_inc(x_in, 16)
            sp.dma_start(src_pad[EC - 1:EC, P - EPAD:P], padi[0:1, 0:EPAD]).then_inc(pads_out, 16)
            sp.dma_start(dst_pad[EC - 1:EC, P - EPAD:P], padi[0:1, 0:EPAD]).then_inc(pads_out, 16)
            sp.dma_start(keys[0:1, 0:1], strayf[0:1, 0:1]).then_inc(pads_out, 16)
            sp.dma_start(keys[0:1, SX * P + 1:SX * P + 2], strayf[0:1, 1:2]).then_inc(pads_out, 16)
            sp.wait_ge(edges_in, 32)
            sp.wait_ge(pads_out, 64)
            sp.dma_start(lin, src_pad.rearrange("a b -> (a b)").rearrange("(p f) -> p f", p=P)).then_inc(lin_in, 16)
            sp.wait_ge(lin_in, 16)
            sp.dma_start(dlin, dst_pad.rearrange("a b -> (a b)").rearrange("(p f) -> p f", p=P)).then_inc(lin_in, 16)

            sp.wait_ge(chunks_ready, 2)
            sp.dma_start(keys[0:1, 1:1 + SX * P].rearrange("o (b p e) -> (o p) b e", p=P, e=P),
                         key[:, :, 1:P + 1]).then_inc(key_out, 16)
            with nc.allow_non_contiguous_dma(reason="one element of each step"):
                sp.dma_start(tile_of.rearrange("o (b p) -> (o p) b", p=P), tsc).then_inc(tiles_out, 16)
                sp.wait_ge(key_out, 16)
                kv = keys[0:1, 0:SX * P].rearrange("o (b p e) -> (o p) b e", p=P, e=P)
                sp.dma_start(key[:, :, 0:1], kv[:, :, 0:1]).then_inc(key_edge, 16)
                kn = keys[0:1, 2:SX * P + 2].rearrange("o (b p e) -> (o p) b e", p=P, e=P)
                sp.dma_start(key[:, :, P + 1:P + 2], kn[:, :, P - 1:P]).then_inc(key_edge, 16)
                sp.wait_ge(tiles_out, 16)
                sp.dma_start(trow[0:1, :], tile_of).then_inc(tiles_in, 16)
                sp.wait_ge(flags_ready, 1)
                sp.dma_start(start_rows.rearrange("(b p) e -> p b e", p=P), b3(sfr)).then_inc(flags_out, 16)
                sp.dma_start(end_rows.rearrange("(b p) e -> p b e", p=P), b3(efr)).then_inc(flags_out, 16)
                sp.dma_start(start_any.rearrange("o (b p) -> (o p) b", p=P), sany).then_inc(flags_out, 16)
                sp.dma_start(end_any.rearrange("o (b p) -> (o p) b", p=P), eany).then_inc(flags_out, 16)

            for q in range(NI):
                sp.wait_ge(ln_rows, TB * (q + 1))
                sp.dma_start(conv_tab[0].rearrange("(t p) c -> p t c", p=P)[:, q * TB:(q + 1) * TB, :],
                             xa[:, q * TB:(q + 1) * TB, :]).then_inc(table_stored, 16)

            def store_stage(table, width, m):
                with nc.sync.Fori(0, NI) as i:
                    sp.wait_ge(staged, 2 + m * NT + i * TB + TB)
                    sp.dma_start(rows_of(table, i, width), stage[:, 0, :, 0:width]).then_inc(table_stored, 16)

            def fetch_idx(b, col, width):
                sp.dma_start(idx[:, b * G:b * G + width], sidx[:, bass.ds(col, width)]).then_inc(idx_in[b], 16)

            for k in range(HOPS):
                if k:
                    sp.wait_ge(staged, 2 + k * NT)
                sp.dma_start(wc[:, :].rearrange("p (b n) -> p b n", b=2),
                             gw[k].rearrange("(b p) n -> p b n", p=P)).then_inc(w_in, 16)
                sp.dma_start(bias[:, :], gb[k:k + 1, :].to_broadcast([P, C])).then_inc(w_in, 16)
                if k == 0:
                    sp.wait_ge(steps_ready, 1)
                with nc.sync.Fori(0, S // U) as i:
                    for b in range(2):
                        sp.wait_ge(products_done, k * S + i * U + (b + 1) * UH)
                        fetch_idx(b, i * U + b * UH, UH)
                if k < HOPS - 1:
                    store_stage(conv_tab[k + 1], C, k)
                else:
                    sp.wait_ge(added, 4 + HOPS * S)
                    for q in range(NI):
                        a, b = q * TB, min((q + 1) * TB, NFULL)
                        sp.dma_start(xr[:, a:b, :], x[a * P:b * P, :].rearrange("(t p) c -> p t c", p=P)
                                     ).then_inc(back_in, 16)
                        if q == 0:
                            sp.dma_start(xr[0:NREST, NFULL, :], x[NFULL * P:N, :]).then_inc(rest_in, 16)
                        sp.wait_ge(back_in, 16 * (q + 1))
                    with nc.sync.Fori(0, NI) as i:
                        sp.wait_ge(mid_ready, i * TB + TB)
                        sp.dma_start(rows_of(x1_tab, i, C), acc3[:, bass.ds(i * TB, TB), 0:C]).then_inc(stored, 16)

            for l in range(LAYERS):
                w, s_, d_ = ((w1, as1, ad1), (w2, as2, ad2))[l]
                if l:
                    sp.wait_ge(projected, 2 + (HOPS + l) * NT)
                sp.dma_start(wcat[:, :].rearrange("p (b n) -> p b n", b=2)[:, :, 0:C],
                             w.rearrange("(b p) n -> p b n", p=P)).then_inc(w_in, 16)
                sp.dma_start(att[:, 0:C], s_.rearrange("o h c -> o (h c)").to_broadcast([P, C])).then_inc(w_in, 16)
                sp.dma_start(att[:, C:2 * C], d_.rearrange("o h c -> o (h c)").to_broadcast([P, C])).then_inc(w_in, 16)
                store_stage(attn_tab[l], TW, HOPS - 1 + l)
                sp.wait_ge(mid_ready, (l + 1) * NT)
                sp.dma_start(bias[:, :], (b1, b2)[l].rearrange("(o c) -> o c", o=1).to_broadcast([P, C])).then_inc(w_in, 16)
                if l == 0:
                    sp.wait_ge(flags_out, 64)
                def fetch_group(it, b, last=False):
                    sp.wait_ge(expo_ready, it * GB + (l * (NG + 1) + b + 1))
                    g0 = (it * GB + b) * G
                    if not last:
                        fetch_idx(b, g0, G)
                    for h in range(H):
                        sp.dma_start(sfl[h * G:(h + 1) * G, b * P:(b + 1) * P],
                                     start_rows[bass.ds(g0, G), :]).then_inc(flags_in[b], 16)
                        sp.dma_start(efl[h * G:(h + 1) * G, b * P:(b + 1) * P],
                                     end_rows[bass.ds(g0, G), :]).then_inc(flags_in[b], 16)
                    o = b * H * G
                    for to, of, at in ((hg(rsf[0:1, o:o + H * G])[:, :, 1:G], start_any, g0),
                                       (hg(ref[0:1, o:o + H * G])[:, :, 0:G - 1], end_any, g0 + 1)):
                        sp.dma_start(to, of[0:1, bass.ds(at, G - 1)].rearrange("o (h g) -> o h g", h=1)
                                     .to_broadcast([1, H, G - 1])).then_inc(flags_in[b], 16)
                    sp.dma_start(rlast[0:1, b:b + 1], start_any[0:1, bass.ds(g0 + G - 1, 1)]).then_inc(flags_in[b], 16)

                with nc.sync.Fori(0, NG // GB) as it:
                    for b in range(GB):
                        fetch_group(it, b)
                fetch_group(NG // GB, 0, last=True)
                sp.wait_ge(added, 4 + (HOPS + l + 1) * S)
                sp.wait_ge(e_ready, 2 * (l + 1) * (NG + 1))
                sp.wait_ge(weighted_v, (l + 1) * (S + LEAD))
                for q in range(NI):
                    sp.dma_start(xr[:, q * TB:(q + 1) * TB, :],
                                 attn_tab[l].rearrange("(t p) c -> p t c", p=P)[:, q * TB:(q + 1) * TB, 0:C]
                                 ).then_inc(back_in, 16)
                    sp.wait_ge(back_in, 16 * (NI + l * NI + q + 1))
            for q in range(NI):
                sp.wait_ge(mid_ready, 2 * NT + TB * (q + 1))
                sp.dma_start(xr[:, q * TB:(q + 1) * TB, :],
                             x1_tab.rearrange("(t p) c -> p t c", p=P)[:, q * TB:(q + 1) * TB, :]
                             ).then_inc(back_in, 16)
                sp.wait_ge(back_in, 16 * (3 * NI + q + 1))
            for q in range(NI):
                a, b = q * TB, min((q + 1) * TB, NFULL)
                sp.wait_ge(mid_ready, 3 * NT + TB * (q + 1))
                sp.dma_start(out[a * P:b * P, :].rearrange("(t p) c -> p t c", p=P), acc3[:, a:b, 0:C]
                             ).then_inc(stored, 16)
            sp.dma_start(out[NFULL * P:N, :], acc3[0:NREST, NFULL, 0:C]).then_inc(stored, 16)
            sp.wait_ge(stored, 16 * (2 * NI + 1))
            sp.wait_ge(table_stored, 16 * NI * (HOPS + LAYERS))

        @block.gpsimd
        def _(pool):
            chain = [0]

            def link(ins):
                chain[0] += 1
                ins.then_inc(pool_chain, 1)
                pool.wait_ge(pool_chain, chain[0])

            nc.gpsimd.memset(padi, OUTSIDE).then_inc(pads_set, 1)
            link(nc.gpsimd.memset(strayf, -5.0))
            nc.gpsimd.memset(xa[:, NFULL, :], 0.0).then_inc(pads_set, 1)
            link(nc.gpsimd.memset(ident[:, :], 0.0))
            link(nc.gpsimd.affine_select(out=ident[:, :], in_=ident[:, :], compare_op=ALU.not_equal, fill=1.0,
                                         base=0, pattern=[[-1, P]], channel_multiplier=1))
            link(nc.gpsimd.memset(ones[:, :], 1.0))
            link(nc.gpsimd.memset(zt, 0.0))
            link(nc.gpsimd.memset(zrow[:, :], 0.0))
            link(nc.gpsimd.iota(iota[:, :], pattern=[[1, P]], base=0, channel_multiplier=0,
                                allow_small_or_imprecise_dtypes=True))
            link(nc.gpsimd.iota(iota_b, pattern=[[1, P]], base=0, channel_multiplier=0,
                                allow_small_or_imprecise_dtypes=True))
            link(nc.gpsimd.iota(thr, pattern=[[P, NT]], base=P, channel_multiplier=0,
                                allow_small_or_imprecise_dtypes=True))
            link(nc.gpsimd.iota(sid, pattern=[[P, SB]], base=0, channel_multiplier=1,
                                allow_small_or_imprecise_dtypes=True))
            nc.gpsimd.memset(zero_b, 0.0).then_inc(consts, 1)

            pool.wait_ge(chunks_ready, 1)
            pool.wait_ge(lin_in, 32)
            for b in range(SB):
                for row, tab in ((srow, src_pad), (drow, dst_pad)):
                    pool.indirect_dma_start(b3(row)[:, b, :], None, tab,
                                            bass.IndirectOffsetOnAxis(ap=ci[:, b:b + 1], axis=0)
                                            ).then_inc(rows_in, 16)

            def clear_first():
                pool.wait_ge(table_stored, 16 * NI)
                with nc.gpsimd.Fori(0, NT) as i:
                    pool.nop(nofuse=True)
                    nc.gpsimd.tensor_copy(acc[:, bass.ds(i * AW, AW)], zrow[:, :]).then_inc(acc_clear, 1)

            def feed(k):
                pool.wait_ge(added, 4 + (k + 1) * S)
                if k == 0:
                    pool.wait_ge(norm_in, 3)
                with nc.gpsimd.Fori(0, NI) as i:
                    for j in range(TB):
                        t = i * TB + j
                        pool.wait_ge(rows_T, CR + k * NT + t + (0 if j == 0 else -1))
                        pool.nop(nofuse=True)
                        nc.gpsimd.tensor_copy(nb[:, (j % 2) * C:(j % 2 + 1) * C], acc[:, bass.ds(t * AW, C)]
                                              ).then_inc(nb_ready, 1)
                        if k < HOPS - 1:
                            pool.wait_ge(nb_ready, k * NT + t + 1)
                            pool.nop(nofuse=True)
                            nc.gpsimd.tensor_copy(acc[:, bass.ds(t * AW, AW)], zrow[:, :]).then_inc(acc_clear, 1)

            def clear(m):
                with nc.gpsimd.Fori(0, NT) as i:
                    pool.wait_ge(nb_ready, m * NT + i + 1)
                    pool.nop(nofuse=True)
                    nc.gpsimd.tensor_copy(acc[:, bass.ds(i * AW, AW)], zrow[:, :]).then_inc(acc_clear, 1)

            def gather_conv(k):
                pool.wait_ge(table_stored, 16 * NI * (k + 1))
                with nc.gpsimd.Fori(0, S // U) as i:
                    for j in range(U):
                        if j % UH == 0:
                            pool.wait_ge(idx_in[j // UH], 16 * k * (S // U) + i * 16 + 16)
                        pool.wait_ge(products_done, k * S + i * U + j + 1)
                        pool.nop(nofuse=True)
                        pool.indirect_dma_start(ring3[:, j, 0:C], None, conv_tab[k],
                                                bass.IndirectOffsetOnAxis(ap=idx[:, (j // UH) * G + j % UH:(j // UH) * G + j % UH + 1], axis=0)
                                                ).then_inc(gathered[j], 16)

            def gather_attn(l):
                pool.wait_ge(table_stored, 16 * NI * (HOPS + l + 1))
                with nc.gpsimd.Fori(0, NG // GB) as i:
                    for j in range(GB * G):
                        if j % G == 0:
                            n = (HOPS * (S // U) if j < U else 0) + l * (NG // GB)
                            pool.wait_ge(idx_in[j // G], 16 * n + i * 16 + 16)
                        pool.wait_ge(products_done, CR + (HOPS + l) * S + i * GB * G + j + 1 - GB * G)
                        pool.nop(nofuse=True)
                        pool.indirect_dma_start(ring3[:, j, 0:TW], None, attn_tab[l],
                                                bass.IndirectOffsetOnAxis(ap=idx[:, j:j + 1], axis=0)
                                                ).then_inc(group_in[j // G], 16)

            clear_first()
            pool.wait_ge(steps_ready, 1)
            link(nc.gpsimd.memset(xr[:, NFULL, :], 0.0))
            nc.gpsimd.memset(ring3[:, 0:U, ONES_COL:ONES_COL + 1], 1.0).then_inc(steps_ready, 1)
            for k in range(HOPS):
                gather_conv(k)
                feed(k)
            pool.wait_ge(stored, 16 * NI)
            clear(HOPS)
            for l in range(LAYERS):
                gather_attn(l)
                pool.wait_ge(nself, l + 1)
                with nc.gpsimd.Fori(0, NI) as i:
                    pool.wait_ge(back_in, 16 * (NI + l * NI) + i * 16 + 16)
                    for j in range(TB):
                        r4 = ring[:, bass.ds((i * TB + j) * C, C)].rearrange("p (h c) -> p h c", h=H)
                        e4 = es[:, bass.ds((i * TB + j) * H, H)].rearrange("p (h o) -> p h o", o=1).to_broadcast([P, H, CH])
                        nc.gpsimd.tensor_tensor(r4, r4, e4, ALU.mult).then_inc(self_ready, 1)
                if l < LAYERS - 1:
                    clear(HOPS + 1)

        @block.scalar
        def _(act):
            chain = [0]

            def link(ins):
                chain[0] += 1
                ins.then_inc(act_chain, 1)
                act.wait_ge(act_chain, chain[0])

            act.wait_ge(consts, 1)
            nc.scalar.copy(t1[:, 1:2], ones[:, 0:1]).then_inc(staged, 2)
            act.wait_ge(dlin_ready, 1)
            for t in range(NT):
                link(nc.scalar.activation(sgn, dlin_f, ACT.Sign, scale=-1.0, bias=thr[:, t:t + 1],
                                          accum_out=cnt[:, t:t + 1]))
            nc.scalar.copy(t1[:, 0:1], cnt[:, 0:1]).then_inc(counts_ready, 1)

            def root(dst_, n):
                act.wait_ge(norm_in, n)
                nc.scalar.activation(dst_, dst_, ACT.Sqrt).then_inc(norm_sq, 1)

            root(rstd[:, :], 1)
            root(onorm[:, :], 2)
            act.wait_ge(norm_ready, 1)
            for t in range(NT):
                nc.scalar.activation(xa[:, t, :], xa[:, t, :], ACT.Relu, scale=rstd[:, t:t + 1],
                                     bias=nbias[:, t:t + 1]).then_inc(ln_rows, 1)

            for k in range(HOPS - 1):
                if k == 0:
                    root(inorm[:, :], 3)
                with nc.scalar.Fori(0, NI) as i:
                    act.wait_ge(table_stored, 16 * (NI * (k + 1)) + i * 16)
                    for j in range(TB):
                        act.wait_ge(proj_read, 2 + k * NT + i * TB + j + 1)
                        nc.scalar.activation(stage[:, 0, j, 0:C], tmp[:, (j % 2) * C:(j % 2 + 1) * C], ACT.Relu,
                                             scale=onorm[:, bass.ds(i * TB + j, 1)]).then_inc(staged, 1)
            root(rstd[:, :], 4)
            act.wait_ge(norm_ready, 2)
            def feed(m, ready, scaled):
                with nc.scalar.Fori(0, NI) as i:
                    for j in range(TB):
                        t = i * TB + j
                        act.wait_ge(ready[0], ready[1] + t + 1)
                        act.wait_ge(rows_T, CR + m * NT + t + (0 if j == 0 else -1))
                        to, a = nb[:, (j % 2) * C:(j % 2 + 1) * C], acc[:, bass.ds(t * AW, C)]
                        if scaled:
                            nc.scalar.activation(to, a, ACT.Relu, scale=rstd[:, bass.ds(t, 1)],
                                                 bias=nbias[:, bass.ds(t, 1)]).then_inc(nb_ready, 1)
                        else:
                            nc.scalar.activation(to, a, ACT.Relu).then_inc(nb_ready, 1)

            feed(HOPS, (mid_ready, 0), True)

            for l in range(LAYERS):
                def copy_quad(q, qq):
                    act.wait_ge(ohT_done, q + 1)
                    act.wait_ge(logits_done, q + 1)
                    nc.scalar.copy(ohT[:, (qq % 2) * 4 * P:(qq % 2 + 1) * 4 * P], pso[qq % 2][:, :]
                                   ).then_inc(ohT_copied, 1)

                def copy_logits(g, b):
                    act.wait_ge(logits_done, g * Q + (2 + qb + Q))
                    nc.scalar.copy(ad[:, b % 2 * 2 * H * G:(b % 2 + 1) * 2 * H * G], psad[:, 0:G * 2 * H]
                                   ).then_inc(ad_ready, 1)

                def square_quad(col, at):
                    for k in range(4):
                        sq = nc.scalar.activation(oh[:, (at + k) * P:(at + k + 1) * P], iota[:, :], ACT.Square,
                                                  scale=-1.0, bias=dloc[:, col(k)])
                    sq.then_inc(squares_ready, 1)

                def onehot_quad(at, c):
                    act.wait_ge(squares_ready, c)
                    o4 = oh[:, at * P:(at + 4) * P]
                    nc.scalar.activation(o4, o4, ACT.Relu, scale=-1.0, bias=ones[:, 0:1]).then_inc(quads_ready, 1)

                def exponentials(g, b):
                    act.wait_ge(expo_ready, g + (GB + l * (NG + 1) + 1))
                    nc.scalar.activation(slot(b)[:, :, C:C + H].rearrange("p g h -> p h g"),
                                         hg(dd[:, 0:H * G]), ACT.Exp).then_inc(e_ready, 1)
                    nc.scalar.activation(eself[:, :], dd[:, H * G:2 * H * G], ACT.Exp).then_inc(e_ready, 1)
                    act.wait_ge(lf_done, g + (l * (NG + 1) + 1))
                    nc.scalar.activation(resc[:, :], psb[:, HALF + 4:HALF + 4 + H], ACT.Exp).then_inc(factor_ready, 1)

                def weigh(b, k):
                    for h in range(DVEC // CH, H):
                        r = ring3[:, b * G + k, h * CH:(h + 1) * CH]
                        nc.scalar.activation(r, r, ACT.Copy, scale=ring3[:, b * G + k, C + h:C + h + 1]
                                             ).then_inc(weighted_a, 1)

                act.wait_ge(table_stored, 16 * NI * (HOPS + l + 1))
                act.wait_ge(proj_read, 2 + (HOPS + l + 1) * NT)
                qb = l * (NG + 2) * Q
                for q in range(2 * Q + 1):
                    square_quad(lambda k: slice(4 * q + k, 4 * q + k + 1), 4 * q)
                    onehot_quad(4 * q, l * QL + q + 1)
                    if q:
                        copy_quad(qb + q - 1, q - 1)
                    if q == Q:
                        copy_logits(0, 0)
                copy_logits(1, 1)
                exponentials(0, 0)
                with nc.scalar.Fori(0, NG // GB) as it:
                    for b in range(GB):
                        g = it * GB + b
                        n = it * GB * Q + (qb + (b + 2) * Q)
                        act.wait_ge(e_ready, it * GB * 2 + 2 * (l * (NG + 1) + b + 1))
                        for k in range(G):
                            weigh(b, k)
                            q = k // 3
                            if q < Q and k % 3 == 0:
                                at = (b + 2) * G + 4 * (q + 1)
                                square_quad(lambda k: bass.ds(it * GB * G + at + k, 1), at % RING)
                            if q < Q and k % 3 == 1:
                                onehot_quad(at % RING, it * GB * Q + (l * QL + (b + 2) * Q + q + 2))
                                copy_quad(n + q, q)
                        copy_logits(g + 2, b)
                        exponentials(g + 1, (b + 1) % GB)
                if l < LAYERS - 1:
                    feed(HOPS + 1, (mid_ready, NT), False)

        @block.tensor
        def _(pe):
            pe.wait_ge(consts, 1)
            nc.tensor.matmul(psad[:, 0:NT], zero_b, zero_b[:, 0:NT], start=True, stop=False,
                             skip_group_check=True).then_inc(products_done, CR)
            nc.tensor.matmul(psb[:, 0:2], ident[:, :], ident[:, 0:2], start=True, stop=True).then_inc(hist_done, 2)
            nc.tensor.matmul(psb[:, 0:2], ident[:, :], ident[:, 0:2], start=True, stop=True).then_inc(rows_T, CR)
            nc.tensor.matmul(psb[:, 0:2], ident[:, :], ident[:, 0:2], start=True, stop=True).then_inc(logits_done, 2)
            nc.tensor.matmul(psb[:, 0:2], ident[:, :], ident[:, 0:2], start=True, stop=True).then_inc(projected, 2)
            def hist(first, end):
                with nc.tensor.Fori(first, end) as i:
                    for b in range(2):
                        pe.wait_ge(hist_onehots, 2 * i + b + 1)
                        for j in range(HB):
                            mm = nc.tensor.matmul(psad[:, 0:NT], oh_lo[:, b, j, :], oh_hi[:, b, j, :], start=False,
                                                  stop=False, skip_group_check=True)
                        mm.then_inc(hist_done, 1)

            hist(0, NH // 2)
            pe.wait_ge(counts_ready, 1)
            nc.tensor.matmul(main[0][:, 0:NT], ones[:, :], cnt, start=True, stop=True).then_inc(counts_sum, 1)
            hist(NH // 2, NH)
            nc.tensor.matmul(psad[:, 0:NT], zero_b, zero_b[:, 0:NT], start=False, stop=True,
                             skip_group_check=True).then_inc(hist_done, 1)
            n = 0
            for tabl, w in ((srowf, 1), (dl, 1), (efr, 2)):
                pe.wait_ge(rowsf_ready, w)
                for b in range(SB):
                    if n >= 4:
                        pe.wait_ge(rowsT_read, n - 3)
                    nc.tensor.transpose(main[n % 4][:, 0:P], b3(tabl)[:, b, :], ident[:, :]).then_inc(rowsT_done, 1)
                    n += 1

            def conv(k):
                with nc.tensor.Fori(0, S // U) as i:
                    for j in range(U):
                        pe.wait_ge(onehots, oh_base(k) + i * U + j + 1)
                        pe.wait_ge(added, k * S + i * U + j + 1)
                        pe.wait_ge(gathered[j], 16 * k * (S // U) + i * 16 + 16)
                        nc.tensor.matmul(main[j % 4][:, 0:C + 1], oh[:, (j % OHR) * P:(j % OHR + 1) * P],
                                         ring3[:, j, 0:C + 1], start=True, stop=True).then_inc(products_done, 1)

            def project(m, weights, width):
                def turn(i, j):
                    pe.wait_ge(nb_ready, m * NT + i * TB + j + 1)
                    pe.wait_ge(rows_T_copied, m * NT + i * TB + j + (2 if j == 0 else 1))
                    for b in range(2):
                        mm = nc.tensor.transpose(pso[j % 2][:, b * P:(b + 1) * P],
                                                 nb[:, (j % 2) * C + b * P:(j % 2) * C + (b + 1) * P], ident[:, :])
                    mm.then_inc(rows_T, 1)

                def multiply(i, j):
                    pe.wait_ge(rows_T_copied, m * NT + i * TB + j + 3)
                    pe.wait_ge(proj_read, m * NT + i * TB + j + (2 if j == 0 else 1))
                    for b in range(2):
                        mm = nc.tensor.matmul(main[j % 2][:, 0:width], aT[:, (j % 2) * C + b * P:(j % 2) * C + (b + 1) * P],
                                              weights[:, b * width:(b + 1) * width], start=b == 0, stop=b == 1)
                    mm.then_inc(projected, 1)

                with nc.tensor.Fori(0, NI) as i:
                    turn(i, 0)
                    for j in range(TB):
                        if j < TB - 1:
                            turn(i, j + 1)
                        multiply(i, j)

            for k in range(HOPS):
                conv(k)
                pe.wait_ge(added, 4 + (k + 1) * S)
                pe.wait_ge(w_in, 32 * (k + 1))
                project(k, wc, C)
            for l in range(LAYERS):
                pe.wait_ge(wcat_ready, l + 1)
                project(HOPS + l, wcat, PW)
                qb = l * (NG + 2) * Q

                def turn_quad(n, b, q):
                    pe.wait_ge(quads_ready, n + (l + q + 1))
                    pe.wait_ge(ohT_copied, n + q + 1)
                    for k in range(4 * q, 4 * q + 4):
                        mm = nc.tensor.transpose(pso[q % 2][:, (k % 4) * P:(k % 4 + 1) * P],
                                                 oh[:, (b * G + k) * P:(b * G + k + 1) * P], ident[:, :])
                    mm.then_inc(ohT_done, 1)

                def tiles_of(g):
                    return nc.values_load_multi_w_load_instructions(
                        tpk[0:1, bass.ds(g * Q, Q)], engines=[mybir.EngineType.PE], min_val=0,
                        max_val=(1 << 24) - 1)[1]

                def logit_step(n, pk, j):
                    q, k = j // 4, j % 4
                    if k == 0:
                        pe.wait_ge(ohT_copied, n + q + 3)
                    t = tile_number((pk[q] >> (6 * k)) & 63)
                    mm = nc.tensor.matmul(psad[:, j * 2 * H:(j + 1) * 2 * H],
                                          ohT[:, ((q % 2) * 4 + k) * P:((q % 2) * 4 + k + 1) * P],
                                          tv[:, bass.ds(t * 2 * H, 2 * H)], start=True, stop=True)
                    if k == 3:
                        mm.then_inc(logits_done, 1)

                def turn_logits(c):
                    pe.wait_ge(v_ready, c)
                    pe.nop(nofuse=True)
                    nc.tensor.transpose(psb[0:H * G, 0:P], v[:, :], ident[:, :]).then_inc(vT_done, 1)

                def turn_ends(c):
                    pe.wait_ge(scan_ready, c)
                    pe.nop(nofuse=True)
                    nc.tensor.transpose(psb[0:1, HALF:HALF + H * G], f1[:, P - 1:P], ident[0:H * G, 0:H * G])
                    nc.tensor.transpose(psb[0:1, HALF + H * G:HALF + 2 * H * G], r1[:, 0:1], ident[0:H * G, 0:H * G]
                                        ).then_inc(ends_done, 1)

                def turn_carries(c):
                    pe.wait_ge(carry_ready, c)
                    nc.tensor.matmul(psb[0:H * G, HALF:HALF + 1], co[0:1, :], ones[0:1, 0:1], start=True, stop=True)
                    nc.tensor.matmul(psb[0:H * G, HALF + 1:HALF + 2], do[0:1, :], ones[0:1, 0:1],
                                     start=True, stop=True).then_inc(carry_done, 1)

                def turn_maxima(c):
                    pe.wait_ge(max_ready, c)
                    pe.nop(nofuse=True)
                    nc.tensor.transpose(psb[:, P:P + H * G], mrow[:, :], ident[0:H * G, 0:H * G]).then_inc(maxT_done, 1)

                def spread_factor(c, b):
                    pe.wait_ge(expo_ready, GB + c)
                    nc.tensor.matmul(psb[:, HALF + 4:HALF + 4 + H], oh[0:1, b * G * P:b * G * P + P], lf[0:1, :],
                                     start=True, stop=True).then_inc(lf_done, 1)

                for g in range(2):
                    pk = tiles_of(g)
                    if g + l:
                        pe.wait_ge(ad_ready, l * (NG + 2) + g)
                    for q in range(Q):
                        turn_quad(qb + g * Q, g, q)
                        for j in range(4 * q, 4 * q + 4):
                            logit_step(qb + g * Q, pk, j)
                turn_logits(l * (NG + 1) + 1)
                turn_ends(l * (NG + 1) + 1)
                turn_carries(l * (NG + 1) + 1)
                turn_maxima(l * (NG + 1) + 1)
                spread_factor(l * (NG + 1) + 1, 0)
                with nc.tensor.Fori(0, NG // GB) as it:
                    for b in range(GB):
                        pk = tiles_of(it * GB + b + 2)
                        n = it * GB * Q + (qb + (b + 2) * Q)
                        c = it * GB + (l * (NG + 1) + b + 2)
                        for k in range(G):
                            if k % 3 == 0 and k // 3 < Q:
                                turn_quad(n, (b + 2) % GB, k // 3)
                            s = (HOPS + l) * S + it * GB * G + b * G + k
                            pe.wait_ge(added, s + 1)
                            pe.wait_ge(weighted_v, s + (LEAD * l - HOPS * S + 1))
                            pe.wait_ge(weighted_a, (s - HOPS * S + 1) * (H - DVEC // CH))
                            nc.tensor.matmul(main[k % 4][:, 0:AW], oh[:, (b * G + k) * P:(b * G + k + 1) * P],
                                             ring3[:, b * G + k, :], start=True, stop=True).then_inc(products_done, 1)
                            if k == 1:
                                turn_logits(c)
                            if k == 4:
                                turn_ends(c)
                            if k == 7:
                                turn_carries(c)
                            if k == 10:
                                turn_maxima(c)
                            if k == G - 2:
                                spread_factor(c, (b + 1) % GB)
                            if k == 3:
                                pe.wait_ge(ad_ready, c + l)
                            for j in range(G):
                                if 3 + j * (G - 3) // G == k:
                                    logit_step(n, pk, j)

        @block.vector
        def _(dve):
            chain = [0]

            def link(ins):
                chain[0] += 1
                ins.then_inc(dve_chain, 1)
                dve.wait_ge(dve_chain, chain[0])

            link(nc.vector.memset(sm4[:, :], 0.0))
            nc.vector.memset(t2[:, :], 0.0).then_inc(added, 4)
            nc.vector.memset(f1[:, :], 0.0).then_inc(rows_T_copied, 2)
            nc.vector.memset(r1[:, :], 0.0).then_inc(proj_read, 2)
            nc.vector.memset(v[:, :], 0.0).then_inc(ohT_copied, 2)
            nc.vector.memset(alpha[:, :], 0.0).then_inc(expo_ready, GB)

            dve.wait_ge(lin_in, 16)
            link(nc.vector.tensor_scalar(hi_i, lin, 7, None, ALU.arith_shift_right))
            link(nc.vector.tensor_scalar(lo_i, lin, P - 1, None, ALU.bitwise_and))
            link(nc.vector.tensor_copy(hi_b, hi_i))
            link(nc.vector.tensor_copy(lo_b, lo_i))
            dve.wait_ge(consts, 1)
            dve.wait_ge(lin_in, 32)
            link(nc.vector.tensor_scalar(thr, thr, -0.5, None, ALU.add))
            nc.vector.tensor_copy(dlin_f, dlin).then_inc(dlin_ready, 1)

            def hist(a, b):
                with nc.vector.Fori(a, b) as i:
                    for c in range(2):
                        dve.wait_ge(hist_done, 2 * i + c + 1)
                        for to, of, n in ((oh_lo, lo_b, P), (oh_hi, hi_b, NT)):
                            mm = nc.vector.tensor_tensor(
                                to[:, c, :, :],
                                of[:, bass.ds((2 * i + c) * HB, HB)].rearrange("p (k o) -> p k o", o=1)
                                .to_broadcast([P, HB, n]),
                                iota_b[:, 0:n].rearrange("p (o n) -> p o n", o=1).to_broadcast([P, HB, n]),
                                ALU.is_equal)
                        mm.then_inc(hist_onehots, 1)

            hist(0, NH // 2)

            dve.wait_ge(counts_sum, 1)
            link(nc.vector.tensor_scalar(bf, main[0][:, 0:NT], float(EC * P), 0.5, ALU.add, ALU.mult))
            link(nc.vector.tensor_scalar(bf, bf, float(E), None, ALU.min))
            link(nc.vector.tensor_copy(bi, bf))
            link(nc.vector.tensor_scalar(fl, bi, 7, None, ALU.arith_shift_right))
            link(nc.vector.tensor_scalar(bi, bi, float(P - 1), None, ALU.add))
            link(nc.vector.tensor_scalar(ce, bi, 7, None, ALU.arith_shift_right))
            link(nc.vector.tensor_tensor(ov, ce, fl, ALU.subtract))
            link(nc.vector.tensor_tensor_scan(out=pre, data0=zt, data1=ov, initial=0.0, op0=ALU.add, op1=ALU.add))
            link(nc.vector.tensor_tensor(pre, pre, ov, ALU.subtract))
            link(nc.vector.tensor_tensor(cum, pre, ce, ALU.add))
            link(nc.vector.tensor_tensor(cmpt, sid.rearrange("p (b o) -> p b o", o=1).to_broadcast([P, SB, NT]),
                                         cum.rearrange("p (o t) -> p o t", o=1).to_broadcast([P, SB, NT]), ALU.is_ge))
            link(nc.vector.tensor_reduce(ts, cmpt, AX.X, ALU.add))
            link(nc.vector.tensor_tensor(cmpo, cmpt, ov.rearrange("p (o t) -> p o t", o=1).to_broadcast([P, SB, NT]),
                                         ALU.mult))
            link(nc.vector.tensor_reduce(cs, cmpo, AX.X, ALU.add))
            link(nc.vector.tensor_tensor(cs, sid, cs, ALU.subtract))
            link(nc.vector.tensor_scalar(cs, cs, float(EC - 1), 0.0, ALU.min, ALU.max))
            link(nc.vector.tensor_scalar(tsc, ts, float(NT - 1), None, ALU.min))
            link(nc.vector.tensor_scalar(t128, ts, float(P), None, ALU.mult))
            nc.vector.tensor_copy(ci, cs).then_inc(chunks_ready, 1)

            hist(NH // 2, NH)

            dve.wait_ge(rows_in, 16 * 2 * SB)
            tb = t128.rearrange("p (b o) -> p b o", o=1).to_broadcast([P, SB, P])
            link(nc.vector.tensor_tensor(b3(dl), b3(drow), tb, ALU.subtract))
            link(nc.vector.tensor_scalar(dl, dl, -1.0, float(P), ALU.max, ALU.min))
            link(nc.vector.tensor_tensor(key[:, :, 1:P + 1], b3(dl), tb, ALU.add))
            nc.vector.tensor_tensor(key[:, :, 1:P + 1], key[:, :, 1:P + 1], tb, ALU.add).then_inc(chunks_ready, 1)
            nc.vector.tensor_scalar(srowf, srow, float(N - 1), None, ALU.min).then_inc(rowsf_ready, 1)

            dve.wait_ge(hist_done, 2 * NH + 3)
            link(nc.vector.tensor_scalar(onorm[:, :], psad[:, 0:NT], 1.0, None, ALU.max))
            dve.wait_ge(x_in, 16 * 8)
            for t in range(NT):
                link(nc.vector.bn_stats(bnst[:, 0:6], xa[:, t, :]))
                link(nc.vector.bn_aggr(stat3[:, t, :], bnst[:, 0:6]))

            def row_scales(n, m):
                nc.vector.tensor_scalar(rstd[:, :], stat3[:, :, 1], EPS, None, ALU.add).then_inc(norm_in, 1)
                dve.wait_ge(norm_sq, n)
                link(nc.vector.reciprocal(rstd[:, :], rstd[:, :]))
                link(nc.vector.tensor_tensor(nbias[:, :], stat3[:, :, 0], rstd[:, :], ALU.mult))
                return nc.vector.tensor_scalar(nbias[:, :], nbias[:, :], -1.0, None, ALU.mult)

            link(row_scales(1, 1))
            nc.vector.tensor_copy(onorm[:, :], onorm[:, :]).then_inc(norm_in, 1)
            dve.wait_ge(norm_sq, 2)
            link(nc.vector.reciprocal(onorm[:, :], onorm[:, :]))
            link(nc.vector.tensor_tensor(rstd[:, :], rstd[:, :], onorm[:, :], ALU.mult))
            nc.vector.tensor_tensor(nbias[:, :], nbias[:, :], onorm[:, :], ALU.mult).then_inc(norm_ready, 1)

            dve.wait_ge(key_edge, 32)
            link(nc.vector.tensor_tensor(b3(sfr), key[:, :, 1:P + 1], key[:, :, 0:P], ALU.not_equal))
            link(nc.vector.tensor_scalar(sfr, sfr, -BIG, None, ALU.mult))
            nc.vector.tensor_tensor(b3(efr), key[:, :, 1:P + 1], key[:, :, 2:P + 2], ALU.not_equal
                                    ).then_inc(rowsf_ready, 1)
            for n in range(2 * SB):
                dve.wait_ge(rowsT_done, n + 1)
                to = sidx if n < SB else dloc
                b = n % SB
                nc.vector.tensor_copy(to[:, b * P:(b + 1) * P], main[n % 4][:, 0:P]).then_inc(rowsT_read, 1)
            for n in range(2 * SB, 3 * SB):
                dve.wait_ge(rowsT_done, n + 1)
                b = n % SB
                nc.vector.tensor_copy(endt[:, b * P:(b + 1) * P], main[n % 4][:, 0:P]).then_inc(rowsT_read, 1)
            link(nc.vector.tensor_scalar(efr, efr, -BIG, None, ALU.mult))
            link(nc.vector.tensor_reduce(sany, b3(sfr), AX.X, ALU.min))
            nc.vector.tensor_reduce(eany, b3(efr), AX.X, ALU.min).then_inc(flags_ready, 1)
            dve.wait_ge(rowsT_read, 3 * SB)
            dve.wait_ge(tiles_in, 16)
            tq = trow[0:1, :].rearrange("p (q k) -> p q k", k=4)
            link(nc.vector.tensor_copy(tsum[0:1, :], tq[:, :, 3]))
            for k in (2, 1, 0):
                link(nc.vector.scalar_tensor_tensor(out=tsum[0:1, :], in0=tsum[0:1, :], scalar=64.0, in1=tq[:, :, k],
                                                    op0=ALU.mult, op1=ALU.add))
            link(nc.vector.tensor_copy(tpk[0:1, :], tsum[0:1, :]))
            dve.wait_ge(flags_out, 64)
            nc.vector.memset(sm4[:, :], 0.0).then_inc(steps_ready, 1)
            dve.wait_ge(steps_ready, 2)
            dve.wait_ge(acc_clear, NT)

            def onehot(col, at):
                return nc.vector.tensor_scalar(oh[:, at * P:(at + 1) * P], iota[:, :], dloc[:, col], None,
                                               ALU.is_equal).then_inc(onehots, 1)

            def accumulate(t, k, width, s):
                dve.wait_ge(products_done, CR + s + 1)
                dve.wait_ge(added, 4 + s)
                a = acc[:, bass.ds(t * AW, width)]
                nc.vector.tensor_tensor(a, a, main[k][:, 0:width], ALU.add).then_inc(added, 1)

            def conv(k):
                dve.wait_ge(table_stored, 16 * NI * (k + 1))
                if k:
                    dve.wait_ge(onehots, oh_base(k))
                    dve.wait_ge(acc_clear, NT * (k + 1))
                for s in range(AHEAD):
                    onehot(slice(s, s + 1), s)
                with nc.vector.Fori(0, S // U) as i:
                    for j in range(U):
                        if j % 4 == 0:
                            pk = dve.value_load(tpk[0:1, bass.ds(i * (U // 4) + j // 4, 1)], min_val=0,
                                                max_val=(1 << 24) - 1)
                        dve.wait_ge(products_done, CR + k * S + i * U + j)
                        onehot(bass.ds(i * U + j + AHEAD, 1), (j + AHEAD) % OHR)
                        t = tile_number((pk >> (6 * (j % 4))) & 63)
                        accumulate(t, j % 4, C + 1, k * S + i * U + j)

            def project(m, epilogue, prepare=None):
                def copy_out(i, j):
                    dve.wait_ge(rows_T, CR + m * NT + i * TB + j + 1)
                    dve.wait_ge(projected, m * NT + i * TB + j + (2 if j == 0 else 1))
                    nc.vector.tensor_copy(aT[:, (j % 2) * C:(j % 2 + 1) * C], pso[j % 2][:, 0:C]
                                          ).then_inc(rows_T_copied, 1)

                with nc.vector.Fori(0, NI) as i:
                    copy_out(i, 0)
                    for j in range(TB):
                        if j < TB - 1:
                            copy_out(i, j + 1)
                        dve.wait_ge(projected, 2 + m * NT + i * TB + j + 1)
                        epilogue(i, j)

            def with_norm_and_bias(to, i, j):
                return nc.vector.scalar_tensor_tensor(out=to, in0=main[j % 2][:, 0:C],
                                                      scalar=inorm[:, bass.ds(i * TB + j, 1)], in1=bias[:, :],
                                                      op0=ALU.mult, op1=ALU.add)

            for k in range(HOPS):
                conv(k)
                dve.wait_ge(added, 4 + (k + 1) * S)
                dve.wait_ge(w_in, 32 * (k + 1))
                if k == 0:
                    link(nc.vector.tensor_scalar(indeg0[:, :], acc3[:, :, ONES_COL], 0.0, None, ALU.is_equal))
                    nc.vector.tensor_scalar(inorm[:, :], acc3[:, :, ONES_COL], 1.0, None, ALU.max).then_inc(norm_in, 1)
                    dve.wait_ge(norm_sq, 3)
                    link(nc.vector.reciprocal(inorm[:, :], inorm[:, :]))
                if k < HOPS - 1:
                    def epilogue(i, j):
                        dve.wait_ge(staged, k * NT + i * TB + j + (2 if j == 0 else 1))
                        with_norm_and_bias(tmp[:, (j % 2) * C:(j % 2 + 1) * C], i, j).then_inc(proj_read, 1)
                    project(k, epilogue)
                else:
                    def epilogue(i, j):
                        if j == 0:
                            dve.wait_ge(rest_in, 16)
                            dve.wait_ge(back_in, i * 16 + 16)
                        t = i * TB + j
                        a = acc[:, bass.ds(t * AW, C)]
                        dve.wait_ge(proj_read, 2 + k * NT + t)
                        with_norm_and_bias(tmp[:, 0:C], i, j).then_inc(proj_read, 1)
                        dve.wait_ge(proj_read, 2 + k * NT + t + 1)
                        nc.vector.tensor_tensor(tmp[:, C:2 * C], tmp[:, 0:C], ring[:, bass.ds(t * C, C)], ALU.add
                                                ).then_inc(dve_chain, 1)
                        dve.wait_ge(dve_chain, chain[0] + 4 * t + 1)
                        dve.nop(nofuse=True)
                        nc.vector.bn_stats(bnst[:, 0:6], tmp[:, C:2 * C]).then_inc(dve_chain, 1)
                        nc.vector.tensor_copy(a, tmp[:, C:2 * C]).then_inc(mid_ready, 1)
                        dve.wait_ge(dve_chain, chain[0] + 4 * t + 2)
                        dve.nop(nofuse=True)
                        nc.vector.bn_aggr(bnst[:, 6:8], bnst[:, 0:6]).then_inc(dve_chain, 1)
                        dve.wait_ge(dve_chain, chain[0] + 4 * t + 3)
                        nc.vector.tensor_copy(stat[:, bass.ds(t * 2, 2)], bnst[:, 6:8]).then_inc(dve_chain, 1)
                        dve.wait_ge(dve_chain, chain[0] + 4 * t + 4)
                        dve.wait_ge(mid_ready, t + 1)
                    project(k, epilogue)
                    chain[0] += 4 * NT
                    row_scales(4, 2).then_inc(norm_ready, 1)

            def logit_columns(l):
                dve.wait_ge(w_in, 32 * HOPS + 64 * l + 48)
                for b in range(2):
                    for a in range(2):
                        link(nc.vector.tensor_tensor(tmp[:, 0:C], wcat[:, b * PW:b * PW + C], att[:, a * C:(a + 1) * C],
                                                     ALU.mult))
                        red = nc.vector.tensor_reduce(wcat[:, b * PW + C + a * H:b * PW + C + (a + 1) * H],
                                                      tmp[:, 0:C].rearrange("p (h c) -> p h c", h=H), AX.X, ALU.add)
                        if a + b < 2:
                            link(red)
                red.then_inc(wcat_ready, 1)
                dve.wait_ge(wcat_ready, l + 1)

            for l in range(LAYERS):
                logit_columns(l)

                def epilogue(i, j):
                    t = i * TB + j
                    if j == 0:
                        dve.wait_ge(table_stored, 16 * NI * (HOPS + l) + i * 16)
                    nc.vector.tensor_copy(stage[:, 0, j, 0:PW], main[j % 2][:, 0:PW]).then_inc(staged, 1)
                    dve.wait_ge(staged, 2 + (HOPS - 1 + l) * NT + t + 1)
                    nc.vector.tensor_copy(tv[:, bass.ds(t * 2 * H, 2 * H)], stage[:, 0, j, C:PW]
                                          ).then_inc(proj_read, 1)
                project(HOPS + l, epilogue)
                dve.wait_ge(proj_read, 2 + (HOPS + l + 1) * NT)
                dve.wait_ge(table_stored, 16 * NI * (HOPS + l + 1))
                dve.wait_ge(acc_clear, NT * (HOPS + l + 1))

                for b in range(GB):
                    o = b * H * G
                    link(nc.vector.memset(hg(rsf[0:1, o:o + H * G])[:, :, 0:1], -BIG))
                    link(nc.vector.memset(hg(ref[0:1, o:o + H * G])[:, :, G - 1:G], -BIG))
                link(nc.vector.memset(hg(dw[0:1, :])[:, :, G - 1:G], -BIG))
                link(nc.vector.memset(hg(cw[0:1, :])[:, :, 0:1], 0.0))

                mark_base, marks = chain[0], [0]

                def mark(ins):
                    marks[0] += 1
                    ins.then_inc(dve_chain, 1)
                    return marks[0]

                def after(m):
                    dve.wait_ge(dve_chain, mark_base + m)

                def logits_part(i, b, c):
                    asrc = slot(b)[:, :, C:C + H].rearrange("p g h -> p h g")
                    asrc_dst, adst_dst = logits_of(b)
                    per = NG // GB
                    rounds = (i + 1) * (per - 1) // per if b == 0 else i
                    dve.wait_ge(group_in[b], rounds * (16 * G) + 16 * G * (l * (NG // GB) + 1))
                    dve.wait_ge(ad_ready, c + l)
                    nc.vector.tensor_tensor(hg(v[:, :]), asrc, asrc_dst, ALU.max).then_inc(v_ready, 1)
                    m1 = mark(nc.vector.tensor_tensor(hg(t1[:, :]), asrc, adst_dst, ALU.add))
                    m2 = mark(nc.vector.tensor_tensor(hg(t2[:, :]), asrc_dst, adst_dst, ALU.add))
                    after(m1)
                    mark(nc.vector.scalar_tensor_tensor(out=alpha[:, :], in0=t1[:, :], scalar=SLOPE, in1=t1[:, :],
                                                        op0=ALU.mult, op1=ALU.max))
                    after(m2)
                    return mark(nc.vector.scalar_tensor_tensor(out=lself[:, :], in0=t2[:, :], scalar=SLOPE,
                                                               in1=t2[:, :], op0=ALU.mult, op1=ALU.max))

                def rows_part(b, c):
                    sf, ef = sfl[:, b * P:(b + 1) * P], efl[:, b * P:(b + 1) * P]
                    dve.wait_ge(flags_in[b], flags_at[0])
                    dve.wait_ge(vT_done, c)
                    mark(nc.vector.tensor_tensor_scan(out=f1[:, :], data0=sf, data1=psb[0:H * G, 0:P], initial=-BIG,
                                                      op0=ALU.add, op1=ALU.max))
                    nc.vector.tensor_tensor_scan(out=r1[:, ::-1], data0=ef[:, ::-1], data1=psb[0:H * G, 0:P][:, ::-1],
                                                 initial=-BIG, op0=ALU.add, op1=ALU.max).then_inc(scan_ready, 1)
                    mark(nc.vector.tensor_scalar(sm4[0:1, 4 * H:4 * H + 1], sf[0:1, 0:1], 0.0, None, ALU.is_equal))

                def carry_part(b, c):
                    o = b * H * G
                    ends = psb[0:1, HALF:HALF + 2 * H * G]
                    dve.wait_ge(ends_done, c)
                    m1 = mark(nc.vector.tensor_copy(hg(cw[0:1, :])[:, :, 1:G], hg(ends[:, 0:H * G])[:, :, 0:G - 1]))
                    m2 = mark(nc.vector.tensor_copy(hg(dw[0:1, :])[:, :, 0:G - 1], hg(ends[:, H * G:])[:, :, 1:G]))
                    after(m1)
                    m3 = mark(nc.vector.tensor_tensor_scan(out=co[0:1, :], data0=rsf[0:1, o:o + H * G],
                                                           data1=cw[0:1, :], initial=-BIG, op0=ALU.add, op1=ALU.max))
                    after(m2)
                    m4 = mark(nc.vector.tensor_tensor_scan(out=do[0:1, ::-1], data0=ref[0:1, o:o + H * G][:, ::-1],
                                                           data1=dw[0:1, ::-1], initial=-BIG, op0=ALU.add, op1=ALU.max))
                    after(m3)
                    nc.vector.scalar_tensor_tensor(
                        out=nxt[0:1, :].rearrange("p (h o) -> p h o", o=1), in0=hg(co[0:1, :])[:, :, G - 1:G],
                        scalar=rlast[0:1, b:b + 1], in1=hg(ends[:, 0:H * G])[:, :, G - 1:G],
                        op0=ALU.add, op1=ALU.max).then_inc(carry_ready, 1)
                    after(m4)

                def maxima_part(b, c):
                    sf, ef = sfl[:, b * P:(b + 1) * P], efl[:, b * P:(b + 1) * P]
                    dve.wait_ge(carry_done, c)
                    after(mark(nc.vector.tensor_copy(cin[:, :], psb[0:H * G, HALF:HALF + 2])))
                    mark(nc.vector.tensor_tensor_scan(out=f2[:, :], data0=sf, data1=psb[0:H * G, 0:P],
                                                      initial=cin[:, 0:1], op0=ALU.add, op1=ALU.max))
                    after(mark(nc.vector.tensor_tensor_scan(out=r2[:, ::-1], data0=ef[:, ::-1],
                                                            data1=psb[0:H * G, 0:P][:, ::-1], initial=cin[:, 1:2],
                                                            op0=ALU.add, op1=ALU.max)))
                    nc.vector.tensor_tensor(mrow[:, :], f2[:, :], r2[:, :], ALU.max).then_inc(max_ready, 1)

                def exponents_part(b, c):
                    adst_dst = logits_of(b)[1]
                    one = "p (h o) -> p h o"
                    old, new = sm4[0:1, 0:H], sm4[0:1, H:2 * H]
                    dve.wait_ge(maxT_done, c)
                    m1 = mark(nc.vector.tensor_tensor(hg(t1[:, :]), hg(psb[:, P:P + H * G]), adst_dst, ALU.add))
                    m2 = mark(nc.vector.tensor_tensor(old.rearrange(one, o=1), hg(cw[0:1, :])[:, :, 0:1],
                                                      adst_dst[0:1, :, 0:1], ALU.add))
                    after(m1)
                    m3 = mark(nc.vector.scalar_tensor_tensor(out=mx[:, :], in0=t1[:, :], scalar=SLOPE, in1=t1[:, :],
                                                             op0=ALU.mult, op1=ALU.max))
                    after(m2)
                    m4 = mark(nc.vector.scalar_tensor_tensor(out=new, in0=old, scalar=SLOPE, in1=old,
                                                             op0=ALU.mult, op1=ALU.max))
                    after(m3)
                    mark(nc.vector.tensor_tensor(dd[:, 0:H * G], alpha[:, :], mx[:, :], ALU.subtract))
                    after(m4)
                    m5 = mark(nc.vector.tensor_tensor(old.rearrange(one, o=1), new.rearrange(one, o=1),
                                                      hg(mx[0:1, :])[:, :, 0:1], ALU.subtract))
                    mark(nc.vector.tensor_tensor(dd[:, H * G:2 * H * G], lself[:, :], mx[:, :], ALU.subtract))
                    m6 = mark(nc.vector.tensor_copy(hg(cw[0:1, :])[:, :, 0:1], nxt[0:1, :].rearrange(one, o=1)))
                    after(m5)
                    nc.vector.tensor_scalar(lf[0:1, :], old, sm4[0:1, 4 * H:4 * H + 1], None, ALU.mult
                                            ).then_inc(expo_ready, 1)
                    after(m6)

                c0 = l * (NG + 1) + 1
                flags_at = [FLAG_INCS * (l * (NG // GB + 1) + 1)]
                logits_part(0, 0, c0)
                rows_part(0, c0)
                carry_part(0, c0)
                maxima_part(0, c0)
                exponents_part(0, c0)
                chain[0] += marks[0]
                dve.wait_ge(dve_chain, chain[0])

                def fold_self(b, e, cols):
                    sl = slot(b)
                    dve.wait_ge(e_ready, e)
                    return mark(nc.vector.tensor_tensor(
                        sl[:, :, C + H:AW].rearrange("p g h -> p h g"), hg(eself[:, :]),
                        endt[:, cols].rearrange("p (o g) -> p o g", o=1).to_broadcast([P, H, G]), ALU.mult))

                def weigh(b, k):
                    r = ring3[:, b * G + k, 0:DVEC].rearrange("p (h c) -> p h c", c=CH)
                    w = ring3[:, b * G + k, C:C + DVEC // CH].rearrange("p (h o) -> p h o", o=1)
                    nc.vector.tensor_tensor(r, r, w.to_broadcast([P, DVEC // CH, CH]), ALU.mult
                                            ).then_inc(weighted_v, 1)

                mark_base, marks[0] = chain[0], 0
                fold_self(0, 2 * (l * (NG + 1) + 1), slice(0, G))
                chain[0] += marks[0]
                for k in range(LEAD):
                    weigh(0, k)

                with nc.vector.Fori(0, NG // GB) as it:
                    mark_base, marks[0] = it * MARKS + chain[0], 0
                    for b in range(GB):
                        nb_, s0 = (b + 1) % GB, (HOPS + l) * S + it * GB * G + b * G
                        c = it * GB + (l * (NG + 1) + b + 2)
                        over = 1 if b == GB - 1 else 0
                        per = NG // GB + (nb_ == 0)
                        flags_at[0] = it * FLAG_INCS + FLAG_INCS * (l * per + over + 1)
                        pk = nc.values_load_multi_w_load_instructions(
                            tpk[0:1, bass.ds(it * GB * Q + b * Q, Q)], engines=[mybir.EngineType.DVE], min_val=0,
                            max_val=(1 << 24) - 1)[1]

                        def tile_at(k):
                            return tile_number((pk[k // 4] >> (6 * (k % 4))) & 63)

                        def rescale():
                            dve.wait_ge(factor_ready, it * GB + (l * (NG + 1) + b + 1))
                            dve.wait_ge(added, 4 + s0)
                            t = tile_at(0)
                            a4 = acc[:, bass.ds(t * AW, C)].rearrange("p (h c) -> p h c", h=H)
                            f4 = resc[:, :].rearrange("p (h o) -> p h o", o=1).to_broadcast([P, H, CH])
                            mark(nc.vector.tensor_tensor(a4, a4, f4, ALU.mult))
                            aw = acc[:, bass.ds(t * AW + C, H)]
                            return mark(nc.vector.tensor_tensor(aw, aw, resc[:, :], ALU.mult))

                        def add(k):
                            accumulate(tile_at(k), k % 4, AW, s0 + k)

                        rescaled = rescale()
                        for k in range(G):
                            if k == 0:
                                logits_part(it + over, nb_, c)
                            if k == 3:
                                rows_part(nb_, c)
                            if k == 6:
                                carry_part(nb_, c)
                            if k == 9:
                                maxima_part(nb_, c)
                            if k == 12:
                                exponents_part(nb_, c)
                            if k == 0:
                                after(rescaled)
                            if k == G - LEAD:
                                add(k)
                                fold_self(nb_, it * GB * 2 + 2 * (l * (NG + 1) + b + 2),
                                          bass.ds(it * GB * G + (b + 1) * G, G))
                            if k < G - LEAD:
                                weigh(b, k + LEAD)
                            else:
                                weigh(nb_, k + LEAD - G)
                            if k != G - LEAD:
                                add(k)
                assert marks[0] == MARKS, marks[0]
                chain[0] += MARKS * (NG // GB)

                dve.wait_ge(added, 4 + (HOPS + l + 1) * S)
                link(nc.vector.tensor_tensor(es3, acc3[:, :, C + H:AW],
                                             indeg0[:, :].rearrange("p (t o) -> p t o", o=1).to_broadcast([P, NT, H]),
                                             ALU.add))
                link(nc.vector.tensor_tensor(rs3, es3, acc3[:, :, C:C + H], ALU.add))
                link(nc.vector.tensor_scalar(rs[:, :], rs[:, :], 1e-16, None, ALU.max))
                nc.vector.reciprocal(rs[:, :], rs[:, :]).then_inc(nself, 1)
                dve.wait_ge(nself, l + 1)
                dve.wait_ge(w_in, 32 * HOPS + 64 * (l + 1))
                cb2 = chain[0]
                with nc.vector.Fori(0, NT) as i:
                    dve.wait_ge(self_ready, l * NT + i + 1)
                    a = acc[:, bass.ds(i * AW, C)]
                    a4 = a.rearrange("p (h c) -> p h c", h=H)
                    nc.vector.tensor_tensor(a, a, ring[:, bass.ds(i * C, C)], ALU.add).then_inc(dve_chain, 1)
                    dve.wait_ge(dve_chain, cb2 + 2 * i + 1)
                    nc.vector.tensor_tensor(a4, a4, rs[:, bass.ds(i * H, H)].rearrange("p (h o) -> p h o", o=1)
                                            .to_broadcast([P, H, CH]), ALU.mult).then_inc(dve_chain, 1)
                    dve.wait_ge(dve_chain, cb2 + 2 * i + 2)
                    nc.vector.tensor_tensor(a, a, bias[:, :], ALU.add).then_inc(mid_ready, 1)
                chain[0] += 2 * NT
            dve.wait_ge(mid_ready, 3 * NT)
            with nc.vector.Fori(0, NI) as i:
                dve.wait_ge(back_in, 16 * (3 * NI) + i * 16 + 16)
                for j in range(TB):
                    a = acc[:, bass.ds((i * TB + j) * AW, C)]
                    nc.vector.tensor_tensor(a, a, ring[:, bass.ds((i * TB + j) * C, C)], ALU.add).then_inc(mid_ready, 1)


_INS = ['x', 'src', 'dst', 'L0_gnn_W', 'L0_gnn_b', 'L1_gnn_W1', 'L1_gnn_att_src1', 'L1_gnn_att_dst1', 'L1_gnn_b1',
        'L1_gnn_W2', 'L1_gnn_att_src2', 'L1_gnn_att_dst2', 'L1_gnn_b2']


def kernel(**inputs):
    import numpy as _np
    import concourse.bacc as _bacc
    from concourse import mybir as _mybir
    from concourse.bass_utils import run_bass_kernel_spmd as _run

    nc = _bacc.Bacc("TRN2", target_bir_lowering=False, num_devices=1)
    arrays, args = {}, []
    for name in _INS:
        a = _np.ascontiguousarray(inputs[name])
        arrays[f"in_{name}_dram"] = a
        args.append(nc.dram_tensor(f"in_{name}_dram", a.shape, _mybir.dt.from_np(a.dtype), kind="ExternalInput").ap())
    args.append(nc.dram_tensor("out_0_dram", (N, C), _mybir.dt.float32, kind="ExternalOutput").ap())
    gnn(nc, *args)
    r = _run(nc, [arrays], core_ids=[0])
    return r.results[0]["out_0_dram"]
```

```python
import concourse.bass as bass
from concourse import mybir
from contextlib import ExitStack

F32 = mybir.dt.float32
BF16 = mybir.dt.bfloat16
I32 = mybir.dt.int32
ALU = mybir.AluOpType
ACT = mybir.ActivationFunctionType
AX = mybir.AxisListType

P = 128
N = 6250
E = 100000
C = 256
H = 4
CH = C // H
HOPS = 3
LAYERS = 2
NT = -(-N // P)
NFULL = N // P
NREST = N - NFULL * P
EC = -(-E // P)
EPAD = EC * P - E
G = 16
GB = 4
NG = -(-(EC + NT - 1) // G)
NG += -NG % GB
S = NG * G
Q = G // 4
SB = -(-(S + 2 * G + 4) // P)
SX = SB * P
OUTSIDE = 50 * P
BIG = 1e30
EPS = 1e-5
SLOPE = 0.2
AW = C + 2 * H
TW = C + H
PW = C + 2 * H
RING = GB * G
U = 32
UH = U // 2
AHEAD = 3
OHR = 4
LW = 3 * 2 * H
TB = 7
NI = NT // TB
XB = 4
HB = 17
NH = EC // (2 * HB)
DVEC = 2 * CH
CR = U
assert EC % (2 * HB) == 0 and NT % TB == 0 and S % U == 0 and  S >= EC + NT - 1


def gnn(nc, x, src, dst, gw, gb, w1, as1, ad1, b1, w2, as2, ad2, b2, out):
    ctx = ExitStack()
    with ctx:
        def sb(name, shape, dt=F32):
            return ctx.enter_context(nc.sbuf_tensor(name, shape, dt))

        def sem(name):
            return ctx.enter_context(nc.semaphore(name))

        def dram(name, shape, dt=F32):
            return nc.dram_tensor(name, shape, dt, kind="Internal").ap()

        src_pad = dram("src_pad", (EC, P), I32)
        dst_pad = dram("dst_pad", (EC, P), I32)
        keys = dram("keys", (1, SX * P + 2))
        start_rows = dram("start_rows", (SX, P))
        end_rows = dram("end_rows", (SX, P))
        start_any = dram("start_any", (1, SX))
        end_any = dram("end_any", (1, SX))
        tile_of = dram("tile_of", (1, SX))
        conv_tab = [dram(f"conv_tab{k}", (NT * P, C)) for k in range(HOPS)]
        attn_tab = [dram(f"attn_tab{k}", (NT * P, TW)) for k in range(LAYERS)]
        x1_tab = dram("x1_tab", (NT * P, C))

        ring = sb("ring", [P, RING * AW])
        acc = sb("acc", [P, NT * AW])
        oh = sb("oh", [P, RING * P])
        dloc = sb("dloc", [P, SX])
        sidx = sb("sidx", [P, SX], I32)
        endt = sb("endt", [P, SX])
        tpk = sb("tpk", [1, SX // 4], I32)
        iota = sb("iota", [P, P])
        ident = sb("ident", [P, P])
        ones = sb("ones", [P, P])
        zrow = sb("zrow", [P, AW])
        onorm = sb("onorm", [P, NT])
        inorm = sb("inorm", [P, NT])
        indeg0 = sb("indeg0", [P, NT])
        stat = sb("stat", [P, NT * 2])
        bnst = sb("bnst", [P, 2 * 6])
        rstd = sb("rstd", [P, NT])
        nbias = sb("nbias", [P, NT])
        wc = sb("wc", [P, 2 * C])
        wcat = sb("wcat", [P, 2 * PW])
        bias = sb("bias", [P, C])
        att = sb("att", [P, 2 * C])
        nb = sb("nb", [P, 2 * C])
        aT = sb("aT", [P, 2 * C])
        tmp = sb("tmp", [P, 2 * C])
        tv = sb("tv", [P, NT * 2 * H])
        tvb = sb("tvb", [P, NT * LW], BF16)
        ohT_room = sb("ohT_room", [P, SX])
        ohT = ohT_room[:, 0:4 * P].bitcast(BF16)
        idx = sb("idx", [P, GB * G], I32)
        ad = sb("ad", [P, 2 * G * LW])
        sfl = sb("sfl", [H * G, GB * P])
        efl = sb("efl", [H * G, GB * P])
        rsf = sb("rsf", [1, GB * H * G])
        ref = sb("ref", [1, GB * H * G])
        v = sb("v", [P, H * G])
        f1 = sb("f1", [H * G, P])
        r1 = sb("r1", [H * G, P])
        f2 = sb("f2", [H * G, P])
        r2 = sb("r2", [H * G, P])
        mrow = sb("mrow", [H * G, P])
        alpha = sb("alpha", [P, H * G])
        mx = sb("mx", [P, H * G])
        t1 = sb("t1", [P, H * G])
        t2 = sb("t2", [P, H * G])
        dd = sb("dd", [P, 2 * H * G])
        lself = sb("lself", [P, H * G])
        eself = sb("eself", [P, H * G])
        cin = sb("cin", [H * G, 2])
        cw = sb("cw", [1, H * G])
        dw = sb("dw", [1, H * G])
        co = sb("co", [1, H * G])
        do = sb("do", [1, H * G])
        rlast = sb("rlast", [1, GB])
        nxt = sb("nxt", [1, H])
        sm4 = sb("sm4", [1, 4 * H + 1])
        lf = sb("lf", [1, H])
        resc = sb("resc", [P, H])
        es = sb("es", [P, NT * H])
        rs = sb("rs", [P, NT * H])

        main = [ctx.enter_context(nc.psum_tensor(f"main{i}", [P, 512], F32)) for i in range(4)]
        pso = [ctx.enter_context(nc.psum_tensor(f"pso{i}", [P, 512], F32)) for i in range(2)]
        psad = ctx.enter_context(nc.psum_tensor("psad", [P, 512], F32))
        psb = ctx.enter_context(nc.psum_tensor("psb", [P, 512], F32))

        ring3 = ring[:, :].rearrange("p (s w) -> p s w", w=AW)
        acc3 = acc[:, :].rearrange("p (t w) -> p t w", w=AW)
        xr = ring[:, 0:NT * C].rearrange("p (t c) -> p t c", c=C)
        xa = acc[:, 0:NT * C].rearrange("p (t c) -> p t c", c=C)
        x1_in = oh[:, 0:XB * TB * C].rearrange("p (b t c) -> p b t c", b=XB, c=C)
        stat3 = stat[:, :].rearrange("p (t k) -> p t k", k=2)
        tv3 = tv[:, :].rearrange("p (t k) -> p t k", k=2 * H)
        es3 = es[:, :].rearrange("p (t h) -> p t h", h=H)
        rs3 = rs[:, :].rearrange("p (t h) -> p t h", h=H)
        ad3 = ad[:, :].rearrange("p (b g k) -> p b g k", b=2, k=LW)

        def hg(ap):
            return ap.rearrange("p (h g) -> p h g", h=H)

        def logits_of(b):
            return (ad3[:, b % 2, :, 0:H].rearrange("p g h -> p h g"), ad3[:, b % 2, :, H:2 * H].rearrange("p g h -> p h g"))

        def slot(b):
            return ring3[:, b * G:(b + 1) * G, :]

        lin = ring[:, 0:EC].bitcast(I32)
        lo_i = ring[:, EC:2 * EC].bitcast(I32)
        hi_i = ring[:, 2 * EC:3 * EC].bitcast(I32)
        lo_b = ring[:, 3 * EC:3 * EC + EC // 2].bitcast(BF16)
        hi_b = ring[:, 3 * EC + EC // 2:4 * EC].bitcast(BF16)
        dlin = ring[:, 4 * EC:5 * EC].bitcast(I32)
        dlin_f = ring[:, 5 * EC:6 * EC]
        sgn = ring[:, 6 * EC:7 * EC]
        o_lo, o_hi = 7 * EC, 7 * EC + HB * P
        oh_lo = ring[:, o_lo:o_hi].bitcast(BF16).rearrange("p (b k n) -> p b k n", b=2, n=P)
        oh_hi = ring[:, o_hi:o_hi + HB * NT].bitcast(BF16).rearrange("p (b k n) -> p b k n", b=2, n=NT)
        o_c = o_hi + HB * NT
        iota_b = ring[:, o_c:o_c + P // 2].bitcast(BF16)
        zero_b = ring[:, o_c + P // 2:o_c + P].bitcast(BF16)
        o_c += P
        thr = ring[:, o_c:o_c + NT]
        cnt = ring[:, o_c + NT:o_c + 2 * NT]
        bf = ring[:, o_c + 2 * NT:o_c + 3 * NT]
        bi = ring[:, o_c + 3 * NT:o_c + 4 * NT].bitcast(I32)
        fl = ring[:, o_c + 4 * NT:o_c + 5 * NT].bitcast(I32)
        ce = ring[:, o_c + 5 * NT:o_c + 6 * NT].bitcast(I32)
        ov = ring[:, o_c + 6 * NT:o_c + 7 * NT]
        pre = ring[:, o_c + 7 * NT:o_c + 8 * NT]
        cum = ring[:, o_c + 8 * NT:o_c + 9 * NT]
        zt = ring[:, o_c + 9 * NT:o_c + 10 * NT]
        o_c += 10 * NT
        sid = ring[:, o_c:o_c + SB]
        ts = ring[:, o_c + SB:o_c + 2 * SB]
        cs = ring[:, o_c + 2 * SB:o_c + 3 * SB]
        ci = ring[:, o_c + 3 * SB:o_c + 4 * SB].bitcast(I32)
        tsc = ring[:, o_c + 4 * SB:o_c + 5 * SB]
        t128 = ring[:, o_c + 5 * SB:o_c + 6 * SB]
        sany = ring[:, o_c + 6 * SB:o_c + 7 * SB]
        eany = ring[:, o_c + 7 * SB:o_c + 8 * SB]
        padi = ring[0:1, o_c + 8 * SB:o_c + 8 * SB + P].bitcast(I32)
        strayf = ring[0:1, o_c + 8 * SB + P:o_c + 8 * SB + P + 2]
        o_c += 8 * SB + P + 2
        assert o_c <= RING * AW
        srow = oh[:, 0:SX].bitcast(I32)
        drow = oh[:, SX:2 * SX].bitcast(I32)
        key = oh[:, 2 * SX:2 * SX + SB * (P + 2)].rearrange("p (b e) -> p b e", e=P + 2)
        o_k = 2 * SX + SB * (P + 2)
        srowf = oh[:, o_k:o_k + SX]
        dl = oh[:, o_k + SX:o_k + 2 * SX]
        sfr = oh[:, o_k + 2 * SX:o_k + 3 * SX]
        assert o_k + 3 * SX <= RING * P
        efr = ohT_room[:, :]
        cmpt = dloc[:, 0:SB * NT].rearrange("p (b t) -> p b t", t=NT)
        cmpo = endt[:, 0:SB * NT].rearrange("p (b t) -> p b t", t=NT)
        trow = sb("trow", [1, SX])
        tsum = sb("tsum", [1, SX // 4])

        def b3(ap):
            return ap.rearrange("p (b e) -> p b e", e=P)

        def bc(ap, shape):
            return ap.to_broadcast(shape)

        edges_in = sem("edges_in")
        pads_set = sem("pads_set")
        pads_out = sem("pads_out")
        lin_in = sem("lin_in")
        x_in = sem("x_in")
        consts = sem("consts")
        pool_chain = sem("pool_chain")
        dve_chain = sem("dve_chain")
        act_chain = sem("act_chain")
        hist_onehots = sem("hist_onehots")
        hist_done = sem("hist_done")
        dlin_ready = sem("dlin_ready")
        counts_ready = sem("counts_ready")
        counts_sum = sem("counts_sum")
        chunks_ready = sem("chunks_ready")
        rows_in = sem("rows_in")
        rowsf_ready = sem("rowsf_ready")
        rowsT_done = sem("rowsT_done")
        rowsT_read = sem("rowsT_read")
        key_out = sem("key_out")
        key_edge = sem("key_edge")
        flags_ready = sem("flags_ready")
        flags_out = sem("flags_out")
        tiles_out = sem("tiles_out")
        tiles_in = sem("tiles_in")
        steps_ready = sem("steps_ready")
        norm_in = sem("norm_in")
        norm_sq = sem("norm_sq")
        norm_ready = sem("norm_ready")
        ln_rows = sem("ln_rows")
        acc_clear = sem("acc_clear")
        table_stored = sem("table_stored")
        gathered = [sem(f"gathered{j}") for j in range(U)]
        idx_in = [sem(f"idx_in{j}") for j in range(GB)]
        group_in = [sem(f"group_in{j}") for j in range(GB)]
        onehots = sem("onehots")
        quads_ready = sem("quads_ready")
        parts_ready = sem("parts_ready")
        squares_ready = sem("squares_ready")
        products_done = sem("products_done")
        added = sem("added")
        w_in = sem("w_in")
        wcat_ready = sem("wcat_ready")
        nb_ready = sem("nb_ready")
        rows_T = sem("rows_T")
        rows_T_copied = sem("rows_T_copied")
        projected = sem("projected")
        proj_read = sem("proj_read")
        staged = sem("staged")
        mid_ready = sem("mid_ready")
        back_in = sem("back_in")
        x1_back = sem("x1_back")
        rest_in = sem("rest_in")
        stored = sem("stored")
        ohT_done = sem("ohT_done")
        ohT_copied = sem("ohT_copied")
        logits_done = sem("logits_done")
        ad_ready = sem("ad_ready")
        flags_in = [sem(f"flags_in{j}") for j in range(GB)]
        v_ready = sem("v_ready")
        vT_done = sem("vT_done")
        scan_ready = sem("scan_ready")
        ends_done = sem("ends_done")
        carry_ready = sem("carry_ready")
        carry_done = sem("carry_done")
        max_ready = sem("max_ready")
        maxT_done = sem("maxT_done")
        expo_ready = sem("expo_ready")
        lf_done = sem("lf_done")
        e_ready = sem("e_ready")
        factor_ready = sem("factor_ready")
        weighted_v = sem("weighted_v")
        weighted_a = sem("weighted_a")
        self_ready = sem("self_ready")
        nself = sem("nself")

        def tile_number(value):
            return nc.s_assert_within(value, 0, NT - 1, skip_runtime_bounds_check_because="clamped on the chip before it is packed")

        ONES_COL = C
        FLAG_INCS = 16 * (2 * H + 3)
        LEAD = 3
        MARKS = GB * 26
        HALF = 2 * P

        def oh_base(k):
            return k * (S + AHEAD)

        QT = (NG + 2) * Q + 2
        QL = QT + 1
        TURN_AT = (2, 6, 10, 13)
        LOGITS_AT = [max(j // 2, j - 3) for j in range(G)]

        def staged_rows(i, j, width, first=0):
            return oh[:, bass.ds((i & 1) * TB * AW + (j * AW + first), width)]

        def rows_of(tab, i, width):
            return tab.rearrange("(t p) c -> p t c", p=P)[:, bass.ds(i * TB, TB), 0:width]

        block = ctx.enter_context(nc.Block())

        @block.sync
        def _(sp):
            sp.dma_start(src_pad.rearrange("a b -> (a b)")[0:E].rearrange("(k f) -> k f", k=16),
                         src.rearrange("(k f) -> k f", k=16)).then_inc(edges_in, 16)
            sp.dma_start(dst_pad.rearrange("a b -> (a b)")[0:E].rearrange("(k f) -> k f", k=16),
                         dst.rearrange("(k f) -> k f", k=16)).then_inc(edges_in, 16)
            for q in range(7):
                sp.dma_start(xa[:, q * TB:min((q + 1) * TB, NFULL), :],
                             x[q * TB * P:min((q + 1) * TB, NFULL) * P, :].rearrange("(t p) c -> p t c", p=P)
                             ).then_inc(x_in, 16)
            sp.wait_ge(pads_set, 2)
            sp.dma_start(xa[0:NREST, NFULL, :], x[NFULL * P:N, :]).then_inc(x_in, 16)
            sp.dma_start(src_pad[EC - 1:EC, P - EPAD:P], padi[0:1, 0:EPAD]).then_inc(pads_out, 16)
            sp.dma_start(dst_pad[EC - 1:EC, P - EPAD:P], padi[0:1, 0:EPAD]).then_inc(pads_out, 16)
            sp.dma_start(keys[0:1, 0:1], strayf[0:1, 0:1]).then_inc(pads_out, 16)
            sp.dma_start(keys[0:1, SX * P + 1:SX * P + 2], strayf[0:1, 1:2]).then_inc(pads_out, 16)
            sp.wait_ge(edges_in, 32)
            sp.wait_ge(pads_out, 64)
            sp.dma_start(lin, src_pad.rearrange("a b -> (a b)").rearrange("(p f) -> p f", p=P)).then_inc(lin_in, 16)
            sp.wait_ge(lin_in, 16)
            sp.dma_start(dlin, dst_pad.rearrange("a b -> (a b)").rearrange("(p f) -> p f", p=P)).then_inc(lin_in, 16)

            sp.wait_ge(chunks_ready, 2)
            sp.dma_start(keys[0:1, 1:1 + SX * P].rearrange("o (b p e) -> (o p) b e", p=P, e=P),
                         key[:, :, 1:P + 1]).then_inc(key_out, 16)
            with nc.allow_non_contiguous_dma(reason="one element of each step"):
                sp.dma_start(tile_of.rearrange("o (b p) -> (o p) b", p=P), tsc).then_inc(tiles_out, 16)
                sp.wait_ge(key_out, 16)
                kv = keys[0:1, 0:SX * P].rearrange("o (b p e) -> (o p) b e", p=P, e=P)
                sp.dma_start(key[:, :, 0:1], kv[:, :, 0:1]).then_inc(key_edge, 16)
                kn = keys[0:1, 2:SX * P + 2].rearrange("o (b p e) -> (o p) b e", p=P, e=P)
                sp.dma_start(key[:, :, P + 1:P + 2], kn[:, :, P - 1:P]).then_inc(key_edge, 16)
                sp.wait_ge(tiles_out, 16)
                sp.dma_start(trow[0:1, :], tile_of).then_inc(tiles_in, 16)
                sp.wait_ge(flags_ready, 1)
                sp.dma_start(start_rows.rearrange("(b p) e -> p b e", p=P), b3(sfr)).then_inc(flags_out, 16)
                sp.dma_start(end_rows.rearrange("(b p) e -> p b e", p=P), b3(efr)).then_inc(flags_out, 16)
                sp.dma_start(start_any.rearrange("o (b p) -> (o p) b", p=P), sany).then_inc(flags_out, 16)
                sp.dma_start(end_any.rearrange("o (b p) -> (o p) b", p=P), eany).then_inc(flags_out, 16)

            for q in range(NI):
                sp.wait_ge(ln_rows, TB * (q + 1))
                sp.dma_start(conv_tab[0].rearrange("(t p) c -> p t c", p=P)[:, q * TB:(q + 1) * TB, :],
                             xa[:, q * TB:(q + 1) * TB, :]).then_inc(table_stored, 16)

            def store_stage(table, width, m, before):
                with nc.sync.Fori(0, NI) as i:
                    sp.wait_ge(staged, 2 + m * NT + i * TB + TB)
                    sp.wait_ge(table_stored, 16 * NI * before + i * 16)
                    rows = oh[:, bass.ds((i & 1) * TB * AW, TB * AW)].rearrange("p (t w) -> p t w", w=AW)
                    sp.dma_start(rows_of(table, i, width), rows[:, :, 0:width]).then_inc(table_stored, 16)

            def fetch_idx(b, col, width):
                sp.dma_start(idx[:, b * G:b * G + width], sidx[:, bass.ds(col, width)]).then_inc(idx_in[b], 16)

            for k in range(HOPS):
                if k:
                    sp.wait_ge(staged, 2 + k * NT)
                sp.dma_start(wc[:, :].rearrange("p (b n) -> p b n", b=2),
                             gw[k].rearrange("(b p) n -> p b n", p=P)).then_inc(w_in, 16)
                sp.dma_start(bias[:, :], gb[k:k + 1, :].to_broadcast([P, C])).then_inc(w_in, 16)
                if k == 0:
                    sp.wait_ge(steps_ready, 1)
                with nc.sync.Fori(0, S // U) as i:
                    for b in range(2):
                        sp.wait_ge(products_done, k * S + i * U + (b + 1) * UH)
                        fetch_idx(b, i * U + b * UH, UH)
                if k < HOPS - 1:
                    store_stage(conv_tab[k + 1], C, k, k + 1)
                else:
                    sp.wait_ge(added, 4 + HOPS * S)
                    for q in range(NI):
                        a, b = q * TB, min((q + 1) * TB, NFULL)
                        sp.dma_start(xr[:, a:b, :], x[a * P:b * P, :].rearrange("(t p) c -> p t c", p=P)
                                     ).then_inc(back_in, 16)
                        if q == 0:
                            sp.dma_start(xr[0:NREST, NFULL, :], x[NFULL * P:N, :]).then_inc(rest_in, 16)
                        sp.wait_ge(back_in, 16 * (q + 1))
                    with nc.sync.Fori(0, NI) as i:
                        sp.wait_ge(mid_ready, i * TB + TB)
                        sp.dma_start(rows_of(x1_tab, i, C), acc3[:, bass.ds(i * TB, TB), 0:C]).then_inc(stored, 16)

            def load_weights(l):
                w, s_, d_ = ((w1, as1, ad1), (w2, as2, ad2))[l]
                if l:
                    sp.wait_ge(projected, 2 + (HOPS + l) * NT)
                    sp.wait_ge(wcat_ready, l)
                sp.dma_start(wcat[:, :].rearrange("p (b n) -> p b n", b=2)[:, :, 0:C],
                             w.rearrange("(b p) n -> p b n", p=P)).then_inc(w_in, 16)
                sp.dma_start(att[:, 0:C], s_.rearrange("o h c -> o (h c)").to_broadcast([P, C])).then_inc(w_in, 16)
                sp.dma_start(att[:, C:2 * C], d_.rearrange("o h c -> o (h c)").to_broadcast([P, C])).then_inc(w_in, 16)

            load_weights(0)
            for l in range(LAYERS):
                store_stage(attn_tab[l], TW, HOPS - 1 + l, HOPS + l)
                sp.wait_ge(mid_ready, (l + 1) * NT)
                sp.dma_start(bias[:, :], (b1, b2)[l].rearrange("(o c) -> o c", o=1).to_broadcast([P, C])).then_inc(w_in, 16)
                if l == 0:
                    sp.wait_ge(flags_out, 64)
                def fetch_group(it, b, last=False):
                    sp.wait_ge(expo_ready, it * GB + (l * (NG + 1) + b + 1))
                    g0 = (it * GB + b) * G
                    if not last:
                        fetch_idx(b, g0, G)
                    for h in range(H):
                        sp.dma_start(sfl[h * G:(h + 1) * G, b * P:(b + 1) * P],
                                     start_rows[bass.ds(g0, G), :]).then_inc(flags_in[b], 16)
                        sp.dma_start(efl[h * G:(h + 1) * G, b * P:(b + 1) * P],
                                     end_rows[bass.ds(g0, G), :]).then_inc(flags_in[b], 16)
                    o = b * H * G
                    for to, of, at in ((hg(rsf[0:1, o:o + H * G])[:, :, 1:G], start_any, g0),
                                       (hg(ref[0:1, o:o + H * G])[:, :, 0:G - 1], end_any, g0 + 1)):
                        sp.dma_start(to, of[0:1, bass.ds(at, G - 1)].rearrange("o (h g) -> o h g", h=1)
                                     .to_broadcast([1, H, G - 1])).then_inc(flags_in[b], 16)
                    sp.dma_start(rlast[0:1, b:b + 1], start_any[0:1, bass.ds(g0 + G - 1, 1)]).then_inc(flags_in[b], 16)

                with nc.sync.Fori(0, NG // GB) as it:
                    for b in range(GB):
                        fetch_group(it, b)
                fetch_group(NG // GB, 0, last=True)
                if l < LAYERS - 1:
                    load_weights(l + 1)
                sp.wait_ge(added, 4 + (HOPS + l + 1) * S)
                sp.wait_ge(e_ready, 2 * (l + 1) * (NG + 1))
                sp.wait_ge(weighted_v, (l + 1) * (S + LEAD))

                def rows_back(q):
                    sp.dma_start(xr[:, q * TB:(q + 1) * TB, :],
                                 attn_tab[l].rearrange("(t p) c -> p t c", p=P)[:, q * TB:(q + 1) * TB, 0:C]
                                 ).then_inc(back_in, 16)

                if l < LAYERS - 1:
                    for q in range(NI):
                        rows_back(q)
                        sp.wait_ge(back_in, 16 * (NI + l * NI + q + 1))
            sp.wait_ge(quads_ready, LAYERS * QL)
            sp.wait_ge(ohT_done, LAYERS * QT)
            sp.wait_ge(lf_done, LAYERS * (NG + 1))

            def store_result(q):
                a, b = q * TB, min((q + 1) * TB, NFULL)
                sp.wait_ge(mid_ready, 2 * NT + 2 * TB * (q + 1))
                sp.dma_start(out[a * P:b * P, :].rearrange("(t p) c -> p t c", p=P), acc3[:, a:b, 0:C]
                             ).then_inc(stored, 16)

            for q in range(NI):
                if q >= XB:
                    store_result(q - XB)
                rows_back(q)
                sp.dma_start(x1_in[:, q % XB, :, :],
                             x1_tab.rearrange("(t p) c -> p t c", p=P)[:, q * TB:(q + 1) * TB, :]
                             ).then_inc(x1_back, 16)
                sp.wait_ge(back_in, 16 * (LAYERS * NI + q + 1))
                sp.wait_ge(x1_back, 16 * (q + 1))
            for q in range(NI - XB, NI):
                store_result(q)
            sp.dma_start(out[NFULL * P:N, :], acc3[0:NREST, NFULL, 0:C]).then_inc(stored, 16)
            sp.wait_ge(stored, 16 * (2 * NI + 1))
            sp.wait_ge(table_stored, 16 * NI * (HOPS + LAYERS))

        @block.gpsimd
        def _(pool):
            chain = [0]

            def link(ins):
                chain[0] += 1
                ins.then_inc(pool_chain, 1)
                pool.wait_ge(pool_chain, chain[0])

            nc.gpsimd.memset(padi, OUTSIDE).then_inc(pads_set, 1)
            link(nc.gpsimd.memset(strayf, -5.0))
            nc.gpsimd.memset(xa[:, NFULL, :], 0.0).then_inc(pads_set, 1)
            link(nc.gpsimd.memset(ident[:, :], 0.0))
            link(nc.gpsimd.affine_select(out=ident[:, :], in_=ident[:, :], compare_op=ALU.not_equal, fill=1.0,
                                         base=0, pattern=[[-1, P]], channel_multiplier=1))
            link(nc.gpsimd.memset(ones[:, :], 1.0))
            link(nc.gpsimd.memset(zt, 0.0))
            link(nc.gpsimd.memset(zrow[:, :], 0.0))
            link(nc.gpsimd.iota(iota[:, :], pattern=[[1, P]], base=0, channel_multiplier=0,
                                allow_small_or_imprecise_dtypes=True))
            link(nc.gpsimd.iota(iota_b, pattern=[[1, P]], base=0, channel_multiplier=0,
                                allow_small_or_imprecise_dtypes=True))
            link(nc.gpsimd.iota(thr, pattern=[[P, NT]], base=P, channel_multiplier=0,
                                allow_small_or_imprecise_dtypes=True))
            link(nc.gpsimd.iota(sid, pattern=[[P, SB]], base=0, channel_multiplier=1,
                                allow_small_or_imprecise_dtypes=True))
            nc.gpsimd.memset(zero_b, 0.0).then_inc(consts, 1)

            pool.wait_ge(chunks_ready, 1)
            pool.wait_ge(lin_in, 32)
            for b in range(SB):
                for row, tab in ((srow, src_pad), (drow, dst_pad)):
                    pool.indirect_dma_start(b3(row)[:, b, :], None, tab,
                                            bass.IndirectOffsetOnAxis(ap=ci[:, b:b + 1], axis=0)
                                            ).then_inc(rows_in, 16)

            def clear_first():
                pool.wait_ge(table_stored, 16 * NI)
                with nc.gpsimd.Fori(0, NT) as i:
                    pool.nop(nofuse=True)
                    nc.gpsimd.tensor_copy(acc[:, bass.ds(i * AW, AW)], zrow[:, :]).then_inc(acc_clear, 1)

            def clear(m):
                with nc.gpsimd.Fori(0, NT) as i:
                    pool.wait_ge(nb_ready, m * NT + i + 1)
                    pool.nop(nofuse=True)
                    nc.gpsimd.tensor_copy(acc[:, bass.ds(i * AW, AW)], zrow[:, :]).then_inc(acc_clear, 1)

            def gather_conv(k):
                pool.wait_ge(table_stored, 16 * NI * (k + 1))
                with nc.gpsimd.Fori(0, S // U) as i:
                    for j in range(U):
                        if j % UH == 0:
                            pool.wait_ge(idx_in[j // UH], 16 * k * (S // U) + i * 16 + 16)
                        pool.wait_ge(products_done, k * S + i * U + j + 1)
                        pool.nop(nofuse=True)
                        pool.indirect_dma_start(ring3[:, j, 0:C], None, conv_tab[k],
                                                bass.IndirectOffsetOnAxis(ap=idx[:, (j // UH) * G + j % UH:(j // UH) * G + j % UH + 1], axis=0)
                                                ).then_inc(gathered[j], 16)

            def gather_attn(l):
                pool.wait_ge(table_stored, 16 * NI * (HOPS + l + 1))
                with nc.gpsimd.Fori(0, NG // GB) as i:
                    for j in range(GB * G):
                        if j % G == 0:
                            n = (HOPS * (S // U) if j < U else 0) + l * (NG // GB)
                            pool.wait_ge(idx_in[j // G], 16 * n + i * 16 + 16)
                        pool.wait_ge(products_done, CR + (HOPS + l) * S + i * GB * G + j + 1 - GB * G)
                        pool.nop(nofuse=True)
                        pool.indirect_dma_start(ring3[:, j, 0:TW], None, attn_tab[l],
                                                bass.IndirectOffsetOnAxis(ap=idx[:, j:j + 1], axis=0)
                                                ).then_inc(group_in[j // G], 16)

            clear_first()
            pool.wait_ge(steps_ready, 1)
            link(nc.gpsimd.memset(xr[:, NFULL, :], 0.0))
            nc.gpsimd.memset(ring3[:, 0:U, ONES_COL:ONES_COL + 1], 1.0).then_inc(steps_ready, 1)
            for k in range(HOPS):
                gather_conv(k)
                if k == 0:
                    pool.wait_ge(norm_in, 3)
                if k < HOPS - 1:
                    clear(k)
            pool.wait_ge(stored, 16 * NI)
            clear(HOPS)
            for l in range(LAYERS):
                gather_attn(l)
                pool.wait_ge(nself, l + 1)
                with nc.gpsimd.Fori(0, NI) as i:
                    pool.wait_ge(back_in, 16 * (NI + l * NI) + i * 16 + 16)
                    for j in range(TB):
                        r4 = ring[:, bass.ds((i * TB + j) * C, C)].rearrange("p (h c) -> p h c", h=H)
                        e4 = es[:, bass.ds((i * TB + j) * H, H)].rearrange("p (h o) -> p h o", o=1).to_broadcast([P, H, CH])
                        nc.gpsimd.tensor_tensor(r4, r4, e4, ALU.mult).then_inc(self_ready, 1)
                if l < LAYERS - 1:
                    clear(HOPS + 1)

        @block.scalar
        def _(act):
            chain = [0]

            def link(ins):
                chain[0] += 1
                ins.then_inc(act_chain, 1)
                act.wait_ge(act_chain, chain[0])

            act.wait_ge(consts, 1)
            nc.scalar.copy(t1[:, 1:2], ones[:, 0:1]).then_inc(staged, 2)
            act.wait_ge(dlin_ready, 1)
            for t in range(NT):
                link(nc.scalar.activation(sgn, dlin_f, ACT.Sign, scale=-1.0, bias=thr[:, t:t + 1],
                                          accum_out=cnt[:, t:t + 1]))
            nc.scalar.copy(t1[:, 0:1], cnt[:, 0:1]).then_inc(counts_ready, 1)

            def root(dst_, n):
                act.wait_ge(norm_in, n)
                nc.scalar.activation(dst_, dst_, ACT.Sqrt).then_inc(norm_sq, 1)

            root(rstd[:, :], 1)
            root(onorm[:, :], 2)
            act.wait_ge(norm_ready, 1)
            for t in range(NT):
                nc.scalar.activation(xa[:, t, :], xa[:, t, :], ACT.Relu, scale=rstd[:, t:t + 1],
                                     bias=nbias[:, t:t + 1]).then_inc(ln_rows, 1)

            def feed_sums(k, t, j):
                act.wait_ge(rows_T, CR + k * NT + t + (0 if j == 0 else -1))
                nc.scalar.activation(nb[:, (j % 2) * C:(j % 2 + 1) * C], acc[:, bass.ds(t * AW, C)], ACT.Copy
                                     ).then_inc(nb_ready, 1)

            for k in range(HOPS - 1):
                if k == 0:
                    root(inorm[:, :], 3)

                def tiles(i, last):
                    act.wait_ge(table_stored, i * 16 + (16 * (NI * (k + 1)) - 16))
                    for j in range(TB):
                        if not (last and j + 2 >= TB):
                            feed_sums(k, i * TB + j + 2, (j + 2) % TB)
                        act.wait_ge(proj_read, 2 + k * NT + i * TB + j + 1)
                        nc.scalar.activation(staged_rows(i, j, C), tmp[:, (j % 2) * C:(j % 2 + 1) * C], ACT.Relu,
                                             scale=onorm[:, bass.ds(i * TB + j, 1)]).then_inc(staged, 1)

                act.wait_ge(added, 4 + (k + 1) * S)
                for j in range(2):
                    feed_sums(k, j, j)
                with nc.scalar.Fori(0, NI - 1) as i:
                    tiles(i, False)
                tiles(NI - 1, True)
            act.wait_ge(added, 4 + HOPS * S)
            with nc.scalar.Fori(0, NI) as i:
                for j in range(TB):
                    feed_sums(HOPS - 1, i * TB + j, j)
            root(rstd[:, :], 4)
            act.wait_ge(norm_ready, 2)
            def feed(m, ready, scaled):
                with nc.scalar.Fori(0, NI) as i:
                    for j in range(TB):
                        t = i * TB + j
                        act.wait_ge(ready[0], ready[1] + t + 1)
                        act.wait_ge(rows_T, CR + m * NT + t + (0 if j == 0 else -1))
                        to, a = nb[:, (j % 2) * C:(j % 2 + 1) * C], acc[:, bass.ds(t * AW, C)]
                        if scaled:
                            nc.scalar.activation(to, a, ACT.Relu, scale=rstd[:, bass.ds(t, 1)],
                                                 bias=nbias[:, bass.ds(t, 1)]).then_inc(nb_ready, 1)
                        else:
                            nc.scalar.activation(to, a, ACT.Relu).then_inc(nb_ready, 1)

            feed(HOPS, (mid_ready, 0), True)

            for l in range(LAYERS):
                def copy_quad(n, qq):
                    act.wait_ge(ohT_done, n + (l * QT + 1))
                    act.wait_ge(logits_done, n + (l * (NG + 2) * Q + 1))
                    nc.scalar.copy(ohT[:, (qq % 2) * 4 * P:(qq % 2 + 1) * 4 * P], pso[qq % 2][:, :]
                                   ).then_inc(ohT_copied, 1)

                def copy_logits(g, b):
                    act.wait_ge(logits_done, g * Q + (2 + qb + Q))
                    nc.scalar.copy(ad[:, b % 2 * LW * G:(b % 2 + 1) * LW * G], psad[:, 0:LW * G]
                                   ).then_inc(ad_ready, 1)

                def square_quad(col, at):
                    for k in range(4):
                        sq = nc.scalar.activation(oh[:, (at + k) * P:(at + k + 1) * P], iota[:, :], ACT.Square,
                                                  scale=-1.0, bias=dloc[:, col(k)])
                    sq.then_inc(squares_ready, 1)

                def onehot_quad(at, c):
                    act.wait_ge(squares_ready, c)
                    o4 = oh[:, at * P:(at + 4) * P]
                    nc.scalar.activation(o4, o4, ACT.Relu, scale=-1.0, bias=ones[:, 0:1]).then_inc(quads_ready, 1)

                def exponentials(g, b):
                    act.wait_ge(expo_ready, g + (GB + l * (NG + 1) + 1))
                    nc.scalar.activation(slot(b)[:, :, C:C + H].rearrange("p g h -> p h g"),
                                         hg(dd[:, 0:H * G]), ACT.Exp).then_inc(e_ready, 1)
                    nc.scalar.activation(eself[:, :], dd[:, H * G:2 * H * G], ACT.Exp).then_inc(e_ready, 1)
                    act.wait_ge(lf_done, g + (l * (NG + 1) + 1))
                    nc.scalar.activation(resc[:, :], psb[:, HALF + 4:HALF + 4 + H], ACT.Exp).then_inc(factor_ready, 1)

                def weigh(b, k):
                    for h in range(DVEC // CH, H):
                        r = ring3[:, b * G + k, h * CH:(h + 1) * CH]
                        nc.scalar.activation(r, r, ACT.Copy, scale=ring3[:, b * G + k, C + h:C + h + 1]
                                             ).then_inc(weighted_a, 1)

                act.wait_ge(table_stored, 16 * NI * (HOPS + l + 1))
                act.wait_ge(proj_read, 2 + (HOPS + l + 1) * NT)
                qb = l * (NG + 2) * Q
                for q in range(2 * Q + 3):
                    square_quad(lambda k: slice(4 * q + k, 4 * q + k + 1), 4 * q)
                    onehot_quad(4 * q, l * QL + q + 1)
                    if q:
                        copy_quad(q - 1, q - 1)
                    if q == Q:
                        copy_logits(0, 0)
                copy_logits(1, 1)
                exponentials(0, 0)
                with nc.scalar.Fori(0, NG // GB) as it:
                    for b in range(GB):
                        g = it * GB + b
                        act.wait_ge(e_ready, it * GB * 2 + 2 * (l * (NG + 1) + b + 1))
                        for k in range(LEAD - 1):
                            weigh(b, k)
                        for k in range(G):
                            if k + LEAD - 1 < G:
                                weigh(b, k + LEAD - 1)
                            at = (b + 2) * G + 4 * (k // 4 + 3)
                            if k % 4 == 0:
                                square_quad(lambda k: bass.ds(it * GB * G + at + k, 1), at % RING)
                            if k % 4 == 1:
                                onehot_quad(at % RING, it * GB * Q + (l * QL + at // 4 + 1))
                            if k == G - 2:
                                exponentials(g + 1, (b + 1) % GB)
                            if k - 1 in TURN_AT:
                                q = TURN_AT.index(k - 1) + 2
                                copy_quad(it * GB * Q + (b + 2) * Q + q, q)
                        copy_logits(g + 2, b)
                if l < LAYERS - 1:
                    feed(HOPS + 1, (mid_ready, NT), False)

        @block.tensor
        def _(pe):
            pe.wait_ge(consts, 1)
            nc.tensor.matmul(psad[:, 0:NT], zero_b, zero_b[:, 0:NT], start=True, stop=False,
                             skip_group_check=True).then_inc(products_done, CR)
            nc.tensor.matmul(psb[:, 0:2], ident[:, :], ident[:, 0:2], start=True, stop=True).then_inc(hist_done, 2)
            nc.tensor.matmul(psb[:, 0:2], ident[:, :], ident[:, 0:2], start=True, stop=True).then_inc(rows_T, CR)
            nc.tensor.matmul(psb[:, 0:2], ident[:, :], ident[:, 0:2], start=True, stop=True).then_inc(logits_done, 2)
            nc.tensor.matmul(psb[:, 0:2], ident[:, :], ident[:, 0:2], start=True, stop=True).then_inc(projected, 2)
            def hist(first, end):
                with nc.tensor.Fori(first, end) as i:
                    for b in range(2):
                        pe.wait_ge(hist_onehots, 2 * i + b + 1)
                        for j in range(HB):
                            mm = nc.tensor.matmul(psad[:, 0:NT], oh_lo[:, b, j, :], oh_hi[:, b, j, :], start=False,
                                                  stop=False, skip_group_check=True)
                        mm.then_inc(hist_done, 1)

            hist(0, NH // 2)
            pe.wait_ge(counts_ready, 1)
            nc.tensor.matmul(main[0][:, 0:NT], ones[:, :], cnt, start=True, stop=True).then_inc(counts_sum, 1)
            hist(NH // 2, NH)
            nc.tensor.matmul(psad[:, 0:NT], zero_b, zero_b[:, 0:NT], start=False, stop=True,
                             skip_group_check=True).then_inc(hist_done, 1)
            n = 0
            for tabl, w in ((srowf, 1), (dl, 1), (efr, 2)):
                pe.wait_ge(rowsf_ready, w)
                for b in range(SB):
                    if n >= 4:
                        pe.wait_ge(rowsT_read, n - 3)
                    nc.tensor.transpose(main[n % 4][:, 0:P], b3(tabl)[:, b, :], ident[:, :]).then_inc(rowsT_done, 1)
                    n += 1

            def conv(k):
                with nc.tensor.Fori(0, S // U) as i:
                    for j in range(U):
                        pe.wait_ge(onehots, oh_base(k) + i * U + j + 1)
                        pe.wait_ge(added, k * S + i * U + j + 1)
                        pe.wait_ge(gathered[j], 16 * k * (S // U) + i * 16 + 16)
                        nc.tensor.matmul(main[j % 4][:, 0:C + 1], oh[:, (j % OHR) * P:(j % OHR + 1) * P],
                                         ring3[:, j, 0:C + 1], start=True, stop=True).then_inc(products_done, 1)

            def project(m, weights, width):
                def turn(i, j):
                    pe.wait_ge(nb_ready, m * NT + i * TB + j + 1)
                    pe.wait_ge(rows_T_copied, m * NT + i * TB + j + (2 if j == 0 else 1))
                    for b in range(2):
                        mm = nc.tensor.transpose(pso[j % 2][:, b * P:(b + 1) * P],
                                                 nb[:, (j % 2) * C + b * P:(j % 2) * C + (b + 1) * P], ident[:, :])
                    mm.then_inc(rows_T, 1)

                def multiply(i, j):
                    pe.wait_ge(rows_T_copied, m * NT + i * TB + j + 3)
                    pe.wait_ge(proj_read, m * NT + i * TB + j + (2 if j == 0 else 1))
                    for b in range(2):
                        mm = nc.tensor.matmul(main[j % 2][:, 0:width], aT[:, (j % 2) * C + b * P:(j % 2) * C + (b + 1) * P],
                                              weights[:, b * width:(b + 1) * width], start=b == 0, stop=b == 1)
                    mm.then_inc(projected, 1)

                with nc.tensor.Fori(0, NI) as i:
                    turn(i, 0)
                    for j in range(TB):
                        if j < TB - 1:
                            turn(i, j + 1)
                        multiply(i, j)

            for k in range(HOPS):
                conv(k)
                pe.wait_ge(added, 4 + (k + 1) * S)
                pe.wait_ge(w_in, 32 * (k + 1))
                project(k, wc, C)
            for l in range(LAYERS):
                pe.wait_ge(wcat_ready, l + 1)
                project(HOPS + l, wcat, PW)
                pe.wait_ge(parts_ready, l + 1)

                def turn_quad(n, q):
                    pe.wait_ge(quads_ready, n + (l * QL + q + 1))
                    pe.wait_ge(ohT_copied, n + (l * QT + q + 1))
                    for k in range(4):
                        at = (4 * q + k) % RING
                        mm = nc.tensor.transpose(pso[q % 2][:, k * P:(k + 1) * P],
                                                 oh[:, at * P:(at + 1) * P], ident[:, :])
                    mm.then_inc(ohT_done, 1)

                def tiles_of(g):
                    return nc.values_load_multi_w_load_instructions(
                        tpk[0:1, bass.ds(g * Q, Q)], engines=[mybir.EngineType.PE], min_val=0,
                        max_val=(1 << 24) - 1)[1]

                def logit_step(n, pk, j):
                    q, k = j // 4, j % 4
                    if k == 0:
                        pe.wait_ge(ohT_copied, n + (l * QT + q + 3))
                    t = tile_number((pk[q] >> (6 * k)) & 63)
                    mm = nc.tensor.matmul(psad[:, j * LW:(j + 1) * LW],
                                          ohT[:, ((q % 2) * 4 + k) * P:((q % 2) * 4 + k + 1) * P],
                                          tvb[:, bass.ds(t * LW, LW)], start=True, stop=True)
                    if k == 3:
                        mm.then_inc(logits_done, 1)

                def turn_logits(c):
                    pe.wait_ge(v_ready, c)
                    pe.nop(nofuse=True)
                    nc.tensor.transpose(psb[0:H * G, 0:P], v[:, :], ident[:, :]).then_inc(vT_done, 1)

                def turn_ends(c):
                    pe.wait_ge(scan_ready, c)
                    pe.nop(nofuse=True)
                    nc.tensor.transpose(psb[0:1, HALF:HALF + H * G], f1[:, P - 1:P], ident[0:H * G, 0:H * G])
                    nc.tensor.transpose(psb[0:1, HALF + H * G:HALF + 2 * H * G], r1[:, 0:1], ident[0:H * G, 0:H * G]
                                        ).then_inc(ends_done, 1)

                def turn_carries(c):
                    pe.wait_ge(carry_ready, c)
                    nc.tensor.matmul(psb[0:H * G, HALF:HALF + 1], co[0:1, :], ones[0:1, 0:1], start=True, stop=True)
                    nc.tensor.matmul(psb[0:H * G, HALF + 1:HALF + 2], do[0:1, :], ones[0:1, 0:1],
                                     start=True, stop=True).then_inc(carry_done, 1)

                def turn_maxima(c):
                    pe.wait_ge(max_ready, c)
                    pe.nop(nofuse=True)
                    nc.tensor.transpose(psb[:, P:P + H * G], mrow[:, :], ident[0:H * G, 0:H * G]).then_inc(maxT_done, 1)

                def spread_factor(c, b):
                    pe.wait_ge(expo_ready, GB + c)
                    nc.tensor.matmul(psb[:, HALF + 4:HALF + 4 + H], oh[0:1, b * G * P:b * G * P + P], lf[0:1, :],
                                     start=True, stop=True).then_inc(lf_done, 1)

                if l:
                    pe.wait_ge(ad_ready, l * (NG + 2))
                for g in range(2):
                    pk = tiles_of(g)
                    if g:
                        pe.wait_ge(ad_ready, l * (NG + 2) + 1)
                    for q in range(Q):
                        turn_quad(0, g * Q + q)
                        for j in range(4 * q, 4 * q + 4):
                            logit_step(g * Q, pk, j)
                turn_quad(0, 2 * Q)
                turn_quad(0, 2 * Q + 1)
                turn_logits(l * (NG + 1) + 1)
                turn_ends(l * (NG + 1) + 1)
                turn_carries(l * (NG + 1) + 1)
                turn_maxima(l * (NG + 1) + 1)
                spread_factor(l * (NG + 1) + 1, 0)
                with nc.tensor.Fori(0, NG // GB) as it:
                    for b in range(GB):
                        pk = tiles_of(it * GB + b + 2)
                        n = it * GB * Q
                        c = it * GB + (l * (NG + 1) + b + 2)
                        for k in range(G):
                            if k in TURN_AT:
                                turn_quad(n, (b + 2) * Q + TURN_AT.index(k) + 2)
                            s = (HOPS + l) * S + it * GB * G + b * G + k
                            pe.wait_ge(weighted_v, s + (LEAD * l - HOPS * S + 1))
                            pe.wait_ge(weighted_a, (s - HOPS * S + 1) * (H - DVEC // CH))
                            nc.tensor.matmul(main[k % 4][:, 0:AW], oh[:, (b * G + k) * P:(b * G + k + 1) * P],
                                             ring3[:, b * G + k, :], start=True, stop=True).then_inc(products_done, 1)
                            if k == 2:
                                turn_logits(c)
                            if k == 5:
                                turn_ends(c)
                            if k == 8:
                                turn_carries(c)
                            if k == 11:
                                turn_maxima(c)
                            if k == G - 2:
                                spread_factor(c, (b + 1) % GB)
                            if k == 0:
                                pe.wait_ge(ad_ready, c + l)
                            for j in range(G):
                                if LOGITS_AT[j] == k:
                                    logit_step(n + (b + 2) * Q, pk, j)

        @block.vector
        def _(dve):
            chain = [0]

            def link(ins):
                chain[0] += 1
                ins.then_inc(dve_chain, 1)
                dve.wait_ge(dve_chain, chain[0])

            link(nc.vector.memset(sm4[:, :], 0.0))
            nc.vector.memset(t2[:, :], 0.0).then_inc(added, 4)
            nc.vector.memset(f1[:, :], 0.0).then_inc(rows_T_copied, 2)
            nc.vector.memset(r1[:, :], 0.0).then_inc(proj_read, 2)
            nc.vector.memset(v[:, :], 0.0).then_inc(ohT_copied, 2)
            nc.vector.memset(alpha[:, :], 0.0).then_inc(expo_ready, GB)

            dve.wait_ge(lin_in, 16)
            link(nc.vector.tensor_scalar(hi_i, lin, 7, None, ALU.arith_shift_right))
            link(nc.vector.tensor_scalar(lo_i, lin, P - 1, None, ALU.bitwise_and))
            link(nc.vector.tensor_copy(hi_b, hi_i))
            link(nc.vector.tensor_copy(lo_b, lo_i))
            dve.wait_ge(consts, 1)
            dve.wait_ge(lin_in, 32)
            link(nc.vector.tensor_scalar(thr, thr, -0.5, None, ALU.add))
            nc.vector.tensor_copy(dlin_f, dlin).then_inc(dlin_ready, 1)

            def hist(a, b):
                with nc.vector.Fori(a, b) as i:
                    for c in range(2):
                        dve.wait_ge(hist_done, 2 * i + c + 1)
                        for to, of, n in ((oh_lo, lo_b, P), (oh_hi, hi_b, NT)):
                            mm = nc.vector.tensor_tensor(
                                to[:, c, :, :],
                                of[:, bass.ds((2 * i + c) * HB, HB)].rearrange("p (k o) -> p k o", o=1)
                                .to_broadcast([P, HB, n]),
                                iota_b[:, 0:n].rearrange("p (o n) -> p o n", o=1).to_broadcast([P, HB, n]),
                                ALU.is_equal)
                        mm.then_inc(hist_onehots, 1)

            hist(0, NH // 2)

            dve.wait_ge(counts_sum, 1)
            link(nc.vector.tensor_scalar(bf, main[0][:, 0:NT], float(EC * P), 0.5, ALU.add, ALU.mult))
            link(nc.vector.tensor_scalar(bf, bf, float(E), None, ALU.min))
            link(nc.vector.tensor_copy(bi, bf))
            link(nc.vector.tensor_scalar(fl, bi, 7, None, ALU.arith_shift_right))
            link(nc.vector.tensor_scalar(bi, bi, float(P - 1), None, ALU.add))
            link(nc.vector.tensor_scalar(ce, bi, 7, None, ALU.arith_shift_right))
            link(nc.vector.tensor_tensor(ov, ce, fl, ALU.subtract))
            link(nc.vector.tensor_tensor_scan(out=pre, data0=zt, data1=ov, initial=0.0, op0=ALU.add, op1=ALU.add))
            link(nc.vector.tensor_tensor(pre, pre, ov, ALU.subtract))
            link(nc.vector.tensor_tensor(cum, pre, ce, ALU.add))
            link(nc.vector.tensor_tensor(cmpt, sid.rearrange("p (b o) -> p b o", o=1).to_broadcast([P, SB, NT]),
                                         cum.rearrange("p (o t) -> p o t", o=1).to_broadcast([P, SB, NT]), ALU.is_ge))
            link(nc.vector.tensor_reduce(ts, cmpt, AX.X, ALU.add))
            link(nc.vector.tensor_tensor(cmpo, cmpt, ov.rearrange("p (o t) -> p o t", o=1).to_broadcast([P, SB, NT]),
                                         ALU.mult))
            link(nc.vector.tensor_reduce(cs, cmpo, AX.X, ALU.add))
            link(nc.vector.tensor_tensor(cs, sid, cs, ALU.subtract))
            link(nc.vector.tensor_scalar(cs, cs, float(EC - 1), 0.0, ALU.min, ALU.max))
            link(nc.vector.tensor_scalar(tsc, ts, float(NT - 1), None, ALU.min))
            link(nc.vector.tensor_scalar(t128, ts, float(P), None, ALU.mult))
            nc.vector.tensor_copy(ci, cs).then_inc(chunks_ready, 1)

            hist(NH // 2, NH)

            dve.wait_ge(rows_in, 16 * 2 * SB)
            tb = t128.rearrange("p (b o) -> p b o", o=1).to_broadcast([P, SB, P])
            link(nc.vector.tensor_tensor(b3(dl), b3(drow), tb, ALU.subtract))
            link(nc.vector.tensor_scalar(dl, dl, -1.0, float(P), ALU.max, ALU.min))
            link(nc.vector.tensor_tensor(key[:, :, 1:P + 1], b3(dl), tb, ALU.add))
            nc.vector.tensor_tensor(key[:, :, 1:P + 1], key[:, :, 1:P + 1], tb, ALU.add).then_inc(chunks_ready, 1)
            nc.vector.tensor_scalar(srowf, srow, float(N - 1), None, ALU.min).then_inc(rowsf_ready, 1)

            dve.wait_ge(hist_done, 2 * NH + 3)
            link(nc.vector.tensor_scalar(onorm[:, :], psad[:, 0:NT], 1.0, None, ALU.max))
            dve.wait_ge(x_in, 16 * 8)
            for t in range(NT):
                link(nc.vector.bn_stats(bnst[:, 0:6], xa[:, t, :]))
                link(nc.vector.bn_aggr(stat3[:, t, :], bnst[:, 0:6]))

            def row_scales(n, m):
                nc.vector.tensor_scalar(rstd[:, :], stat3[:, :, 1], EPS, None, ALU.add).then_inc(norm_in, 1)
                dve.wait_ge(norm_sq, n)
                link(nc.vector.reciprocal(rstd[:, :], rstd[:, :]))
                link(nc.vector.tensor_tensor(nbias[:, :], stat3[:, :, 0], rstd[:, :], ALU.mult))
                return nc.vector.tensor_scalar(nbias[:, :], nbias[:, :], -1.0, None, ALU.mult)

            link(row_scales(1, 1))
            nc.vector.tensor_copy(onorm[:, :], onorm[:, :]).then_inc(norm_in, 1)
            dve.wait_ge(norm_sq, 2)
            link(nc.vector.reciprocal(onorm[:, :], onorm[:, :]))
            link(nc.vector.tensor_tensor(rstd[:, :], rstd[:, :], onorm[:, :], ALU.mult))
            nc.vector.tensor_tensor(nbias[:, :], nbias[:, :], onorm[:, :], ALU.mult).then_inc(norm_ready, 1)

            dve.wait_ge(key_edge, 32)
            link(nc.vector.tensor_tensor(b3(sfr), key[:, :, 1:P + 1], key[:, :, 0:P], ALU.not_equal))
            link(nc.vector.tensor_scalar(sfr, sfr, -BIG, None, ALU.mult))
            nc.vector.tensor_tensor(b3(efr), key[:, :, 1:P + 1], key[:, :, 2:P + 2], ALU.not_equal
                                    ).then_inc(rowsf_ready, 1)
            for n in range(2 * SB):
                dve.wait_ge(rowsT_done, n + 1)
                to = sidx if n < SB else dloc
                b = n % SB
                nc.vector.tensor_copy(to[:, b * P:(b + 1) * P], main[n % 4][:, 0:P]).then_inc(rowsT_read, 1)
            for n in range(2 * SB, 3 * SB):
                dve.wait_ge(rowsT_done, n + 1)
                b = n % SB
                nc.vector.tensor_copy(endt[:, b * P:(b + 1) * P], main[n % 4][:, 0:P]).then_inc(rowsT_read, 1)
            link(nc.vector.tensor_scalar(efr, efr, -BIG, None, ALU.mult))
            link(nc.vector.tensor_reduce(sany, b3(sfr), AX.X, ALU.min))
            nc.vector.tensor_reduce(eany, b3(efr), AX.X, ALU.min).then_inc(flags_ready, 1)
            dve.wait_ge(rowsT_read, 3 * SB)
            dve.wait_ge(tiles_in, 16)
            tq = trow[0:1, :].rearrange("p (q k) -> p q k", k=4)
            link(nc.vector.tensor_copy(tsum[0:1, :], tq[:, :, 3]))
            for k in (2, 1, 0):
                link(nc.vector.scalar_tensor_tensor(out=tsum[0:1, :], in0=tsum[0:1, :], scalar=64.0, in1=tq[:, :, k],
                                                    op0=ALU.mult, op1=ALU.add))
            link(nc.vector.tensor_copy(tpk[0:1, :], tsum[0:1, :]))
            dve.wait_ge(flags_out, 64)
            nc.vector.memset(sm4[:, :], 0.0).then_inc(steps_ready, 1)
            dve.wait_ge(steps_ready, 2)
            dve.wait_ge(acc_clear, NT)

            def onehot(col, at):
                return nc.vector.tensor_scalar(oh[:, at * P:(at + 1) * P], iota[:, :], dloc[:, col], None,
                                               ALU.is_equal).then_inc(onehots, 1)

            def accumulate(t, k, width, s):
                dve.wait_ge(products_done, CR + s + 1)
                dve.wait_ge(added, 4 + s)
                a = acc[:, bass.ds(t * AW, width)]
                nc.vector.tensor_tensor(a, a, main[k][:, 0:width], ALU.add).then_inc(added, 1)

            def conv(k):
                dve.wait_ge(table_stored, 16 * NI * (k + 1))
                if k:
                    dve.wait_ge(onehots, oh_base(k))
                    dve.wait_ge(acc_clear, NT * (k + 1))
                for s in range(AHEAD):
                    onehot(slice(s, s + 1), s)
                with nc.vector.Fori(0, S // U) as i:
                    for j in range(U):
                        if j % 4 == 0:
                            pk = dve.value_load(tpk[0:1, bass.ds(i * (U // 4) + j // 4, 1)], min_val=0,
                                                max_val=(1 << 24) - 1)
                        dve.wait_ge(products_done, CR + k * S + i * U + j)
                        onehot(bass.ds(i * U + j + AHEAD, 1), (j + AHEAD) % OHR)
                        t = tile_number((pk >> (6 * (j % 4))) & 63)
                        accumulate(t, j % 4, C + 1, k * S + i * U + j)

            def project(m, epilogue, prepare=None):
                def copy_out(i, j):
                    dve.wait_ge(rows_T, CR + m * NT + i * TB + j + 1)
                    dve.wait_ge(projected, m * NT + i * TB + j + (2 if j == 0 else 1))
                    nc.vector.tensor_copy(aT[:, (j % 2) * C:(j % 2 + 1) * C], pso[j % 2][:, 0:C]
                                          ).then_inc(rows_T_copied, 1)

                def tiles(i, ahead):
                    copy_out(i, 0)
                    for j in range(TB):
                        if j < TB - 1:
                            copy_out(i, j + 1)
                        dve.wait_ge(projected, 2 + m * NT + i * TB + j + 1)
                        epilogue(i, j)
                        if ahead and j in (0, 2, 4):
                            prepare(i + 1, j // 2)

                if prepare is None:
                    with nc.vector.Fori(0, NI) as i:
                        tiles(i, False)
                else:
                    for p in range(3):
                        prepare(0, p)
                    with nc.vector.Fori(0, NI - 1) as i:
                        tiles(i, True)
                    tiles(NI - 1, False)

            def with_norm_and_bias(to, i, j):
                return nc.vector.scalar_tensor_tensor(out=to, in0=main[j % 2][:, 0:C],
                                                      scalar=inorm[:, bass.ds(i * TB + j, 1)], in1=bias[:, :],
                                                      op0=ALU.mult, op1=ALU.add)

            for k in range(HOPS):
                conv(k)
                dve.wait_ge(added, 4 + (k + 1) * S)
                dve.wait_ge(w_in, 32 * (k + 1))
                if k == 0:
                    link(nc.vector.tensor_scalar(indeg0[:, :], acc3[:, :, ONES_COL], 0.0, None, ALU.is_equal))
                    nc.vector.tensor_scalar(inorm[:, :], acc3[:, :, ONES_COL], 1.0, None, ALU.max).then_inc(norm_in, 1)
                    dve.wait_ge(norm_sq, 3)
                    link(nc.vector.reciprocal(inorm[:, :], inorm[:, :]))
                if k < HOPS - 1:
                    def epilogue(i, j):
                        dve.wait_ge(staged, k * NT + i * TB + j + (2 if j == 0 else 1))
                        with_norm_and_bias(tmp[:, (j % 2) * C:(j % 2 + 1) * C], i, j).then_inc(proj_read, 1)
                    project(k, epilogue)
                else:
                    def epilogue(i, j):
                        if j == 0:
                            dve.wait_ge(rest_in, 16)
                            dve.wait_ge(back_in, i * 16 + 16)
                        t = i * TB + j
                        a = acc[:, bass.ds(t * AW, C)]
                        dve.wait_ge(proj_read, 2 + k * NT + t)
                        with_norm_and_bias(tmp[:, 0:C], i, j).then_inc(proj_read, 1)
                        dve.wait_ge(proj_read, 2 + k * NT + t + 1)
                        nc.vector.tensor_tensor(tmp[:, C:2 * C], tmp[:, 0:C], ring[:, bass.ds(t * C, C)], ALU.add
                                                ).then_inc(dve_chain, 1)
                        dve.wait_ge(dve_chain, chain[0] + 4 * t + 1)
                        dve.nop(nofuse=True)
                        nc.vector.bn_stats(bnst[:, 0:6], tmp[:, C:2 * C]).then_inc(dve_chain, 1)
                        nc.vector.tensor_copy(a, tmp[:, C:2 * C]).then_inc(mid_ready, 1)
                        dve.wait_ge(dve_chain, chain[0] + 4 * t + 2)
                        dve.nop(nofuse=True)
                        nc.vector.bn_aggr(bnst[:, 6:8], bnst[:, 0:6]).then_inc(dve_chain, 1)
                        dve.wait_ge(dve_chain, chain[0] + 4 * t + 3)
                        nc.vector.tensor_copy(stat[:, bass.ds(t * 2, 2)], bnst[:, 6:8]).then_inc(dve_chain, 1)
                        dve.wait_ge(dve_chain, chain[0] + 4 * t + 4)
                        dve.wait_ge(mid_ready, t + 1)
                    project(k, epilogue)
                    chain[0] += 4 * NT
                    row_scales(4, 2).then_inc(norm_ready, 1)

            def logit_columns(l):
                dve.wait_ge(w_in, 32 * HOPS + 64 * l + 48)
                for b in range(2):
                    for a in range(2):
                        link(nc.vector.tensor_tensor(tmp[:, 0:C], wcat[:, b * PW:b * PW + C], att[:, a * C:(a + 1) * C],
                                                     ALU.mult))
                        red = nc.vector.tensor_reduce(wcat[:, b * PW + C + a * H:b * PW + C + (a + 1) * H],
                                                      tmp[:, 0:C].rearrange("p (h c) -> p h c", h=H), AX.X, ALU.add)
                        if a + b < 2:
                            link(red)
                red.then_inc(wcat_ready, 1)
                dve.wait_ge(wcat_ready, l + 1)

            def normalise(l):
                base = chain[0]
                chain[0] += 2 * NI

                def part(i, p):
                    a = acc[:, bass.ds(i * TB * AW, TB * AW)].rearrange("p (t w) -> p t w", w=AW)[:, :, 0:C]
                    if p == 0:
                        dve.wait_ge(self_ready, l * NT + i * TB + TB)
                        own = ring[:, bass.ds(i * TB * C, TB * C)].rearrange("p (t c) -> p t c", c=C)
                        nc.vector.tensor_tensor(a, a, own, ALU.add).then_inc(dve_chain, 1)
                    if p == 1:
                        dve.wait_ge(dve_chain, i * 2 + (base + 1))
                        a4 = a.rearrange("p t (h c) -> p t h c", h=H)
                        r4 = rs[:, bass.ds(i * TB * H, TB * H)].rearrange("p (t h o) -> p t h o", h=H, o=1)
                        nc.vector.tensor_tensor(a4, a4, r4.to_broadcast([P, TB, H, CH]), ALU.mult
                                                ).then_inc(dve_chain, 1)
                    if p == 2:
                        dve.wait_ge(dve_chain, i * 2 + (base + 2))
                        nc.vector.tensor_tensor(a, a, bias[:, :].rearrange("p (o c) -> p o c", o=1)
                                                .to_broadcast([P, TB, C]), ALU.add).then_inc(mid_ready, TB)
                return part

            for l in range(LAYERS):
                logit_columns(l)

                def epilogue(i, j):
                    t = i * TB + j
                    if j == 0:
                        dve.wait_ge(table_stored, i * 16 + (16 * NI * (HOPS + l) - 16))
                    nc.vector.tensor_copy(staged_rows(i, j, PW), main[j % 2][:, 0:PW]).then_inc(staged, 1)
                    dve.wait_ge(staged, 2 + (HOPS - 1 + l) * NT + t + 1)
                    nc.vector.tensor_copy(tv[:, bass.ds(t * 2 * H, 2 * H)], staged_rows(i, j, 2 * H, C)
                                          ).then_inc(proj_read, 1)
                if l:
                    project(HOPS + l, epilogue, normalise(l - 1))
                else:
                    project(HOPS, epilogue)
                dve.wait_ge(proj_read, 2 + (HOPS + l + 1) * NT)
                part = [tvb[:, :].rearrange("p (t m k) -> p t m k", m=3, k=2 * H)[:, :, m, :] for m in range(3)]
                link(nc.vector.tensor_copy(part[0], tv3))
                link(nc.vector.tensor_tensor(tv3, tv3, part[0], ALU.subtract))
                link(nc.vector.tensor_copy(part[1], tv3))
                link(nc.vector.tensor_tensor(tv3, tv3, part[1], ALU.subtract))
                nc.vector.tensor_copy(part[2], tv3).then_inc(parts_ready, 1)
                dve.wait_ge(parts_ready, l + 1)
                dve.wait_ge(table_stored, 16 * NI * (HOPS + l + 1))
                dve.wait_ge(acc_clear, NT * (HOPS + l + 1))

                for b in range(GB):
                    o = b * H * G
                    link(nc.vector.memset(hg(rsf[0:1, o:o + H * G])[:, :, 0:1], -BIG))
                    link(nc.vector.memset(hg(ref[0:1, o:o + H * G])[:, :, G - 1:G], -BIG))
                link(nc.vector.memset(hg(dw[0:1, :])[:, :, G - 1:G], -BIG))
                link(nc.vector.memset(hg(cw[0:1, :])[:, :, 0:1], 0.0))

                mark_base, marks = chain[0], [0]

                def mark(ins):
                    marks[0] += 1
                    ins.then_inc(dve_chain, 1)
                    return marks[0]

                def after(m):
                    dve.wait_ge(dve_chain, mark_base + m)

                def logits_part(i, b, c):
                    asrc = slot(b)[:, :, C:C + H].rearrange("p g h -> p h g")
                    asrc_dst, adst_dst = logits_of(b)
                    per = NG // GB
                    rounds = (i + 1) * (per - 1) // per if b == 0 else i
                    dve.wait_ge(group_in[b], rounds * (16 * G) + 16 * G * (l * (NG // GB) + 1))
                    dve.wait_ge(ad_ready, c + l)
                    for m in (1, 2):
                        a = ad3[:, b % 2, :, 0:2 * H]
                        after(mark(nc.vector.tensor_tensor(a, a, ad3[:, b % 2, :, m * 2 * H:(m + 1) * 2 * H], ALU.add)))
                    nc.vector.tensor_tensor(hg(v[:, :]), asrc, asrc_dst, ALU.max).then_inc(v_ready, 1)
                    m1 = mark(nc.vector.tensor_tensor(hg(t1[:, :]), asrc, adst_dst, ALU.add))
                    m2 = mark(nc.vector.tensor_tensor(hg(t2[:, :]), asrc_dst, adst_dst, ALU.add))
                    after(m1)
                    mark(nc.vector.scalar_tensor_tensor(out=alpha[:, :], in0=t1[:, :], scalar=SLOPE, in1=t1[:, :],
                                                        op0=ALU.mult, op1=ALU.max))
                    after(m2)
                    return mark(nc.vector.scalar_tensor_tensor(out=lself[:, :], in0=t2[:, :], scalar=SLOPE,
                                                               in1=t2[:, :], op0=ALU.mult, op1=ALU.max))

                def rows_part(b, c):
                    sf, ef = sfl[:, b * P:(b + 1) * P], efl[:, b * P:(b + 1) * P]
                    dve.wait_ge(flags_in[b], flags_at[0])
                    dve.wait_ge(vT_done, c)
                    mark(nc.vector.tensor_tensor_scan(out=f1[:, :], data0=sf, data1=psb[0:H * G, 0:P], initial=-BIG,
                                                      op0=ALU.add, op1=ALU.max))
                    nc.vector.tensor_tensor_scan(out=r1[:, ::-1], data0=ef[:, ::-1], data1=psb[0:H * G, 0:P][:, ::-1],
                                                 initial=-BIG, op0=ALU.add, op1=ALU.max).then_inc(scan_ready, 1)
                    mark(nc.vector.tensor_scalar(sm4[0:1, 4 * H:4 * H + 1], sf[0:1, 0:1], 0.0, None, ALU.is_equal))

                def carry_part(b, c):
                    o = b * H * G
                    ends = psb[0:1, HALF:HALF + 2 * H * G]
                    dve.wait_ge(ends_done, c)
                    m1 = mark(nc.vector.tensor_copy(hg(cw[0:1, :])[:, :, 1:G], hg(ends[:, 0:H * G])[:, :, 0:G - 1]))
                    m2 = mark(nc.vector.tensor_copy(hg(dw[0:1, :])[:, :, 0:G - 1], hg(ends[:, H * G:])[:, :, 1:G]))
                    after(m1)
                    m3 = mark(nc.vector.tensor_tensor_scan(out=co[0:1, :], data0=rsf[0:1, o:o + H * G],
                                                           data1=cw[0:1, :], initial=-BIG, op0=ALU.add, op1=ALU.max))
                    after(m2)
                    m4 = mark(nc.vector.tensor_tensor_scan(out=do[0:1, ::-1], data0=ref[0:1, o:o + H * G][:, ::-1],
                                                           data1=dw[0:1, ::-1], initial=-BIG, op0=ALU.add, op1=ALU.max))
                    after(m3)
                    nc.vector.scalar_tensor_tensor(
                        out=nxt[0:1, :].rearrange("p (h o) -> p h o", o=1), in0=hg(co[0:1, :])[:, :, G - 1:G],
                        scalar=rlast[0:1, b:b + 1], in1=hg(ends[:, 0:H * G])[:, :, G - 1:G],
                        op0=ALU.add, op1=ALU.max).then_inc(carry_ready, 1)
                    after(m4)

                def maxima_part(b, c):
                    sf, ef = sfl[:, b * P:(b + 1) * P], efl[:, b * P:(b + 1) * P]
                    dve.wait_ge(carry_done, c)
                    after(mark(nc.vector.tensor_copy(cin[:, :], psb[0:H * G, HALF:HALF + 2])))
                    mark(nc.vector.tensor_tensor_scan(out=f2[:, :], data0=sf, data1=psb[0:H * G, 0:P],
                                                      initial=cin[:, 0:1], op0=ALU.add, op1=ALU.max))
                    after(mark(nc.vector.tensor_tensor_scan(out=r2[:, ::-1], data0=ef[:, ::-1],
                                                            data1=psb[0:H * G, 0:P][:, ::-1], initial=cin[:, 1:2],
                                                            op0=ALU.add, op1=ALU.max)))
                    nc.vector.tensor_tensor(mrow[:, :], f2[:, :], r2[:, :], ALU.max).then_inc(max_ready, 1)

                def exponents_part(b, c):
                    adst_dst = logits_of(b)[1]
                    one = "p (h o) -> p h o"
                    old, new = sm4[0:1, 0:H], sm4[0:1, H:2 * H]
                    dve.wait_ge(maxT_done, c)
                    m1 = mark(nc.vector.tensor_tensor(hg(t1[:, :]), hg(psb[:, P:P + H * G]), adst_dst, ALU.add))
                    m2 = mark(nc.vector.tensor_tensor(old.rearrange(one, o=1), hg(cw[0:1, :])[:, :, 0:1],
                                                      adst_dst[0:1, :, 0:1], ALU.add))
                    after(m1)
                    m3 = mark(nc.vector.scalar_tensor_tensor(out=mx[:, :], in0=t1[:, :], scalar=SLOPE, in1=t1[:, :],
                                                             op0=ALU.mult, op1=ALU.max))
                    after(m2)
                    m4 = mark(nc.vector.scalar_tensor_tensor(out=new, in0=old, scalar=SLOPE, in1=old,
                                                             op0=ALU.mult, op1=ALU.max))
                    after(m3)
                    mark(nc.vector.tensor_tensor(dd[:, 0:H * G], alpha[:, :], mx[:, :], ALU.subtract))
                    after(m4)
                    m5 = mark(nc.vector.tensor_tensor(old.rearrange(one, o=1), new.rearrange(one, o=1),
                                                      hg(mx[0:1, :])[:, :, 0:1], ALU.subtract))
                    mark(nc.vector.tensor_tensor(dd[:, H * G:2 * H * G], lself[:, :], mx[:, :], ALU.subtract))
                    m6 = mark(nc.vector.tensor_copy(hg(cw[0:1, :])[:, :, 0:1], nxt[0:1, :].rearrange(one, o=1)))
                    after(m5)
                    nc.vector.tensor_scalar(lf[0:1, :], old, sm4[0:1, 4 * H:4 * H + 1], None, ALU.mult
                                            ).then_inc(expo_ready, 1)
                    after(m6)

                c0 = l * (NG + 1) + 1
                flags_at = [FLAG_INCS * (l * (NG // GB + 1) + 1)]
                logits_part(0, 0, c0)
                rows_part(0, c0)
                carry_part(0, c0)
                maxima_part(0, c0)
                exponents_part(0, c0)
                chain[0] += marks[0]
                dve.wait_ge(dve_chain, chain[0])

                def fold_self(b, e, cols):
                    sl = slot(b)
                    dve.wait_ge(e_ready, e)
                    return mark(nc.vector.tensor_tensor(
                        sl[:, :, C + H:AW].rearrange("p g h -> p h g"), hg(eself[:, :]),
                        endt[:, cols].rearrange("p (o g) -> p o g", o=1).to_broadcast([P, H, G]), ALU.mult))

                def weigh(b, k):
                    r = ring3[:, b * G + k, 0:DVEC].rearrange("p (h c) -> p h c", c=CH)
                    w = ring3[:, b * G + k, C:C + DVEC // CH].rearrange("p (h o) -> p h o", o=1)
                    nc.vector.tensor_tensor(r, r, w.to_broadcast([P, DVEC // CH, CH]), ALU.mult
                                            ).then_inc(weighted_v, 1)

                mark_base, marks[0] = chain[0], 0
                fold_self(0, 2 * (l * (NG + 1) + 1), slice(0, G))
                chain[0] += marks[0]
                for k in range(LEAD):
                    weigh(0, k)

                with nc.vector.Fori(0, NG // GB) as it:
                    mark_base, marks[0] = it * MARKS + chain[0], 0
                    for b in range(GB):
                        nb_, s0 = (b + 1) % GB, (HOPS + l) * S + it * GB * G + b * G
                        c = it * GB + (l * (NG + 1) + b + 2)
                        over = 1 if b == GB - 1 else 0
                        per = NG // GB + (nb_ == 0)
                        flags_at[0] = it * FLAG_INCS + FLAG_INCS * (l * per + over + 1)
                        pk = nc.values_load_multi_w_load_instructions(
                            tpk[0:1, bass.ds(it * GB * Q + b * Q, Q)], engines=[mybir.EngineType.DVE], min_val=0,
                            max_val=(1 << 24) - 1)[1]

                        def tile_at(k):
                            return tile_number((pk[k // 4] >> (6 * (k % 4))) & 63)

                        def rescale():
                            dve.wait_ge(factor_ready, it * GB + (l * (NG + 1) + b + 1))
                            dve.wait_ge(added, 4 + s0)
                            t = tile_at(0)
                            a4 = acc[:, bass.ds(t * AW, C)].rearrange("p (h c) -> p h c", h=H)
                            f4 = resc[:, :].rearrange("p (h o) -> p h o", o=1).to_broadcast([P, H, CH])
                            mark(nc.vector.tensor_tensor(a4, a4, f4, ALU.mult))
                            aw = acc[:, bass.ds(t * AW + C, H)]
                            return mark(nc.vector.tensor_tensor(aw, aw, resc[:, :], ALU.mult))

                        def add(k):
                            accumulate(tile_at(k), k % 4, AW, s0 + k)

                        rescaled = rescale()
                        for k in range(G):
                            if k == G - LEAD:
                                add(k)
                                fold_self(nb_, it * GB * 2 + 2 * (l * (NG + 1) + b + 2),
                                          bass.ds(it * GB * G + (b + 1) * G, G))
                            if k < G - LEAD:
                                weigh(b, k + LEAD)
                            else:
                                weigh(nb_, k + LEAD - G)
                            if k == 0:
                                logits_part(it + over, nb_, c)
                            if k == 3:
                                rows_part(nb_, c)
                            if k == 6:
                                carry_part(nb_, c)
                            if k == 9:
                                maxima_part(nb_, c)
                            if k == 12:
                                exponents_part(nb_, c)
                            if k == 0:
                                after(rescaled)
                            if k != G - LEAD:
                                add(k)
                assert marks[0] == MARKS, marks[0]
                chain[0] += MARKS * (NG // GB)

                dve.wait_ge(added, 4 + (HOPS + l + 1) * S)
                link(nc.vector.tensor_tensor(es3, acc3[:, :, C + H:AW],
                                             indeg0[:, :].rearrange("p (t o) -> p t o", o=1).to_broadcast([P, NT, H]),
                                             ALU.add))
                link(nc.vector.tensor_tensor(rs3, es3, acc3[:, :, C:C + H], ALU.add))
                link(nc.vector.tensor_scalar(rs[:, :], rs[:, :], 1e-16, None, ALU.max))
                nc.vector.reciprocal(rs[:, :], rs[:, :]).then_inc(nself, 1)
                dve.wait_ge(nself, l + 1)
                dve.wait_ge(w_in, 32 * HOPS + 64 * (l + 1))
            finish = normalise(LAYERS - 1)
            with nc.vector.Fori(0, NI) as i:
                for p in range(3):
                    finish(i, p)
                dve.wait_ge(mid_ready, i * 2 * TB + (2 * NT + TB))
                dve.wait_ge(x1_back, i * 16 + 16)
                a = acc[:, bass.ds(i * TB * AW, TB * AW)].rearrange("p (t w) -> p t w", w=AW)[:, :, 0:C]
                x1 = oh[:, bass.ds((i & (XB - 1)) * TB * C, TB * C)].rearrange("p (t c) -> p t c", c=C)
                nc.vector.tensor_tensor(a, a, x1, ALU.add).then_inc(mid_ready, TB)


_INS = ['x', 'src', 'dst', 'L0_gnn_W', 'L0_gnn_b', 'L1_gnn_W1', 'L1_gnn_att_src1', 'L1_gnn_att_dst1', 'L1_gnn_b1',
        'L1_gnn_W2', 'L1_gnn_att_src2', 'L1_gnn_att_dst2', 'L1_gnn_b2']


def kernel(**inputs):
    import numpy as _np
    import concourse.bacc as _bacc
    from concourse import mybir as _mybir
    from concourse.bass_utils import run_bass_kernel_spmd as _run

    nc = _bacc.Bacc("TRN2", target_bir_lowering=False, num_devices=1)
    arrays, args = {}, []
    for name in _INS:
        a = _np.ascontiguousarray(inputs[name])
        arrays[f"in_{name}_dram"] = a
        args.append(nc.dram_tensor(f"in_{name}_dram", a.shape, _mybir.dt.from_np(a.dtype), kind="ExternalInput").ap())
    args.append(nc.dram_tensor("out_0_dram", (N, C), _mybir.dt.float32, kind="ExternalOutput").ap())
    gnn(nc, *args)
    r = _run(nc, [arrays], core_ids=[0])
    return r.results[0]["out_0_dram"]
```
